# Optimizing a Trainium2 kernel written in Bass

```python
import numpy as np
import jax
import jax.numpy as jnp

def _softmax(x, axis=-1):
    return jax.nn.softmax(x, axis=axis)

def _gelu(x):
    return jax.nn.gelu(x, approximate=True)

def _silu(x):
    return jax.nn.silu(x)

def _sigmoid(x):
    return jax.nn.sigmoid(x)

def _layernorm(x, axis=-1, eps=1e-05):
    m = jnp.mean(x, axis=axis, keepdims=True)
    v = jnp.var(x, axis=axis, keepdims=True)
    return (x - m) / jnp.sqrt(v + eps)

def _scatter_add(tgt, idx, src, axis=0):
    return tgt.at[idx].add(src)

def _segment_sum(src, seg, n):
    return jax.ops.segment_sum(src, seg, n)
kernel_name = 'mk_gps_d2_gnn_r16_1dc33a'

def setup_inputs(seed: int=0):
    np.random.seed(seed)
    _w = jnp.asarray

    def _rec_inputs():
        import jax
        import jax.numpy as jnp
        _gk = jax.random.key(seed)
        x = -0.0003713 + 1 * jax.random.normal(jax.random.fold_in(_gk, 1), (3125, 256), jnp.float32)
        src = jax.random.randint(jax.random.fold_in(_gk, 2), (50000,), 0, 3125, jnp.int32)
        dst = jnp.minimum((3125 * jax.random.uniform(jax.random.fold_in(_gk, 3), (50000,)) ** 2.0).astype(jnp.int32), 49999)
        _o = jnp.argsort(dst, stable=True)
        src = src[_o]
        dst = dst[_o]
        edge_attr_4 = 0.00121237 + 1.00026 * jax.random.normal(jax.random.fold_in(_gk, 12), (50000, 4), jnp.float32)
        edge_attr_8 = jax.random.uniform(jax.random.fold_in(_gk, 13), (50000, 8), jnp.float32, 0.0, 1)
        node_vec1 = jax.random.uniform(jax.random.fold_in(_gk, 14), (3125, 1), jnp.float32, 0.0, 1)
        return (x, src, dst, edge_attr_4, edge_attr_8, node_vec1)
    x, src, dst, edge_attr_4, edge_attr_8, node_vec1 = _rec_inputs()

    def _L0_gnn_setup():
        import jax, jax.numpy as jnp
        import numpy as np
        N_NODES = 3125
        N_EDGES = 50000
        D = 256
        NUM_STEPS = 6
        key = jax.random.key(seed)
        ks = jax.random.split(key, 12)
        s = 1.0 / np.sqrt(D)
        return {'node_feats': jax.random.normal(ks[0], (N_NODES, D), jnp.float32), 'W1': jax.random.normal(ks[1], (D, D), jnp.float32) * s, 'b1': jax.random.normal(ks[2], (D,), jnp.float32) * s, 'W2': jax.random.normal(ks[3], (D, D), jnp.float32) * s, 'b2': jax.random.normal(ks[4], (D,), jnp.float32) * s, 'W_ih': jax.random.normal(ks[5], (3 * D, D), jnp.float32) * s, 'b_ih': jax.random.normal(ks[6], (3 * D,), jnp.float32) * s, 'W_hh': jax.random.normal(ks[7], (3 * D, D), jnp.float32) * s, 'b_hh': jax.random.normal(ks[8], (3 * D,), jnp.float32) * s, 'src': jax.random.randint(ks[9], (N_EDGES,), 0, N_NODES, jnp.int32), 'dst': jax.random.randint(ks[10], (N_EDGES,), 0, N_NODES, jnp.int32)}
    _L0_gnn_all = _L0_gnn_setup()
    _L0_gnn_in = {k: v for k, v in _L0_gnn_all.items() if k in ('W1', 'b1', 'W2', 'b2', 'W_ih', 'b_ih', 'W_hh', 'b_hh')}
    del _L0_gnn_all

    def _L0_mix_setup():
        import jax, jax.numpy as jnp
        import numpy as np
        D_MODEL = 256
        NUM_HEADS = 8
        DEPTH = D_MODEL // NUM_HEADS
        B, L = (32, 256)

        def _feature_map(x):
            return jax.nn.elu(x) + 1.0
        key = jax.random.key(seed)
        ks = jax.random.split(key, 9)
        sc = 1.0 / np.sqrt(D_MODEL)
        return {'x': jax.random.normal(ks[0], (B, L, D_MODEL), dtype=jnp.float32), 'wq': jax.random.normal(ks[1], (D_MODEL, D_MODEL), dtype=jnp.float32) * sc, 'bq': jnp.zeros((D_MODEL,), dtype=jnp.float32), 'wk': jax.random.normal(ks[2], (D_MODEL, D_MODEL), dtype=jnp.float32) * sc, 'bk': jnp.zeros((D_MODEL,), dtype=jnp.float32), 'wv': jax.random.normal(ks[3], (D_MODEL, D_MODEL), dtype=jnp.float32) * sc, 'bv': jnp.zeros((D_MODEL,), dtype=jnp.float32), 'wo': jax.random.normal(ks[4], (D_MODEL, D_MODEL), dtype=jnp.float32) * sc, 'bo': jnp.zeros((D_MODEL,), dtype=jnp.float32)}
    _L0_mix_all = _L0_mix_setup()
    _L0_mix_in = {k: v for k, v in _L0_mix_all.items() if k in ('wq', 'bq', 'wk', 'bk', 'wv', 'bv', 'wo', 'bo')}
    del _L0_mix_all

    def _L0_ffn_setup():
        import jax, jax.numpy as jnp
        import numpy as np
        E, D, H, TOP_K = (6, 256, 256, 2)
        ROUTER_H = D // 2
        key = jax.random.key(seed)
        ks = jax.random.split(key, 12)
        s = 1.0 / np.sqrt(D)
        sh = 1.0 / np.sqrt(H)
        sr = 1.0 / np.sqrt(ROUTER_H)
        return {'features': jax.random.normal(ks[0], (8, 256, D), dtype=jnp.float32), 'router_w1': jax.random.uniform(ks[1], (D, ROUTER_H), jnp.float32, -s, s), 'router_b1': jnp.zeros((ROUTER_H,), jnp.float32), 'router_w2': jax.random.uniform(ks[2], (ROUTER_H, E), jnp.float32, -sr, sr), 'router_b2': jnp.zeros((E,), jnp.float32), 'expert_w1': jax.random.uniform(ks[3], (E, D, H), jnp.float32, -s, s), 'expert_b1': jnp.zeros((E, H), jnp.float32), 'expert_w2': jax.random.uniform(ks[4], (E, H, H), jnp.float32, -sh, sh), 'expert_b2': jnp.zeros((E, H), jnp.float32), 'expert_w3': jax.random.uniform(ks[5], (E, H, D), jnp.float32, -sh, sh), 'expert_b3': jnp.zeros((E, D), jnp.float32)}
    _L0_ffn_all = _L0_ffn_setup()
    _L0_ffn_in = {k: v for k, v in _L0_ffn_all.items() if k in ('router_w1', 'router_b1', 'router_w2', 'router_b2', 'expert_w1', 'expert_b1', 'expert_w2', 'expert_b2', 'expert_w3', 'expert_b3')}
    del _L0_ffn_all

    def _L1_gnn_setup():
        import jax, jax.numpy as jnp
        import numpy as np
        N = 25000
        E = 25000
        MUL = 64
        NB = 8
        RN = 64
        NUM_NEIGH = 16.0
        INV_SQRT3 = 1.0 / np.sqrt(3.0)

        def _forward(node_input, node_attr, edge_attr, edge_length_embedded, W_sc0, W_sc1, W_lin1_0, W_lin1_1, fc_w0, fc_w1, W_lin2_0, W_lin2_1, edge_src, edge_dst):
            Nn = node_input.shape[0]
            z = node_attr
            x0 = node_input[:, :MUL]
            x1 = node_input[:, MUL:].reshape(Nn, MUL, 3)
            inv_m = 1.0 / np.sqrt(MUL)
            s0 = x0 @ W_sc0 * z * inv_m
            s1 = jnp.einsum('nuc,uv->nvc', x1, W_sc1) * z[:, :, None] * inv_m
            h0 = x0 @ W_lin1_0 * z * inv_m
            h1 = jnp.einsum('nuc,uv->nvc', x1, W_lin1_1) * z[:, :, None] * inv_m
            hid = jax.nn.silu(edge_length_embedded @ fc_w0 / np.sqrt(NB))
            w = hid @ fc_w1 / np.sqrt(RN)
            wA, wB, wC, wD = (w[:, :MUL], w[:, MUL:2 * MUL], w[:, 2 * MUL:3 * MUL], w[:, 3 * MUL:])
            xs0 = h0[edge_src]
            xs1 = h1[edge_src]
            sh0 = edge_attr[:, :1]
            sh1 = edge_attr[:, 1:4]
            midA = wA * xs0 * sh0
            midD = wD * jnp.einsum('euc,ec->eu', xs1, sh1) * INV_SQRT3
            midB = (wB * xs0)[:, :, None] * sh1[:, None, :]
            midC = wC[:, :, None] * xs1 * sh0[:, None, :]
            mid0 = jnp.concatenate([midA, midD], axis=1)
            mid1 = jnp.concatenate([midB, midC], axis=1)
            inv_nb = 1.0 / np.sqrt(NUM_NEIGH)
            y0 = jax.ops.segment_sum(mid0, edge_dst, num_segments=Nn) * inv_nb
            y1 = jax.ops.segment_sum(mid1.reshape(mid1.shape[0], -1), edge_dst, num_segments=Nn).reshape(Nn, 2 * MUL, 3) * inv_nb
            inv_2m = 1.0 / np.sqrt(2 * MUL)
            o0 = y0 @ W_lin2_0 * z * inv_2m
            o1 = jnp.einsum('nuc,uv->nvc', y1, W_lin2_1) * z[:, :, None] * inv_2m
            c_s = np.float32(np.sin(np.pi / 8.0))
            c_x = np.float32(np.cos(np.pi / 8.0))
            out0 = c_s * s0 + c_x * o0
            out1 = c_s * s1 + c_x * o1
            return jnp.concatenate([out0, out1.reshape(Nn, 3 * MUL)], axis=1)
        key = jax.random.key(seed)
        ks = jax.random.split(key, 14)
        f32 = jnp.float32
        return {'node_input': jax.random.normal(ks[0], (N, 4 * MUL), f32), 'node_attr': jnp.ones((N, 1), f32), 'edge_src': jax.random.randint(ks[1], (E,), 0, N, dtype=jnp.int32), 'edge_dst': jax.random.randint(ks[2], (E,), 0, N, dtype=jnp.int32), 'edge_attr': jax.random.normal(ks[3], (E, 4), f32), 'edge_length_embedded': jax.random.uniform(ks[4], (E, NB), f32), 'W_sc0': jax.random.normal(ks[5], (MUL, MUL), f32), 'W_sc1': jax.random.normal(ks[6], (MUL, MUL), f32), 'W_lin1_0': jax.random.normal(ks[7], (MUL, MUL), f32), 'W_lin1_1': jax.random.normal(ks[8], (MUL, MUL), f32), 'fc_w0': jax.random.normal(ks[9], (NB, RN), f32), 'fc_w1': jax.random.normal(ks[10], (RN, 4 * MUL), f32), 'W_lin2_0': jax.random.normal(ks[11], (2 * MUL, MUL), f32), 'W_lin2_1': jax.random.normal(ks[12], (2 * MUL, MUL), f32)}
    _L1_gnn_all = _L1_gnn_setup()
    _L1_gnn_in = {k: v for k, v in _L1_gnn_all.items() if k in ('W_sc0', 'W_sc1', 'W_lin1_0', 'W_lin1_1', 'fc_w0', 'fc_w1', 'W_lin2_0', 'W_lin2_1')}
    del _L1_gnn_all

    def _L1_mix_setup():
        import jax, jax.numpy as jnp
        import numpy as np
        HEADS = 8
        DIM_HEAD = 64
        EPS = 1e-05

        def _inst_norm(t):
            mu = jnp.mean(t, axis=-1, keepdims=True)
            var = jnp.var(t, axis=-1, keepdims=True)
            return (t - mu) / jnp.sqrt(var + EPS)
        key = jax.random.key(seed)
        k1, k2, k3, k4 = jax.random.split(key, 4)
        b, n, dim = (4, 512, 256)
        inner = HEADS * DIM_HEAD
        x = jax.random.normal(k1, (b, n, dim), dtype=jnp.float32)
        w_qkv = jax.random.normal(k2, (dim, 3 * inner), dtype=jnp.float32) * (1.0 / DIM_HEAD)
        w_out = jax.random.normal(k3, (inner, dim), dtype=jnp.float32) * dim ** (-0.5)
        b_out = jax.random.normal(k4, (dim,), dtype=jnp.float32) * 0.01
        return {'x': x, 'w_qkv': w_qkv, 'w_out': w_out, 'b_out': b_out}
    _L1_mix_all = _L1_mix_setup()
    _L1_mix_in = {k: v for k, v in _L1_mix_all.items() if k in ('w_qkv', 'w_out', 'b_out')}
    del _L1_mix_all

    def _L1_ffn_setup():
        import jax, jax.numpy as jnp
        import numpy as np
        N_EXPERTS = 8
        TOP_K = 2
        key = jax.random.key(seed)
        ks = jax.random.split(key, 5)
        B, T, C, E, H = (8, 128, 256, 8, 682)
        scale = 1.0 / np.sqrt(C)
        return {'x': jax.random.normal(ks[0], (B, T, C), dtype=jnp.float32), 'router_w': jax.random.normal(ks[1], (E, C), dtype=jnp.float32) * scale, 'w1': jax.random.normal(ks[2], (E, H, C), dtype=jnp.float32) * scale, 'w2': jax.random.normal(ks[3], (E, C, H), dtype=jnp.float32) * (1.0 / np.sqrt(H)), 'w3': jax.random.normal(ks[4], (E, H, C), dtype=jnp.float32) * scale}
    _L1_ffn_all = _L1_ffn_setup()
    _L1_ffn_in = {k: v for k, v in _L1_ffn_all.items() if k in ('router_w', 'w1', 'w2', 'w3')}
    del _L1_ffn_all
    return {'x': x, 'src': src, 'dst': dst, 'edge_attr_4': edge_attr_4, 'edge_attr_8': edge_attr_8, 'node_vec1': node_vec1, 'L0_gnn_W1': _L0_gnn_in['W1'], 'L0_gnn_b1': _L0_gnn_in['b1'], 'L0_gnn_W2': _L0_gnn_in['W2'], 'L0_gnn_b2': _L0_gnn_in['b2'], 'L0_gnn_W_ih': _L0_gnn_in['W_ih'], 'L0_gnn_b_ih': _L0_gnn_in['b_ih'], 'L0_gnn_W_hh': _L0_gnn_in['W_hh'], 'L0_gnn_b_hh': _L0_gnn_in['b_hh'], 'L0_mix_wq': _L0_mix_in['wq'], 'L0_mix_bq': _L0_mix_in['bq'], 'L0_mix_wk': _L0_mix_in['wk'], 'L0_mix_bk': _L0_mix_in['bk'], 'L0_mix_wv': _L0_mix_in['wv'], 'L0_mix_bv': _L0_mix_in['bv'], 'L0_mix_wo': _L0_mix_in['wo'], 'L0_mix_bo': _L0_mix_in['bo'], 'L0_ffn_router_w1': _L0_ffn_in['router_w1'], 'L0_ffn_router_b1': _L0_ffn_in['router_b1'], 'L0_ffn_router_w2': _L0_ffn_in['router_w2'], 'L0_ffn_router_b2': _L0_ffn_in['router_b2'], 'L0_ffn_expert_w1': _L0_ffn_in['expert_w1'], 'L0_ffn_expert_b1': _L0_ffn_in['expert_b1'], 'L0_ffn_expert_w2': _L0_ffn_in['expert_w2'], 'L0_ffn_expert_b2': _L0_ffn_in['expert_b2'], 'L0_ffn_expert_w3': _L0_ffn_in['expert_w3'], 'L0_ffn_expert_b3': _L0_ffn_in['expert_b3'], 'L1_gnn_W_sc0': _L1_gnn_in['W_sc0'], 'L1_gnn_W_sc1': _L1_gnn_in['W_sc1'], 'L1_gnn_W_lin1_0': _L1_gnn_in['W_lin1_0'], 'L1_gnn_W_lin1_1': _L1_gnn_in['W_lin1_1'], 'L1_gnn_fc_w0': _L1_gnn_in['fc_w0'], 'L1_gnn_fc_w1': _L1_gnn_in['fc_w1'], 'L1_gnn_W_lin2_0': _L1_gnn_in['W_lin2_0'], 'L1_gnn_W_lin2_1': _L1_gnn_in['W_lin2_1'], 'L1_mix_w_qkv': _L1_mix_in['w_qkv'], 'L1_mix_w_out': _L1_mix_in['w_out'], 'L1_mix_b_out': _L1_mix_in['b_out'], 'L1_ffn_router_w': _L1_ffn_in['router_w'], 'L1_ffn_w1': _L1_ffn_in['w1'], 'L1_ffn_w2': _L1_ffn_in['w2'], 'L1_ffn_w3': _L1_ffn_in['w3']}

def reference(x, src, dst, edge_attr_4, edge_attr_8, node_vec1, L0_gnn_W1, L0_gnn_b1, L0_gnn_W2, L0_gnn_b2, L0_gnn_W_ih, L0_gnn_b_ih, L0_gnn_W_hh, L0_gnn_b_hh, L0_mix_wq, L0_mix_bq, L0_mix_wk, L0_mix_bk, L0_mix_wv, L0_mix_bv, L0_mix_wo, L0_mix_bo, L0_ffn_router_w1, L0_ffn_router_b1, L0_ffn_router_w2, L0_ffn_router_b2, L0_ffn_expert_w1, L0_ffn_expert_b1, L0_ffn_expert_w2, L0_ffn_expert_b2, L0_ffn_expert_w3, L0_ffn_expert_b3, L1_gnn_W_sc0, L1_gnn_W_sc1, L1_gnn_W_lin1_0, L1_gnn_W_lin1_1, L1_gnn_fc_w0, L1_gnn_fc_w1, L1_gnn_W_lin2_0, L1_gnn_W_lin2_1, L1_mix_w_qkv, L1_mix_w_out, L1_mix_b_out, L1_ffn_router_w, L1_ffn_w1, L1_ffn_w2, L1_ffn_w3):
    import jax
    import jax.numpy as jnp

    def _L0_gnn_ref(node_feats, W1, b1, W2, b2, W_ih, b_ih, W_hh, b_hh, src, dst):
        import jax, jax.numpy as jnp
        import numpy as np
        N_NODES = 3125
        N_EDGES = 50000
        D = 256
        NUM_STEPS = 6
        n_nodes = node_feats.shape[0]
        for _ in range(NUM_STEPS):
            h = jnp.maximum(node_feats @ W1.T + b1, 0.0) @ W2.T + b2
            msg = jax.ops.segment_sum(h[src], dst, num_segments=n_nodes)
            gx = msg @ W_ih.T + b_ih
            gh = node_feats @ W_hh.T + b_hh
            xr, xz, xn = jnp.split(gx, 3, axis=-1)
            hr, hz, hn = jnp.split(gh, 3, axis=-1)
            r = jax.nn.sigmoid(xr + hr)
            z = jax.nn.sigmoid(xz + hz)
            n = jnp.tanh(xn + r * hn)
            node_feats = (1.0 - z) * n + z * node_feats
        return node_feats

    def _L0_mix_ref(x, wq, bq, wk, bk, wv, bv, wo, bo):
        import jax, jax.numpy as jnp
        import numpy as np
        D_MODEL = 256
        NUM_HEADS = 8
        DEPTH = D_MODEL // NUM_HEADS
        B, L = (32, 256)

        def _feature_map(x):
            return jax.nn.elu(x) + 1.0
        b, l, _ = x.shape
        q = (x @ wq + bq).reshape(b, l, NUM_HEADS, DEPTH)
        k = (x @ wk + bk).reshape(b, l, NUM_HEADS, DEPTH)
        v = (x @ wv + bv).reshape(b, l, NUM_HEADS, DEPTH)
        q = _feature_map(q)
        k = _feature_map(k)
        kv = jnp.einsum('blhd,blhe->bhde', k, v)
        k_sum = jnp.sum(k, axis=1)
        qkv = jnp.einsum('blhd,bhde->blhe', q, kv)
        normalizer = jnp.einsum('blhd,bhd->blh', q, k_sum) + 1e-06
        out = qkv / normalizer[..., None]
        out = out.reshape(b, l, D_MODEL)
        return out @ wo + bo

    def _L0_ffn_ref(features, router_w1, router_b1, router_w2, router_b2, expert_w1, expert_b1, expert_w2, expert_b2, expert_w3, expert_b3):
        import jax, jax.numpy as jnp
        import numpy as np
        E, D, H, TOP_K = (6, 256, 256, 2)
        ROUTER_H = D // 2
        rh = jax.nn.relu(features @ router_w1 + router_b1)
        expert_logits = jax.nn.softmax(rh @ router_w2 + router_b2, axis=-1)
        top_w, top_i = jax.lax.top_k(expert_logits, TOP_K)
        routing_weights = jax.nn.softmax(top_w, axis=-1)
        h1 = jax.nn.relu(jnp.einsum('bsd,edh->bseh', features, expert_w1) + expert_b1)
        h2 = jax.nn.relu(jnp.einsum('bseh,ehf->bsef', h1, expert_w2) + expert_b2)
        expert_out = jnp.einsum('bsef,efo->bseo', h2, expert_w3) + expert_b3
        sel = jnp.take_along_axis(expert_out, top_i[:, :, :, None], axis=2)
        combined = jnp.sum(sel * routing_weights[..., None], axis=2)
        return combined

    def _L1_gnn_ref(node_input, node_attr, edge_src, edge_dst, edge_attr, edge_length_embedded, W_sc0, W_sc1, W_lin1_0, W_lin1_1, fc_w0, fc_w1, W_lin2_0, W_lin2_1):
        import jax, jax.numpy as jnp
        import numpy as np
        N = 25000
        E = 25000
        MUL = 64
        NB = 8
        RN = 64
        NUM_NEIGH = 16.0
        INV_SQRT3 = 1.0 / np.sqrt(3.0)

        def _forward(node_input, node_attr, edge_attr, edge_length_embedded, W_sc0, W_sc1, W_lin1_0, W_lin1_1, fc_w0, fc_w1, W_lin2_0, W_lin2_1, edge_src, edge_dst):
            Nn = node_input.shape[0]
            z = node_attr
            x0 = node_input[:, :MUL]
            x1 = node_input[:, MUL:].reshape(Nn, MUL, 3)
            inv_m = 1.0 / np.sqrt(MUL)
            s0 = x0 @ W_sc0 * z * inv_m
            s1 = jnp.einsum('nuc,uv->nvc', x1, W_sc1) * z[:, :, None] * inv_m
            h0 = x0 @ W_lin1_0 * z * inv_m
            h1 = jnp.einsum('nuc,uv->nvc', x1, W_lin1_1) * z[:, :, None] * inv_m
            hid = jax.nn.silu(edge_length_embedded @ fc_w0 / np.sqrt(NB))
            w = hid @ fc_w1 / np.sqrt(RN)
            wA, wB, wC, wD = (w[:, :MUL], w[:, MUL:2 * MUL], w[:, 2 * MUL:3 * MUL], w[:, 3 * MUL:])
            xs0 = h0[edge_src]
            xs1 = h1[edge_src]
            sh0 = edge_attr[:, :1]
            sh1 = edge_attr[:, 1:4]
            midA = wA * xs0 * sh0
            midD = wD * jnp.einsum('euc,ec->eu', xs1, sh1) * INV_SQRT3
            midB = (wB * xs0)[:, :, None] * sh1[:, None, :]
            midC = wC[:, :, None] * xs1 * sh0[:, None, :]
            mid0 = jnp.concatenate([midA, midD], axis=1)
            mid1 = jnp.concatenate([midB, midC], axis=1)
            inv_nb = 1.0 / np.sqrt(NUM_NEIGH)
            y0 = jax.ops.segment_sum(mid0, edge_dst, num_segments=Nn) * inv_nb
            y1 = jax.ops.segment_sum(mid1.reshape(mid1.shape[0], -1), edge_dst, num_segments=Nn).reshape(Nn, 2 * MUL, 3) * inv_nb
            inv_2m = 1.0 / np.sqrt(2 * MUL)
            o0 = y0 @ W_lin2_0 * z * inv_2m
            o1 = jnp.einsum('nuc,uv->nvc', y1, W_lin2_1) * z[:, :, None] * inv_2m
            c_s = np.float32(np.sin(np.pi / 8.0))
            c_x = np.float32(np.cos(np.pi / 8.0))
            out0 = c_s * s0 + c_x * o0
            out1 = c_s * s1 + c_x * o1
            return jnp.concatenate([out0, out1.reshape(Nn, 3 * MUL)], axis=1)
        return _forward(node_input, node_attr, edge_attr, edge_length_embedded, W_sc0, W_sc1, W_lin1_0, W_lin1_1, fc_w0, fc_w1, W_lin2_0, W_lin2_1, edge_src, edge_dst)

    def _L1_mix_ref(x, w_qkv, w_out, b_out):
        import jax, jax.numpy as jnp
        import numpy as np
        HEADS = 8
        DIM_HEAD = 64
        EPS = 1e-05

        def _inst_norm(t):
            mu = jnp.mean(t, axis=-1, keepdims=True)
            var = jnp.var(t, axis=-1, keepdims=True)
            return (t - mu) / jnp.sqrt(var + EPS)
        b, n, dim = x.shape
        qkv = x @ w_qkv
        q, k, v = jnp.split(qkv, 3, axis=-1)
        to_heads = lambda t: t.reshape(b, n, HEADS, DIM_HEAD).transpose(0, 2, 1, 3)
        q, k, v = (to_heads(q), to_heads(k), to_heads(v))
        k = _inst_norm(k)
        v = _inst_norm(v)
        dots = jnp.einsum('bhnd,bhne->bhde', k, v)
        out = jnp.einsum('bhnd,bhde->bhne', q, dots) * (1.0 / n)
        out = out.transpose(0, 2, 1, 3).reshape(b, n, HEADS * DIM_HEAD)
        return out @ w_out + b_out

    def _L1_ffn_ref(x, router_w, w1, w2, w3):
        import jax, jax.numpy as jnp
        import numpy as np
        N_EXPERTS = 8
        TOP_K = 2
        B, T, C = x.shape
        flat = x.reshape(-1, C)
        logits = flat @ router_w.T
        probs = jax.nn.softmax(logits, axis=-1)
        topk_probs, topk_idx = jax.lax.top_k(probs, TOP_K)
        topk_probs = topk_probs / (jnp.sum(topk_probs, axis=-1, keepdims=True) + 1e-09)
        onehot = jax.nn.one_hot(topk_idx, N_EXPERTS, dtype=flat.dtype)
        gates = jnp.einsum('nk,nke->ne', topk_probs, onehot)
        h1 = jnp.einsum('nc,ehc->neh', flat, w1)
        h3 = jnp.einsum('nc,ehc->neh', flat, w3)
        h = jax.nn.silu(h1) * h3
        y = jnp.einsum('neh,ech->nec', h, w2)
        out = jnp.einsum('ne,nec->nc', gates, y)
        return out.reshape(B, T, C)
    xn = _layernorm(x, axis=-1)
    x = x + _L0_gnn_ref(xn, L0_gnn_W1, L0_gnn_b1, L0_gnn_W2, L0_gnn_b2, L0_gnn_W_ih, L0_gnn_b_ih, L0_gnn_W_hh, L0_gnn_b_hh, src, dst) + _L0_mix_ref(xn[None], L0_mix_wq, L0_mix_bq, L0_mix_wk, L0_mix_bk, L0_mix_wv, L0_mix_bv, L0_mix_wo, L0_mix_bo)[0]
    x = x + _L0_ffn_ref(_layernorm(x, axis=-1)[None], L0_ffn_router_w1, L0_ffn_router_b1, L0_ffn_router_w2, L0_ffn_router_b2, L0_ffn_expert_w1, L0_ffn_expert_b1, L0_ffn_expert_w2, L0_ffn_expert_b2, L0_ffn_expert_w3, L0_ffn_expert_b3)[0]
    xn = _layernorm(x, axis=-1)
    x = x + _L1_gnn_ref(xn, node_vec1, src, dst, edge_attr_4, edge_attr_8, L1_gnn_W_sc0, L1_gnn_W_sc1, L1_gnn_W_lin1_0, L1_gnn_W_lin1_1, L1_gnn_fc_w0, L1_gnn_fc_w1, L1_gnn_W_lin2_0, L1_gnn_W_lin2_1) + _L1_mix_ref(xn[None], L1_mix_w_qkv, L1_mix_w_out, L1_mix_b_out)[0]
    x = x + _L1_ffn_ref(_layernorm(x, axis=-1)[None], L1_ffn_router_w, L1_ffn_w1, L1_ffn_w2, L1_ffn_w3)[0]
    return x

_drawn_inputs = setup_inputs


def setup_inputs(seed=0):
    import zlib

    import numpy as np

    out = dict(_drawn_inputs(seed))
    spreads = {'L0_mix_bq': (0.0, 2.0),
     'L0_mix_bk': (0.0, 2.0),
     'L0_mix_bv': (0.0, 0.1),
     'L0_mix_bo': (0.0, 0.1),
     'L0_ffn_router_b1': (0.0, 0.1),
     'L0_ffn_router_b2': (0.0, 0.1),
     'L0_ffn_expert_b1': (0.0, 0.354),
     'L0_ffn_expert_b2': (0.0, 0.1),
     'L0_ffn_expert_b3': (0.0, 0.1)}
    factors = {'L0_mix_wq': 14.015, 'L0_mix_wk': 2.874, 'L1_mix_b_out': 4.421}
    for name, (base, spread) in spreads.items():
        noise = np.random.default_rng([zlib.crc32(name.encode()), seed]).standard_normal(out[name].shape)
        drawn = base * np.exp(spread * noise) if base else spread * noise
        out[name] = jnp.asarray(drawn.astype(out[name].dtype))
    for name, factor in factors.items():
        out[name] = (out[name] * factor).astype(out[name].dtype)
    return out
```

```python
from contextlib import ExitStack

import numpy as np

import concourse.bass as bass
from concourse import mybir

F32 = mybir.dt.float32
I32 = mybir.dt.int32
U32 = mybir.dt.uint32
ALU = mybir.AluOpType
ACT = mybir.ActivationFunctionType
AX = mybir.AxisListType.X

N, D = 3125, 256
RT, NT = 100, 32
GT, NG = 4, 8
GC = RT * GT
NP = RT * NT
LASTROWS = N - RT * (NT - 1)
KD = D // 128
EC, NCH = 125, 400
HALF = 4
ITC = 2 * HALF
NIT = NCH // ITC
W = 64
TOPBASE = NP - W
STEPS = 6
EPS = 1e-5
HEADS0, DH0 = 8, 32
HEADS1, DH1 = 8, 64
INNER = HEADS1 * DH1
E0, E1, HID1 = 6, 8, 682
HCH = [(k * 128, min(128, HID1 - k * 128)) for k in range((HID1 + 127) // 128)]
MUL = 64
NEG = -1e30
START = 16


def wait_alone(eng, sem, value, passed):
    eng.wait_ge(sem, START + value)
    eng.sem_inc(passed, 1)


def build(nc, A, out, debug=None):
    top = ExitStack()
    names = [0]

    held = []

    def sems(*wanted):
        got = [nc.alloc_semaphore(name=n) for n in wanted]
        engines = (nc.gpsimd, nc.sync, nc.scalar, nc.vector, nc.tensor)
        for n, (sem, name) in enumerate(zip(got, wanted)):
            if "gathered" not in name:
                engines[n % len(engines)].sem_inc(sem, START)
        nc.all_engine_barrier()
        held.extend(got)
        return got

    def phase(f, *args):
        f(nc, *args)
        if held:
            nc.clear_and_free_semaphores(held)
            held.clear()
            nc.all_engine_barrier()

    def sb(ctx, name, shape, dt=F32):
        names[0] += 1
        return ctx.enter_context(nc.sbuf_tensor(f"{name}_{names[0]}", shape, dt))

    with top:
        x_rows = sb(top, "x_rows", [RT, NT, D])
        ident = sb(top, "ident", [128, 128])
        iota_w = sb(top, "iota_w", [EC, W])
        src_t = sb(top, "src_t", [EC, NCH], I32)
        rel0 = sb(top, "rel0", [EC, NCH])
        base_row = sb(top, "base_row", [1, NCH], I32)
        rounds_t = sb(top, "rounds_t", [1, 1], I32)
        eps_t = sb(top, "eps_t", [128, 1])
        bank = [top.enter_context(nc.psum_tensor(f"bank{k}", [128, 512], F32)) for k in range(8)]
        h_dram = nc.dram_tensor("h_dram", (NP, D), F32).ap()
        base_dram = nc.dram_tensor("base_dram", (NCH,), F32).ap()
        span_dram = nc.dram_tensor("span_dram", (NCH,), F32).ap()

        phase(setup, A, sems, sb, x_rows, ident, iota_w, src_t, rel0, base_row, rounds_t, eps_t,
              base_dram, span_dram)
        tables = (src_t, rel0, base_row, rounds_t, iota_w)

        with ExitStack() as ctx:
            nf = sb(ctx, "nf", [128, KD, NP])
            mix = sb(ctx, "mix", [128, KD, NP])
            phase(norm_transpose, "n0", sems, sb, x_rows, ident, eps_t, bank, nf, False)
            phase(linear_attention, A, sems, sb, bank, nf, mix)
            phase(gated_graph, A, sems, sb, bank, tables, nf, h_dram)
            phase(add_transposed, sems, bank, sb, ident, x_rows, nf, mix)
        if debug == "l0a":
            return store_rows(nc, sems, x_rows, out)
        with ExitStack() as ctx:
            xt = sb(ctx, "xt", [128, KD, NP])
            phase(norm_transpose, "n1", sems, sb, x_rows, ident, eps_t, bank, xt, False)
            phase(expert_mlp, A, sems, sb, bank, xt, x_rows)
        if debug == "l0":
            return store_rows(nc, sems, x_rows, out)

        with ExitStack() as ctx:
            xt = sb(ctx, "xt", [128, KD, NP])
            wcomb = sb(ctx, "wcomb", [128, KD, D])
            phase(norm_transpose, "n2", sems, sb, x_rows, ident, eps_t, bank, xt, True)
            phase(galerkin_and_nodes, A, sems, sb, bank, xt, wcomb, h_dram)
            phase(edge_convolution, A, sems, sb, bank, tables, xt, wcomb, x_rows, h_dram)
        if debug == "l1a":
            return store_rows(nc, sems, x_rows, out)
        with ExitStack() as ctx:
            xt = sb(ctx, "xt", [128, KD, NP])
            phase(norm_transpose, "n3", sems, sb, x_rows, ident, eps_t, bank, xt, False)
            phase(expert_swiglu, A, sems, sb, bank, xt, x_rows)
        store_rows(nc, sems, x_rows, out)


def store_rows(nc, sems, x_rows, out):
    stored, = sems("out_stored")
    with nc.Block() as block:
        @block.sync
        def _(sp):
            sp.dma_start(out[0:RT * (NT - 1), :].rearrange("(t p) d -> p t d", p=RT),
                         x_rows[:, 0:NT - 1, :]).then_inc(stored, 16)
            sp.dma_start(out[RT * (NT - 1):N, :], x_rows[0:LASTROWS, NT - 1, :]).then_inc(stored, 16)
            sp.wait_ge(stored, START + 32)


def setup(nc, A, sems, sb, x_rows, ident, iota_w, src_t, rel0, base_row, rounds_t, eps_t,
          base_dram, span_dram):
    (x_in, edges_in, ident_zero, ident_done, iota_done, conv, mm_done, mm_stored, bc_loaded,
     tab) = sems("x_in", "edges_in", "ident_zero", "ident_done", "iota_done", "conv", "mm_done",
                 "mm_stored", "bc_loaded", "tab")
    CP = NCH // HALF
    with ExitStack() as ctx:
        dst_t = sb(ctx, "dst_t", [EC, NCH], I32)
        dst_f = sb(ctx, "dst_f", [EC, NCH])
        dst_c = sb(ctx, "dst_c", [CP, HALF, EC], I32)
        dst_cf = sb(ctx, "dst_cf", [CP, HALF, EC])
        lo = sb(ctx, "lo", [CP, HALF])
        hi = sb(ctx, "hi", [CP, HALF])
        span = sb(ctx, "span", [CP, HALF])
        base_bc = sb(ctx, "base_bc", [EC, NCH])
        span_row = sb(ctx, "span_row", [1, NCH])
        widest = sb(ctx, "widest", [1, 1])
        widest_i = sb(ctx, "widest_i", [1, 2], I32)
        iota_i = sb(ctx, "iota_i", [EC, W], I32)
        with nc.Block() as block:
            @block.sync
            def _(sp):
                sp.dma_start(dst_t[:, :], A["dst_t"]).then_inc(edges_in, 16)
                sp.dma_start(dst_c[:, :, :], A["dst_c"]).then_inc(edges_in, 16)
                sp.dma_start(src_t[:, :], A["src_t"]).then_inc(edges_in, 16)
                sp.dma_start(x_rows[:, :, :], A["x_rows"]).then_inc(x_in, 16)
                sp.wait_ge(mm_done, START + 1)
                sp.dma_start(base_dram.rearrange("(p j) -> p j", j=HALF), lo[:, :]).then_inc(mm_stored, 16)
                sp.dma_start(span_dram.rearrange("(p j) -> p j", j=HALF), span[:, :]).then_inc(mm_stored, 16)
                sp.wait_ge(mm_stored, START + 32)
                sp.dma_start(base_bc[:, :], base_dram.rearrange("(o c) -> o c", o=1).broadcast_to((EC, NCH)))\
                  .then_inc(bc_loaded, 16)
                sp.dma_start(span_row[:, :], span_dram.rearrange("(o c) -> o c", o=1)).then_inc(bc_loaded, 16)
                sp.wait_ge(x_in, START + 16)

            @block.gpsimd
            def _(pool):
                nc.gpsimd.memset(ident[:, :], 0.0).then_inc(ident_zero, 1)
                nc.gpsimd.iota(iota_i[:, :], pattern=[[1, W]], base=0, channel_multiplier=0).then_inc(iota_done, 1)
                pool.wait_ge(ident_zero, START + 1)
                nc.gpsimd.affine_select(out=ident[:, :], in_=ident[:, :], compare_op=ALU.not_equal, fill=1.0,
                                        base=0, pattern=[[-1, 128]], channel_multiplier=1).then_inc(ident_done, 1)

            @block.vector
            def _(dve):
                nc.vector.memset(eps_t[:, :], EPS)
                dve.wait_ge(iota_done, START + 1)
                nc.vector.tensor_copy(iota_w[:, :], iota_i[:, :])
                dve.wait_ge(edges_in, START + 48)
                nc.vector.tensor_copy(dst_f[:, :], dst_t[:, :]).then_inc(conv, 1)
                nc.vector.tensor_copy(dst_cf[:, :, :], dst_c[:, :, :]).then_inc(conv, 1)
                dve.wait_ge(conv, START + 2)
                nc.vector.tensor_reduce(lo[:, :], dst_cf[:, :, :], AX, ALU.min).then_inc(conv, 1)
                nc.vector.tensor_reduce(hi[:, :], dst_cf[:, :, :], AX, ALU.max).then_inc(conv, 1)
                dve.wait_ge(conv, START + 4)
                nc.vector.tensor_tensor(span[:, :], hi[:, :], lo[:, :], ALU.subtract).then_inc(mm_done, 1)
                dve.wait_ge(bc_loaded, START + 32)
                nc.vector.tensor_tensor(rel0[:, :], dst_f[:, :], base_bc[:, :], ALU.subtract)
                nc.vector.tensor_copy(base_row[:, :], base_bc[0:1, :])
                nc.vector.tensor_reduce(widest[:, :], span_row[:, :], AX, ALU.max).then_inc(tab, 1)
                dve.wait_ge(tab, START + 1)
                nc.vector.tensor_copy(widest_i[:, 0:1], widest[:, :]).then_inc(tab, 1)
                dve.wait_ge(tab, START + 2)
                nc.vector.tensor_scalar(widest_i[:, 1:2], widest_i[:, 0:1], W.bit_length() - 1, None,
                                        ALU.arith_shift_right).then_inc(tab, 1)
                dve.wait_ge(tab, START + 3)
                nc.vector.tensor_scalar(rounds_t[:, :], widest_i[:, 1:2], 1.0, None, ALU.add)


def norm_transpose(nc, tag, sems, sb, x_rows, ident, eps_t, bank, xt, by_vector):
    stat_done, aggr_done, std_done, rstd_done, *tiles = sems(
        *(f"{tag}_{s}" for s in ("stat", "aggr", "std", "rstd")),
        *(f"{tag}_{s}{j}" for s in ("normed", "turned", "copied") for j in range(GT)))
    normed, turned, copied = tiles[:GT], tiles[GT:2 * GT], tiles[2 * GT:]
    with ExitStack() as ctx:
        stat = sb(ctx, "stat", [RT, NT, 6])
        mv = sb(ctx, "mv", [RT, NT, 2])
        std = sb(ctx, "std", [RT, NT])
        rstd = sb(ctx, "rstd", [RT, NT])
        xn = sb(ctx, "xn", [RT, GT, D])
        with nc.Block() as block:
            @block.vector
            def _(dve):
                with dve.Fori(0, NT) as t:
                    nc.vector.bn_stats(stat[:, bass.ds(t, 1), :], x_rows[:, bass.ds(t, 1), :]).then_inc(stat_done, 1)
                dve.wait_ge(stat_done, START + NT)
                for t in range(NT):
                    ins = nc.vector.bn_aggr(mv[:, t, :], stat[:, t, :])
                ins.then_inc(aggr_done, 1)
                dve.wait_ge(std_done, START + 1)
                nc.vector.reciprocal(rstd[:, :], std[:, :]).then_inc(rstd_done, 1)
                dve.wait_ge(rstd_done, START + 1)
                with dve.Fori(0, NG) as g:
                    for j in range(GT):
                        t = g * GT + j
                        dve.wait_ge(turned[j], START + g)
                        def norm(o, i):
                            return nc.vector.tensor_scalar(o, i, mv[:, bass.ds(t, 1), 0:1].rearrange("p a b -> p (a b)"),
                                                           rstd[:, bass.ds(t, 1)], ALU.subtract, ALU.mult)
                        row = x_rows[:, bass.ds(t, 1), :].rearrange("p a d -> p (a d)")
                        if by_vector:
                            norm(xn[:, j, 0:MUL], row[:, 0:MUL])
                            ins = norm(xn[:, j, MUL:D].rearrange("p (c u) -> p u c", c=3),
                                       row[:, MUL:D].rearrange("p (u c) -> p u c", c=3))
                        else:
                            ins = norm(xn[:, j, :], row)
                        ins.then_inc(normed[j], 1)

            @block.tensor
            def _(pe):
                with pe.Fori(0, NG) as g:
                    for j in range(GT):
                        pe.wait_ge(normed[j], START + g + 1)
                        pe.wait_ge(copied[j], START + g)
                        for k in range(KD):
                            ins = nc.tensor.transpose(bank[j][:, k * RT:(k + 1) * RT], xn[:, j, k * 128:(k + 1) * 128],
                                                      ident[0:RT, 0:RT])
                        ins.then_inc(turned[j], 1)

            @block.scalar
            def _(act):
                act.wait_ge(aggr_done, START + 1)
                nc.scalar.activation(std[:, :], mv[:, :, 1], ACT.Sqrt, bias=eps_t[0:RT, :], scale=1.0).then_inc(std_done, 1)
                with act.Fori(0, NG) as g:
                    for j in range(GT):
                        act.wait_ge(turned[j], START + g + 1)
                        nc.scalar.activation(xt[:, :, bass.ds(g * GC + j * RT, RT)],
                                             bank[j][:, 0:KD * RT].rearrange("p (k r) -> p k r", k=KD),
                                             ACT.Copy).then_inc(copied[j], 1)


def linear_attention(nc, A, sems, sb, bank, xt, mix):
    (w_in, mask_done, staged, kv_mm, kb_done, km_done, ke_done, kf_done, acc_mm, v_done, zero_mm,
     bd_done, q_mm, qm_done, qe_done, qr_done, qf_done, nd_mm, dn_done, rec_done, o_done, out_mm,
     mix_done) = sems(*("a0_" + s for s in (
         "w_in mask staged kv_mm kb km ke kf acc_mm v zero bd q_mm qm qe qr qf nd_mm dn rec o out_mm mix").split()))
    NH = 128 // DH0
    with ExitStack() as ctx:
        wkv = sb(ctx, "wkv", [128, KD, 2 * D])
        wq = sb(ctx, "wq", [128, KD, D])
        wo = sb(ctx, "wo", [128, KD, D])
        bk_bc = sb(ctx, "bk_bc", [RT, D])
        bv_bc = sb(ctx, "bv_bc", [RT, D])
        bq = sb(ctx, "bq", [128, KD])
        bo = sb(ctx, "bo", [128, KD])
        row_bias = sb(ctx, "row_bias", [RT, 2])
        stage = sb(ctx, "stage", [128, KD, GC])
        kb = sb(ctx, "kb", [RT, GT, D])
        km = sb(ctx, "km", [RT, GT, D])
        ke = sb(ctx, "ke", [RT, GT, D])
        vb = sb(ctx, "vb", [RT, GT, D])
        ones = sb(ctx, "ones", [RT, 128])
        zeros = sb(ctx, "zeros", [1, 512])
        kv_bd = sb(ctx, "kv_bd", [128, KD, 128])
        ks_bd = sb(ctx, "ks_bd", [128, KD, 128])
        qm = sb(ctx, "qm", [128, KD, GC])
        qr = sb(ctx, "qr", [128, KD, GC])
        dn = sb(ctx, "dn", [128, KD, GC])
        o_t = sb(ctx, "o_t", [128, KD, GC])
        acc = bank[4]
        with nc.Block() as block:
            @block.sync
            def _(sp):
                for t, name in ((wkv, "wkv0"), (wq, "wq0"), (wo, "wo0")):
                    sp.dma_start(t[:, :, :], A[name].rearrange("(k p) n -> p k n", p=128)).then_inc(w_in, 16)
                for t, name in ((bk_bc, "L0_mix_bk"), (bv_bc, "L0_mix_bv")):
                    sp.dma_start(t[:, :], A[name].rearrange("(o n) -> o n", o=1).broadcast_to((RT, D))).then_inc(w_in, 16)
                for t, name in ((bq, "L0_mix_bq_t"), (bo, "L0_mix_bo_t")):
                    sp.dma_start(t[:, :], A[name]).then_inc(w_in, 16)

            @block.gpsimd
            def _(pool):
                nc.gpsimd.memset(ones[:, :], 1.0).then_inc(mask_done, 1)
                nc.gpsimd.memset(zeros[:, :], 0.0).then_inc(mask_done, 1)
                nc.gpsimd.memset(row_bias[:, :], 0.0).then_inc(mask_done, 1)
                nc.gpsimd.memset(kv_bd[:, :, :], 0.0).then_inc(mask_done, 1)
                nc.gpsimd.memset(ks_bd[:, :, :], 0.0).then_inc(mask_done, 1)
                pool.wait_ge(mask_done, START + 5)
                nc.gpsimd.affine_select(out=row_bias[:, 1:2], in_=row_bias[:, 1:2], compare_op=ALU.is_ge, fill=NEG,
                                        base=LASTROWS - 1, pattern=[[0, 1]], channel_multiplier=-1).then_inc(mask_done, 1)
                with pool.Fori(0, NG) as g:
                    pool.wait_ge(kv_mm, START + g * GT)
                    nc.gpsimd.tensor_copy(stage[:, :, :], xt[:, :, bass.ds(g * GC, GC)]).then_inc(staged, 1)

            @block.tensor
            def _(pe):
                pe.wait_ge(w_in, START + 16 * 7)
                pe.wait_ge(mask_done, START + 6)
                nc.tensor.matmul(acc[:, :], zeros[:, 0:128], zeros[:, :], start=True, stop=False, skip_group_check=True)
                with pe.Fori(0, NG) as g:
                    pe.wait_ge(staged, START + g + 1)
                    for j in range(GT):
                        pe.wait_ge(v_done, START + g * GT)
                        for k in range(KD):
                            ins = nc.tensor.matmul(bank[j][0:RT, :], stage[:, k, j * RT:(j + 1) * RT], wkv[:, k, :],
                                                   start=(k == 0), stop=(k == KD - 1))
                        ins.then_inc(kv_mm, 1)
                    for j in range(GT):
                        pe.wait_ge(kf_done, START + g * GT + j + 1)
                        pe.wait_ge(v_done, START + g * GT + j + 1)
                        for k in range(KD):
                            f = slice(k * 128, (k + 1) * 128)
                            nc.tensor.matmul(acc[:, k * 256:k * 256 + 128], km[:, j, f], vb[:, j, f],
                                             start=False, stop=False, skip_group_check=True)
                            ins = nc.tensor.matmul(acc[:, k * 256 + 128:k * 256 + 256], km[:, j, f], ones[:, :],
                                                   start=False, stop=False, skip_group_check=True)
                        ins.then_inc(acc_mm, 1)
                nc.tensor.matmul(acc[:, :], zeros[:, 0:128], zeros[:, :], start=False, stop=True,
                                 skip_group_check=True).then_inc(zero_mm, 1)
                pe.wait_ge(bd_done, START + 1)
                with pe.Fori(0, NG) as g:
                    cols = bass.ds(g * GC, GC)
                    pe.wait_ge(qr_done, START + g * KD)
                    for f in range(KD):
                        for k in range(KD):
                            ins = nc.tensor.matmul(bank[f][:, 0:GC], wq[:, k, f * 128:(f + 1) * 128], xt[:, k, cols],
                                                   start=(k == 0), stop=(k == KD - 1))
                        ins.then_inc(q_mm, 1)
                    pe.wait_ge(o_done, START + g)
                    for f in range(KD):
                        pe.wait_ge(qf_done, START + g * KD + f + 1)
                        nc.tensor.matmul(bank[2 + f][:, 0:GC], kv_bd[:, f, :], qr[:, f, :], start=True, stop=True)
                        ins = nc.tensor.matmul(bank[5 + f][:, 0:GC], ks_bd[:, f, :], qr[:, f, :], start=True, stop=True)
                        ins.then_inc(nd_mm, 1)
                    pe.wait_ge(o_done, START + g + 1)
                    pe.wait_ge(mix_done, START + g * KD)
                    for f in range(KD):
                        b = (4, 7)[f]
                        for k in range(KD):
                            ins = nc.tensor.matmul(bank[b][:, 0:GC], wo[:, k, f * 128:(f + 1) * 128], o_t[:, k, :],
                                                   start=(k == 0), stop=(k == KD - 1))
                        ins.then_inc(out_mm, 1)

            @block.vector
            def _(dve):
                dve.wait_ge(w_in, START + 16 * 7)
                dve.wait_ge(mask_done, START + 6)

                def keys(g, last):
                    for j in range(GT):
                        n = g * GT + j
                        dve.wait_ge(kv_mm, START + n + 1)
                        dve.wait_ge(acc_mm, START + g * GT)
                        pad = 1 if last and j == GT - 1 else 0
                        nc.vector.scalar_tensor_tensor(out=kb[:, j, :], in0=bank[j][0:RT, 0:D],
                                                       scalar=row_bias[:, pad:pad + 1], in1=bk_bc[:, :],
                                                       op0=ALU.add, op1=ALU.add).then_inc(kb_done, 1)
                        nc.vector.tensor_tensor(vb[:, j, :], bank[j][0:RT, D:2 * D], bv_bc[:, :], ALU.add).then_inc(v_done, 1)
                        dve.wait_ge(kb_done, START + n + 1)
                        nc.vector.tensor_scalar(km[:, j, :], kb[:, j, :], 0.0, None, ALU.min).then_inc(km_done, 1)
                    for j in range(GT):
                        n = g * GT + j
                        dve.wait_ge(ke_done, START + n + 1)
                        nc.vector.scalar_tensor_tensor(out=km[:, j, :], in0=kb[:, j, :], scalar=0.0, in1=ke[:, j, :],
                                                       op0=ALU.max, op1=ALU.add).then_inc(kf_done, 1)
                with dve.Fori(0, NG - 1) as g:
                    keys(g, False)
                keys(NG - 1, True)
                dve.wait_ge(zero_mm, START + 1)
                for f in range(KD):
                    for h in range(NH):
                        s = slice(h * DH0, (h + 1) * DH0)
                        nc.vector.tensor_copy(kv_bd[s, f, s], acc[s, f * 256 + h * DH0:f * 256 + (h + 1) * DH0])
                        ins = nc.vector.tensor_copy(ks_bd[s, f, s], acc[s, f * 256 + 128:f * 256 + 128 + DH0])
                ins.then_inc(bd_done, 1)
                with dve.Fori(0, NG) as g:
                    for f in range(KD):
                        n = g * KD + f
                        dve.wait_ge(q_mm, START + n + 1)
                        nc.vector.tensor_scalar(qm[:, f, :], bank[f][:, 0:GC], bq[:, f:f + 1], 0.0, ALU.add, ALU.min)\
                          .then_inc(qm_done, 1)
                    for f in range(KD):
                        n = g * KD + f
                        dve.wait_ge(qe_done, START + n + 1)
                        dve.wait_ge(qr_done, START + n + 1)
                        nc.vector.tensor_tensor(qr[:, f, :], qr[:, f, :], qm[:, f, :], ALU.add).then_inc(qf_done, 1)
                    for f in range(KD):
                        n = g * KD + f
                        dve.wait_ge(nd_mm, START + n + 1)
                        nc.vector.tensor_scalar(dn[:, f, :], bank[5 + f][:, 0:GC], 1e-6, None, ALU.add).then_inc(dn_done, 1)
                        dve.wait_ge(dn_done, START + n + 1)
                        nc.vector.reciprocal(dn[:, f, :], dn[:, f, :]).then_inc(rec_done, 1)
                        dve.wait_ge(rec_done, START + n + 1)
                        dve.wait_ge(out_mm, START + g * KD)
                        ins = nc.vector.tensor_tensor(o_t[:, f, :], bank[2 + f][:, 0:GC], dn[:, f, :], ALU.mult)
                    ins.then_inc(o_done, 1)

            @block.scalar
            def _(act):
                with act.Fori(0, NG * GT // GT) as g:
                    for j in range(GT):
                        act.wait_ge(km_done, START + g * GT + j + 1)
                        act.wait_ge(kf_done, START + g * GT)
                        nc.scalar.activation(ke[:, j, :], km[:, j, :], ACT.Exp).then_inc(ke_done, 1)
                act.wait_ge(w_in, START + 16 * 7)
                with act.Fori(0, NG) as g:
                    for f in range(KD):
                        n = g * KD + f
                        act.wait_ge(nd_mm, START + g * KD)
                        act.wait_ge(q_mm, START + n + 1)
                        act.wait_ge(qm_done, START + n + 1)
                        nc.scalar.activation(qr[:, f, :], bank[f][:, 0:GC], ACT.Relu, bias=bq[:, f:f + 1], scale=1.0)\
                          .then_inc(qr_done, 1)
                        nc.scalar.activation(qm[:, f, :], qm[:, f, :], ACT.Exp).then_inc(qe_done, 1)
                    for f in range(KD):
                        n = g * KD + f
                        act.wait_ge(out_mm, START + n + 1)
                        nc.scalar.activation(mix[:, f, bass.ds(g * GC, GC)], bank[(4, 7)[f]][:, 0:GC], ACT.Identity,
                                             bias=bo[:, f:f + 1], scale=1.0).then_inc(mix_done, 1)


def gated_graph(nc, A, sems, sb, bank, tables, nf, h_dram):
    src_t, rel0, base_row, rounds_t, iota_w = tables
    (w_in, bias_done, t1_mm, t1_done, h_mm, h_done, h_stored, acc_zero, tab, hot_a, hot_b, sum_a, sum_b,
     added, idx_a, idx_b, r_mm, hn_mm, xn_mm, z_mm, r_done, hn_used, t_done, n_done, z_done, blend,
     nf_done, passed, *gathered) = sems(*("g_" + s for s in (
         "w_in bias t1_mm t1 h_mm h h_stored acc_zero tab hot_a hot_b sum_a sum_b added idx_a idx_b "
         "r_mm hn_mm xn_mm z_mm r hn_used t n z blend nf passed").split()),
                              *(f"g_gathered{j}" for j in range(ITC)))
    hot_ready, summed, idx_ready = (hot_a, hot_b), (sum_a, sum_b), (idx_a, idx_b)
    with ExitStack() as ctx:
        w1 = sb(ctx, "w1", [128, KD, D])
        w2 = sb(ctx, "w2", [128, KD, D])
        wih = sb(ctx, "wih", [128, KD, 3 * D])
        whh = sb(ctx, "whh", [128, KD, 3 * D])
        b1 = sb(ctx, "b1", [128, KD])
        b2_bc = sb(ctx, "b2_bc", [RT, D])
        bih = sb(ctx, "bih", [128, 3 * KD])
        bhh = sb(ctx, "bhh", [128, 3 * KD])
        bsum = sb(ctx, "bsum", [128, 3 * KD])
        msg = sb(ctx, "msg", [128, KD, NP])
        rel = sb(ctx, "rel", [EC, NCH])
        base = sb(ctx, "base", [1, NCH], I32)
        idx = sb(ctx, "idx", [EC, 2, HALF], I32)
        rows = [sb(ctx, f"rows{j}", [EC, D]) for j in range(ITC)]
        hot = sb(ctx, "hot", [EC, 2, HALF, W])
        t1 = sb(ctx, "t1", [128, KD, GC])
        h_rows = sb(ctx, "h_rows", [RT, GT, D])
        r_t = sb(ctx, "r_t", [128, KD, GC])
        t_t = sb(ctx, "t_t", [128, KD, GC])
        n_t = sb(ctx, "n_t", [128, KD, GC])
        z_t = sb(ctx, "z_t", [128, KD, GC])
        d_t = sb(ctx, "d_t", [128, KD, GC])
        p_sum = bank[0:2]
        p_r, p_hn, p_xn, p_z = bank[2:6]
        p_t1 = bank[6:8]
        p_h = (p_r, p_hn, p_xn, p_z)

        def begin(eng, tag):
            rounds = eng.value_load(rounds_t[0:1, 0:1], min_val=1, max_val=NP // W)
            reg = eng.alloc_register(f"g_its_{tag}")
            eng.reg_mov(reg, 0)
            return rounds, reg

        def count(eng, reg):
            return eng.snap(reg, min_val=0, max_val=STEPS * NIT * (NP // W))

        with nc.Block() as block:
            @block.sync
            def _(sp):
                for t, name in ((w1, "w1_0"), (w2, "w2_0"), (wih, "wih_0"), (whh, "whh_0")):
                    sp.dma_start(t[:, :, :], A[name].rearrange("(k p) n -> p k n", p=128)).then_inc(w_in, 16)
                for t, name in ((b1, "L0_gnn_b1_t"), (bih, "L0_gnn_b_ih_t"), (bhh, "L0_gnn_b_hh_t")):
                    sp.dma_start(t[:, :], A[name]).then_inc(w_in, 16)
                sp.dma_start(b2_bc[:, :], A["L0_gnn_b2"].rearrange("(o n) -> o n", o=1).broadcast_to((RT, D))).then_inc(w_in, 16)
                with sp.Fori(0, STEPS) as s:
                    with sp.Fori(0, NG) as g:
                        sp.wait_ge(h_done, START + (s * NG + g) * GT + GT)
                        sp.dma_start(h_dram[bass.ds(g * GC, GC), :].rearrange("(j p) d -> p j d", p=RT),
                                     h_rows[:, :, :]).then_inc(h_stored, 16)
                        wait_alone(sp, h_stored, (s * NG + g) * 16 + 16, passed)

            @block.gpsimd
            def _(pool):
                rounds, reg = begin(pool, "pool")
                with pool.Fori(0, STEPS) as s:
                    wait_alone(pool, z_mm, s * NG * KD, passed)
                    nc.gpsimd.memset(msg[:, :, :], 0.0).then_inc(acc_zero, 1)
                    wait_alone(pool, h_stored, s * NG * 16 + NG * 16, passed)
                    with pool.Fori(0, rounds) as r:
                        with pool.Fori(0, NIT) as i:
                            its = count(pool, reg)
                            for b in range(2):
                                wait_alone(pool, summed[b], its + i, passed)
                                nc.gpsimd.tensor_copy(idx[:, b, :], src_t[:, bass.ds(i * ITC + b * HALF, HALF)])\
                                  .then_inc(idx_ready[b], 1)
                                wait_alone(pool, idx_ready[b], its + i + 1, passed)
                                for j in range(HALF):
                                    nc.gpsimd.indirect_dma_start(
                                        out=rows[b * HALF + j][:, :], out_offset=None, in_=h_dram,
                                        in_offset=bass.IndirectOffsetOnAxis(ap=idx[:, b, j:j + 1], axis=0),
                                    ).then_inc(gathered[b * HALF + j], 16)
                        pool.reg_add(reg, reg, NIT)

            @block.tensor
            def _(pe):
                rounds, reg = begin(pe, "pe")
                pe.wait_ge(w_in, START + 16 * 8)
                with pe.Fori(0, STEPS) as s:
                    wait_alone(pe, nf_done, s * NG, passed)
                    with pe.Fori(0, NG) as g:
                        q = s * NG + g
                        cols = bass.ds(g * GC, GC)
                        for f in range(KD):
                            pe.wait_ge(t1_done, START + q * KD)
                            for k in range(KD):
                                ins = nc.tensor.matmul(p_t1[f][:, 0:GC], w1[:, k, f * 128:(f + 1) * 128], nf[:, k, cols],
                                                       start=(k == 0), stop=(k == KD - 1))
                            ins.then_inc(t1_mm, 1)
                        pe.wait_ge(t1_done, START + q * KD + KD)
                        pe.wait_ge(h_done, START + q * GT)
                        for j in range(GT):
                            for k in range(KD):
                                ins = nc.tensor.matmul(p_h[j][0:RT, 0:D],
                                                       t1[:, k, j * RT:(j + 1) * RT], w2[:, k, :],
                                                       start=(k == 0), stop=(k == KD - 1))
                            ins.then_inc(h_mm, 1)
                    with pe.Fori(0, rounds) as r:
                        with pe.Fori(0, NIT) as i:
                            its = count(pe, reg)
                            for b in range(2):
                                pe.wait_ge(hot_ready[b], START + its + i + 1)
                                pe.wait_ge(added, START + (its + i) * ITC)
                                for j in range(HALF):
                                    pe.wait_ge(gathered[b * HALF + j], (its + i) * 16 + 16)
                                    for k in range(KD):
                                        o = (j * KD + k) * W
                                        ins = nc.tensor.matmul(p_sum[b][:, o:o + W],
                                                               rows[b * HALF + j][:, k * 128:(k + 1) * 128],
                                                               hot[:, b, j, :], start=True, stop=True)
                                ins.then_inc(summed[b], 1)
                        pe.reg_add(reg, reg, NIT)
                    wait_alone(pe, added, count(pe, reg) * ITC, passed)
                    with pe.Fori(0, NG) as g:
                        cols = bass.ds(g * GC, GC)
                        for f in range(KD):
                            q = (s * NG + g) * KD + f

                            def gate(out_p, n, parts):
                                ws = [(w, src, k) for w, src in parts for k in range(KD)]
                                for m, (w, src, k) in enumerate(ws):
                                    ins = nc.tensor.matmul(out_p[:, 0:GC], w[:, k, n * D + f * 128:n * D + (f + 1) * 128],
                                                           src[:, k, cols], start=(m == 0), stop=(m == len(ws) - 1))
                                return ins
                            pe.wait_ge(r_done, START + q)
                            gate(p_r, 0, ((wih, msg), (whh, nf))).then_inc(r_mm, 1)
                            pe.wait_ge(hn_used, START + q)
                            gate(p_hn, 2, ((whh, nf),)).then_inc(hn_mm, 1)
                            pe.wait_ge(t_done, START + q)
                            gate(p_xn, 2, ((wih, msg),)).then_inc(xn_mm, 1)
                            pe.wait_ge(z_done, START + q)
                            gate(p_z, 1, ((wih, msg), (whh, nf))).then_inc(z_mm, 1)

            @block.vector
            def _(dve):
                rounds, reg = begin(dve, "dve")
                tabs = dve.alloc_register("g_tabs")
                dve.reg_mov(tabs, 0)
                dve.wait_ge(w_in, START + 16 * 8)
                nc.vector.tensor_tensor(bsum[:, :], bih[:, :], bhh[:, :], ALU.add).then_inc(bias_done, 1)
                with dve.Fori(0, STEPS) as s:
                    nc.vector.tensor_copy(rel[:, :], rel0[:, :]).then_inc(tab, 1)
                    nc.vector.tensor_copy(base[:, :], base_row[:, :]).then_inc(tab, 1)
                    dve.reg_add(tabs, tabs, 2)
                    with dve.Fori(0, NG) as g:
                        q = s * NG + g
                        dve.wait_ge(h_stored, START + q * 16)
                        for j in range(GT):
                            dve.wait_ge(h_mm, START + q * GT + j + 1)
                            nc.vector.tensor_tensor(h_rows[:, j, :], p_h[j][0:RT, 0:D],
                                                    b2_bc[:, :], ALU.add).then_inc(h_done, 1)
                    wait_alone(dve, acc_zero, s + 1, passed)
                    with dve.Fori(0, rounds) as r:
                        wait_alone(dve, tab, dve.snap(tabs, min_val=0, max_val=1 << 20), passed)
                        with dve.Fori(0, NIT) as i:
                            its = count(dve, reg)
                            for b in range(2):
                                dve.wait_ge(summed[b], START + its + i)
                                nc.vector.tensor_tensor(
                                    hot[:, b, :, :],
                                    iota_w[:, :].rearrange("p (o w) -> p o w", o=1).broadcast_to((EC, HALF, W)),
                                    rel[:, bass.ds(i * ITC + b * HALF, HALF)].rearrange("p (c o) -> p c o", o=1)
                                    .broadcast_to((EC, HALF, W)), ALU.is_equal).then_inc(hot_ready[b], 1)
                            for b in range(2):
                                at = [dve.value_load(base[0:1, bass.ds(i * ITC + b * HALF + j, 1)], min_val=0, max_val=TOPBASE)
                                      for j in range(HALF)]
                                dve.wait_ge(summed[b], START + its + i + 1)
                                for j in range(HALF):
                                    c = b * HALF + j
                                    dve.wait_ge(added, START + (its + i) * ITC + c)
                                    win = msg[:, :, bass.ds(at[j], W)]
                                    nc.vector.tensor_tensor(
                                        win, win, p_sum[b][:, j * KD * W:(j + 1) * KD * W].rearrange("p (k w) -> p k w", k=KD),
                                        ALU.add).then_inc(added, 1)
                        dve.reg_add(reg, reg, NIT)
                        nc.vector.tensor_scalar(rel[:, :], rel[:, :], float(W), None, ALU.subtract).then_inc(tab, 1)
                        nc.vector.tensor_scalar(base[:, :], base[:, :], float(W), float(TOPBASE), ALU.add, ALU.min)\
                          .then_inc(tab, 1)
                        dve.reg_add(tabs, tabs, 2)
                    with dve.Fori(0, NG) as g:
                        cols = bass.ds(g * GC, GC)
                        for f in range(KD):
                            q = (s * NG + g) * KD + f
                            dve.wait_ge(hn_mm, START + q + 1)
                            dve.wait_ge(r_done, START + q + 1)
                            nc.vector.scalar_tensor_tensor(out=t_t[:, f, :], in0=p_hn[:, 0:GC],
                                                           scalar=bhh[:, 2 * KD + f:2 * KD + f + 1], in1=r_t[:, f, :],
                                                           op0=ALU.add, op1=ALU.mult).then_inc(hn_used, 1)
                            dve.wait_ge(hn_used, START + q + 1)
                            dve.wait_ge(xn_mm, START + q + 1)
                            nc.vector.tensor_tensor(t_t[:, f, :], t_t[:, f, :], p_xn[:, 0:GC], ALU.add).then_inc(t_done, 1)
                        q = s * NG + g
                        dve.wait_ge(n_done, START + q * KD + KD)
                        dve.wait_ge(z_done, START + q * KD + KD)
                        nc.vector.tensor_tensor(d_t[:, :, :], nf[:, :, cols], n_t[:, :, :], ALU.subtract).then_inc(blend, 1)
                        dve.wait_ge(blend, START + q * 2 + 1)
                        nc.vector.tensor_tensor(d_t[:, :, :], d_t[:, :, :], z_t[:, :, :], ALU.mult).then_inc(blend, 1)
                        dve.wait_ge(blend, START + q * 2 + 2)
                        nc.vector.tensor_tensor(nf[:, :, cols], d_t[:, :, :], n_t[:, :, :], ALU.add).then_inc(nf_done, 1)

            @block.scalar
            def _(act):
                act.wait_ge(w_in, START + 16 * 8)
                act.wait_ge(bias_done, START + 1)
                with act.Fori(0, STEPS) as s:
                    with act.Fori(0, NG) as g:
                        q = s * NG + g
                        act.wait_ge(h_mm, START + q * GT)
                        for f in range(KD):
                            act.wait_ge(t1_mm, START + q * KD + f + 1)
                            nc.scalar.activation(t1[:, f, :], p_t1[f][:, 0:GC], ACT.Relu, bias=b1[:, f:f + 1], scale=1.0)\
                              .then_inc(t1_done, 1)
                    with act.Fori(0, NG) as g:
                        for f in range(KD):
                            q = (s * NG + g) * KD + f
                            act.wait_ge(r_mm, START + q + 1)
                            act.wait_ge(hn_used, START + q)
                            nc.scalar.activation(r_t[:, f, :], p_r[:, 0:GC], ACT.Sigmoid, bias=bsum[:, f:f + 1], scale=1.0)\
                              .then_inc(r_done, 1)
                            act.wait_ge(t_done, START + q + 1)
                            act.wait_ge(nf_done, START + s * NG + g)
                            nc.scalar.activation(n_t[:, f, :], t_t[:, f, :], ACT.Tanh,
                                                 bias=bih[:, 2 * KD + f:2 * KD + f + 1], scale=1.0).then_inc(n_done, 1)
                            act.wait_ge(z_mm, START + q + 1)
                            nc.scalar.activation(z_t[:, f, :], p_z[:, 0:GC], ACT.Sigmoid, bias=bsum[:, KD + f:KD + f + 1],
                                                 scale=1.0).then_inc(z_done, 1)


def add_transposed(nc, sems, bank, sb, ident, x_rows, a_t, b_t):
    summed, turned, added = sems("at_summed", "at_turned", "at_added")
    with ExitStack() as ctx:
        s_t = sb(ctx, "s_t", [128, KD, GC])
        with nc.Block() as block:
            @block.gpsimd
            def _(pool):
                with pool.Fori(0, NG) as g:
                    cols = bass.ds(g * GC, GC)
                    pool.wait_ge(turned, START + g * GT)
                    nc.gpsimd.tensor_tensor(s_t[:, :, :], a_t[:, :, cols], b_t[:, :, cols], ALU.add).then_inc(summed, 1)

            @block.tensor
            def _(pe):
                with pe.Fori(0, NG) as g:
                    pe.wait_ge(summed, START + g + 1)
                    pe.wait_ge(added, START + g * GT)
                    for j in range(GT):
                        for k in range(KD):
                            ins = nc.tensor.transpose(bank[j][0:RT, k * 128:(k + 1) * 128], s_t[:, k, j * RT:(j + 1) * RT],
                                                      ident[:, :])
                        ins.then_inc(turned, 1)

            @block.vector
            def _(dve):
                with dve.Fori(0, NG) as g:
                    for j in range(GT):
                        dve.wait_ge(turned, START + g * GT + j + 1)
                        row = x_rows[:, bass.ds(g * GT + j, 1), :].rearrange("p a d -> p (a d)")
                        nc.vector.tensor_tensor(row, row, bank[j][0:RT, 0:D], ALU.add).then_inc(added, 1)


def route(nc, tag, A, sems, sb, bank, xt, gates, hidden, count, w_names, b_names):
    (w_in, hid_mm, hid_done, lg_mm, lg_done, step, ex_done, staged, top_done, gate_done) = sems(*(f"{tag}_{s}" for s in (
        "w_in hid_mm hid lg_mm lg step exp staged top gate").split()))
    nw = len(w_names) + len(b_names)
    with ExitStack() as ctx:
        w1 = sb(ctx, "rw1", [128, KD, 128 if hidden else 8])
        w2 = sb(ctx, "rw2", [128, 8])
        b1 = sb(ctx, "rb1", [128, 1])
        b2 = sb(ctx, "rb2", [RT, 8])
        rh = sb(ctx, "rh", [128, KD, GC])
        lg = sb(ctx, "lg", [RT, NT, 8])
        pr = sb(ctx, "pr", [RT, NT, 8])
        mx = sb(ctx, "mx", [RT, NT])
        best = sb(ctx, "best", [RT, NT, 8])
        at = sb(ctx, "at", [RT, NT, 8], U32)
        at_f = sb(ctx, "at_f", [RT, NT, 8])
        iota_i = sb(ctx, "iota8i", [RT, 8], I32)
        iota_f = sb(ctx, "iota8", [RT, 8])
        wt = sb(ctx, "wt", [RT, NT, 2])
        one = sb(ctx, "one", [RT, NT, 8])
        with nc.Block() as block:
            @block.sync
            def _(sp):
                sp.wait_ge(step, START + 1)
                sp.dma_start(w1[:, :, :], A[w_names[0]].rearrange("(k p) n -> p k n", p=128)).then_inc(w_in, 16)
                if hidden:
                    sp.dma_start(w2[:, :], A[w_names[1]]).then_inc(w_in, 16)
                    sp.dma_start(b1[:, :], A[b_names[0]].rearrange("(p o) -> p o", o=1)).then_inc(w_in, 16)
                    sp.dma_start(b2[:, 0:count], A[b_names[1]].rearrange("(o n) -> o n", o=1).broadcast_to((RT, count)))\
                      .then_inc(w_in, 16)

            @block.gpsimd
            def _(pool):
                nc.gpsimd.iota(iota_i[:, :], pattern=[[1, 8]], base=0, channel_multiplier=0).then_inc(staged, 1)
                if not hidden:
                    with pool.Fori(0, NG) as g:
                        pool.wait_ge(lg_mm, START + g)
                        nc.gpsimd.tensor_copy(rh[:, :, :], xt[:, :, bass.ds(g * GC, GC)]).then_inc(hid_done, 1)

            @block.tensor
            def _(pe):
                pe.wait_ge(w_in, START + 16 * nw)
                with pe.Fori(0, NG) as g:
                    if hidden:
                        pe.wait_ge(hid_done, START + g)
                        for k in range(KD):
                            ins = nc.tensor.matmul(bank[0][:, 0:GC], w1[:, k, :], xt[:, k, bass.ds(g * GC, GC)],
                                                   start=(k == 0), stop=(k == KD - 1))
                        ins.then_inc(hid_mm, 1)
                    pe.wait_ge(hid_done, START + g + 1)
                    pe.wait_ge(lg_done, START + g)
                    for j in range(GT):
                        for k in range(1 if hidden else KD):
                            ins = nc.tensor.matmul(bank[1][0:RT, j * 8:j * 8 + 8], rh[:, k, j * RT:(j + 1) * RT],
                                                   w2[:, :] if hidden else w1[:, k, :],
                                                   start=(k == 0), stop=(hidden or k == KD - 1))
                    ins.then_inc(lg_mm, 1)

            @block.scalar
            def _(act):
                if hidden:
                    act.wait_ge(w_in, START + 16 * nw)
                    with act.Fori(0, NG) as g:
                        act.wait_ge(hid_mm, START + g + 1)
                        act.wait_ge(lg_mm, START + g)
                        nc.scalar.activation(rh[:, 0, :], bank[0][:, 0:GC], ACT.Relu, bias=b1[:, :], scale=1.0)\
                          .then_inc(hid_done, 1)
                act.wait_ge(step, START + 3)
                nc.scalar.activation(pr[:, :, :], lg[:, :, :], ACT.Exp).then_inc(ex_done, 1)
                if hidden:
                    act.wait_ge(step, START + 6)
                    nc.scalar.activation(wt[:, :, 1], mx[:, :], ACT.Exp).then_inc(ex_done, 1)

            @block.vector
            def _(dve):
                n = [0]

                def then(ins):
                    n[0] += 1
                    ins.then_inc(step, 1)
                    dve.wait_ge(step, START + n[0])

                def per_node(a):
                    return a.rearrange("p (t o) -> p t o", o=1).broadcast_to((RT, NT, 8))
                then(nc.vector.memset(b2[:, :], NEG if count < 8 else 0.0))
                if hidden:
                    dve.wait_ge(w_in, START + 16 * nw)
                with dve.Fori(0, NG) as g:
                    dve.wait_ge(lg_mm, START + g + 1)
                    nc.vector.tensor_tensor(lg[:, bass.ds(g * GT, GT), :],
                                            bank[1][0:RT, 0:GT * 8].rearrange("p (j e) -> p j e", j=GT),
                                            b2[:, :].rearrange("p (o e) -> p o e", o=1).broadcast_to((RT, GT, 8)),
                                            ALU.add).then_inc(lg_done, 1)
                dve.wait_ge(lg_done, START + NG)
                then(nc.vector.tensor_reduce(mx[:, :], lg[:, :, :], AX, ALU.max))
                then(nc.vector.tensor_tensor(lg[:, :, :], lg[:, :, :], per_node(mx[:, :]), ALU.subtract))
                dve.wait_ge(ex_done, START + 1)
                then(nc.vector.tensor_reduce(mx[:, :], pr[:, :, :], AX, ALU.add))
                then(nc.vector.reciprocal(mx[:, :], mx[:, :]))
                nc.vector.tensor_tensor(pr[:, :, :], pr[:, :, :], per_node(mx[:, :]), ALU.mult).then_inc(top_done, 1)
                dve.wait_ge(top_done, START + 1)
                for t in range(NT):
                    nc.vector.max(best[:, t, :], pr[:, t, :]).then_inc(top_done, 1)
                dve.wait_ge(top_done, START + NT + 1)
                for t in range(NT):
                    nc.vector.max_index(at[:, t, :], best[:, t, :], pr[:, t, :]).then_inc(top_done, 1)
                if hidden:
                    then(nc.vector.tensor_tensor(mx[:, :], best[:, :, 1], best[:, :, 0], ALU.subtract))
                    dve.wait_ge(ex_done, START + 2)
                    then(nc.vector.tensor_scalar(mx[:, :], wt[:, :, 1], 1.0, None, ALU.add))
                    then(nc.vector.reciprocal(wt[:, :, 0], mx[:, :]))
                    then(nc.vector.tensor_tensor(wt[:, :, 1], wt[:, :, 1], wt[:, :, 0], ALU.mult))
                else:
                    then(nc.vector.tensor_tensor(mx[:, :], best[:, :, 1], best[:, :, 0], ALU.add))
                    then(nc.vector.tensor_scalar(mx[:, :], mx[:, :], 1e-9, None, ALU.add))
                    then(nc.vector.reciprocal(mx[:, :], mx[:, :]))
                    nc.vector.tensor_tensor(wt[:, :, 0], best[:, :, 0], mx[:, :], ALU.mult)
                    then(nc.vector.tensor_tensor(wt[:, :, 1], best[:, :, 1], mx[:, :], ALU.mult))
                dve.wait_ge(top_done, START + 2 * NT + 1)
                dve.wait_ge(staged, START + 1)
                nc.vector.tensor_copy(iota_f[:, :], iota_i[:, :])
                then(nc.vector.tensor_copy(at_f[:, :, :], at[:, :, :]))
                every = iota_f[:, :].rearrange("p (o e) -> p o e", o=1).broadcast_to((RT, NT, 8))
                for c, to in ((0, gates), (1, one)):
                    then(nc.vector.tensor_tensor(to[:, :, :], every, at_f[:, :, c:c + 1].broadcast_to((RT, NT, 8)), ALU.is_equal))
                    then(nc.vector.tensor_tensor(to[:, :, :], to[:, :, :], wt[:, :, c:c + 1].broadcast_to((RT, NT, 8)), ALU.mult))
                nc.vector.tensor_tensor(gates[:, :, :], gates[:, :, :], one[:, :, :], ALU.add)


def expert_mlp(nc, A, sems, sb, bank, xt, x_rows):
    w_in, ones_done, h1_mm, h1_done, h2_mm, h2_done, y_mm, y_done = sems(*("e0_" + s for s in (
        "w_in ones h1_mm h1 h2_mm h2 y_mm y").split()))
    with ExitStack() as ctx:
        gates = sb(ctx, "gates", [RT, NT, 8])
        route(nc, "r0", A, sems, sb, bank, xt, gates, True, E0, ("L0_ffn_router_w1", "rw2_0"),
              ("L0_ffn_router_b1", "L0_ffn_router_b2"))
        w = [sb(ctx, f"ew{i}", [128, E0, KD, D]) for i in range(3)]
        b1 = sb(ctx, "eb1", [128, E0, KD])
        b2 = sb(ctx, "eb2", [128, E0, KD])
        b3 = sb(ctx, "eb3", [1, E0, D])
        ones = sb(ctx, "ones", [1, RT])
        h1 = sb(ctx, "h1", [128, 2, KD, GC])
        h2 = sb(ctx, "h2", [128, 2, KD, GC])
        with nc.Block() as block:
            @block.sync
            def _(sp):
                for t, name in zip(w, ("L0_ffn_expert_w1", "L0_ffn_expert_w2", "L0_ffn_expert_w3")):
                    for e in range(E0):
                        sp.dma_start(t[:, e, :, :], A[name][e].rearrange("(k p) n -> p k n", p=128)).then_inc(w_in, 16)
                for t, name in ((b1, "L0_ffn_expert_b1_t"), (b2, "L0_ffn_expert_b2_t")):
                    sp.dma_start(t[:, :, :], A[name]).then_inc(w_in, 16)
                sp.dma_start(b3[:, :, :], A["L0_ffn_expert_b3"].rearrange("(o e) n -> o e n", o=1)).then_inc(w_in, 16)
            NW = 16 * (3 * E0 + 3)

            @block.tensor
            def _(pe):
                pe.wait_ge(w_in, START + NW)
                pe.wait_ge(ones_done, START + 1)
                with pe.Fori(0, NG) as g:
                    cols = bass.ds(g * GC, GC)

                    def layer1(e):
                        pe.wait_ge(h1_done, START + (g * E0 + e) * KD)
                        for f in range(KD):
                            for k in range(KD):
                                ins = nc.tensor.matmul(bank[f][:, 0:GC], w[0][:, e, k, f * 128:(f + 1) * 128], xt[:, k, cols],
                                                       start=(k == 0), stop=(k == KD - 1))
                            ins.then_inc(h1_mm, 1)

                    def layer2(e):
                        pe.wait_ge(h1_done, START + (g * E0 + e) * KD + KD)
                        pe.wait_ge(h2_done, START + (g * E0 + e) * KD)
                        for f in range(KD):
                            for k in range(KD):
                                ins = nc.tensor.matmul(bank[2 + f][:, 0:GC], w[1][:, e, k, f * 128:(f + 1) * 128],
                                                       h1[:, e % 2, k, :], start=(k == 0), stop=(k == KD - 1))
                            ins.then_inc(h2_mm, 1)

                    def layer3(e):
                        pe.wait_ge(h2_done, START + (g * E0 + e) * KD + KD)
                        pe.wait_ge(y_done, START + (g * E0 + e) * GT)
                        for j in range(GT):
                            o = bank[4 + j][0:RT, 0:D]
                            for k in range(KD):
                                nc.tensor.matmul(o, h2[:, e % 2, k, j * RT:(j + 1) * RT], w[2][:, e, k, :],
                                                 start=(k == 0), stop=False)
                            nc.tensor.matmul(o, ones[:, :], b3[:, e, :], start=False, stop=True).then_inc(y_mm, 1)
                    layer1(0)
                    for e in range(E0):
                        layer2(e)
                        if e + 1 < E0:
                            layer1(e + 1)
                        layer3(e)

            @block.scalar
            def _(act):
                act.wait_ge(w_in, START + NW)
                with act.Fori(0, NG) as g:
                    def relu(e, mm, b, bias, to, done):
                        for f in range(KD):
                            act.wait_ge(mm, START + (g * E0 + e) * KD + f + 1)
                            nc.scalar.activation(to[:, e % 2, f, :], b[f][:, 0:GC], ACT.Relu, bias=bias[:, e, f:f + 1],
                                                 scale=1.0).then_inc(done, 1)
                    relu(0, h1_mm, bank[0:2], b1, h1, h1_done)
                    for e in range(E0):
                        relu(e, h2_mm, bank[2:4], b2, h2, h2_done)
                        if e + 1 < E0:
                            relu(e + 1, h1_mm, bank[0:2], b1, h1, h1_done)

            @block.vector
            def _(dve):
                nc.vector.memset(ones[:, :], 1.0).then_inc(ones_done, 1)
                with dve.Fori(0, NG) as g:
                    for e in range(E0):
                        for j in range(GT):
                            n = (g * E0 + e) * GT + j
                            t = g * GT + j
                            dve.wait_ge(y_mm, START + n + 1)
                            if e:
                                dve.wait_ge(y_done, START + n - GT + 1)
                            row = x_rows[:, bass.ds(t, 1), :].rearrange("p a d -> p (a d)")
                            nc.vector.scalar_tensor_tensor(
                                out=row, in0=bank[4 + j][0:RT, 0:D],
                                scalar=gates[:, bass.ds(t, 1), e:e + 1].rearrange("p a b -> p (a b)"),
                                in1=row, op0=ALU.mult, op1=ALU.add).then_inc(y_done, 1)


def galerkin_and_nodes(nc, A, sems, sb, bank, xt, wcomb, h_dram):
    (w_in, const_done, wc_done, staged, k_mm, v_mm, h_mm, k_done, sq_done, var_done, std_done, r_done, rr_done,
     v_done, h_done, h_stored, d_mm, dots_mm, bd_done, m_mm, m_done, c_mm, c_done) = sems(*("m_" + s for s in (
         "w_in const wc staged k_mm v_mm h_mm k sq var std r rr v h h_stored d_mm dots_mm bd m_mm m c_mm c").split()))
    KI = INNER // 128
    with ExitStack() as ctx:
        wkv = sb(ctx, "wkv1", [128, KD, 2 * INNER])
        mean = sb(ctx, "mean", [128, KD, 2 * HEADS1])
        wq_t = sb(ctx, "wq_t", [128, KI, D])
        wout = sb(ctx, "wout", [128, KI, D])
        wlin = sb(ctx, "wlin", [128, KD, 128])
        z = sb(ctx, "z", [RT, NT])
        z8 = sb(ctx, "z8", [RT, NT])
        zeros = sb(ctx, "zeros", [1, 512])
        stage = sb(ctx, "stage", [128, KD, GC])
        kc = sb(ctx, "kc", [RT, 2, INNER])
        sq = sb(ctx, "sq", [RT, 2, 2 * INNER])
        var = sb(ctx, "var", [RT, 2, 2 * HEADS1])
        rr = sb(ctx, "rr", [RT, 2, HEADS1])
        vs = sb(ctx, "vs", [RT, 2, INNER])
        h_rows = sb(ctx, "h_rows", [RT, GT, D])
        dots = sb(ctx, "dots", [128, KI, 128])
        m_s = sb(ctx, "m_s", [128, KI, D])
        eps_t = sb(ctx, "eps", [RT, 1])
        acc = bank[6]
        NW = 16 * 5

        def last(j, f):
            return f

        with nc.Block() as block:
            @block.sync
            def _(sp):
                sp.dma_start(wkv[:, :, :], A["wkv1"].rearrange("(k p) n -> p k n", p=128)).then_inc(w_in, 16)
                sp.dma_start(wq_t[:, :, :], A["wq1_t"].rearrange("(k p) n -> p k n", p=128)).then_inc(w_in, 16)
                sp.dma_start(wout[:, :, :], A["L1_mix_w_out"].rearrange("(k p) n -> p k n", p=128)).then_inc(w_in, 16)
                sp.dma_start(wlin[:, :, :], A["wlin"].rearrange("(k p) n -> p k n", p=128)).then_inc(w_in, 16)
                sp.dma_start(z[:, :], A["z_rows"]).then_inc(w_in, 16)
                with sp.Fori(0, NG) as g:
                    sp.wait_ge(h_done, START + g * GT + GT)
                    sp.dma_start(h_dram[bass.ds(g * GC, GC), :].rearrange("(j p) d -> p j d", p=RT),
                                 h_rows[:, :, :]).then_inc(h_stored, 16)
                sp.wait_ge(h_stored, START + NG * 16)

            @block.gpsimd
            def _(pool):
                nc.gpsimd.memset(zeros[:, :], 0.0).then_inc(const_done, 1)
                nc.gpsimd.memset(dots[:, :, :], 0.0).then_inc(const_done, 1)
                nc.gpsimd.memset(eps_t[:, :], EPS).then_inc(const_done, 1)
                nc.gpsimd.memset(xt[:, :, N:NP], 0.0).then_inc(const_done, 1)
                pool.wait_ge(const_done, START + 4)
                with pool.Fori(0, NG) as g:
                    pool.wait_ge(h_mm, START + g * GT)
                    nc.gpsimd.tensor_copy(stage[:, :, :], xt[:, :, bass.ds(g * GC, GC)]).then_inc(staged, 1)

            @block.tensor
            def _(pe):
                pe.wait_ge(w_in, START + NW)
                pe.wait_ge(const_done, START + 4)
                pe.wait_ge(wc_done, START + 3)
                nc.tensor.matmul(acc[:, :], zeros[:, 0:128], zeros[:, :], start=True, stop=False, skip_group_check=True)
                with pe.Fori(0, NG) as g:
                    pe.wait_ge(staged, START + g + 1)

                    def maps(j):
                        n = g * GT + j
                        b = 3 * (j % 2)
                        rows = slice(j * RT, (j + 1) * RT)
                        pe.wait_ge(sq_done, START + (n if j > 1 else g * GT))
                        pe.wait_ge(v_done, START + (n - 1 if j > 1 else g * GT))
                        pe.wait_ge(h_done, START + (n - 1 if j > 1 else g * GT))
                        for k in range(KD):
                            ins = nc.tensor.matmul(bank[b][0:RT, :], stage[:, k, rows], wkv[:, k, 0:INNER],
                                                   start=(k == 0), stop=(k == KD - 1))
                        ins.then_inc(k_mm, 1)
                        for k in range(KD):
                            ins = nc.tensor.matmul(bank[b + 1][0:RT, :], stage[:, k, rows], wkv[:, k, INNER:],
                                                   start=(k == 0), stop=(k == KD - 1))
                        ins.then_inc(v_mm, 1)
                        for k in range(KD):
                            ins = nc.tensor.matmul(bank[b + 2][0:RT, k * 128:(k + 1) * 128], stage[:, k, rows], wlin[:, k, :],
                                                   start=True, stop=True)
                        ins.then_inc(h_mm, 1)

                    def sums(j):
                        n = g * GT + j
                        pe.wait_ge(k_done, START + n + 1)
                        pe.wait_ge(v_done, START + n + 1)
                        for f in range(KI):
                            s = slice(f * 128, (f + 1) * 128)
                            ins = nc.tensor.matmul(acc[:, s], vs[:, j % 2, s], kc[:, j % 2, s], start=False, stop=False,
                                                   skip_group_check=True)
                        ins.then_inc(d_mm, 1)
                    maps(0)
                    for j in range(GT):
                        if j + 1 < GT:
                            maps(j + 1)
                        sums(j)
                nc.tensor.matmul(acc[:, :], zeros[:, 0:128], zeros[:, :], start=False, stop=True,
                                 skip_group_check=True).then_inc(dots_mm, 1)
                pe.wait_ge(bd_done, START + 1)
                for f in range(KI):
                    ins = nc.tensor.matmul(bank[f][:, 0:D], dots[:, f, :], wout[:, f, :], start=True, stop=True)
                ins.then_inc(m_mm, 1)
                pe.wait_ge(m_done, START + 1)
                for c in range(KD):
                    for f in range(KI):
                        ins = nc.tensor.matmul(bank[4 + c][:, 0:D], wq_t[:, f, c * 128:(c + 1) * 128], m_s[:, f, :],
                                               start=(f == 0), stop=(f == KI - 1))
                ins.then_inc(c_mm, 1)

            @block.scalar
            def _(act):
                act.wait_ge(w_in, START + NW)
                act.wait_ge(const_done, START + 4)
                nc.scalar.activation(z8[:, :], z[:, :], ACT.Copy, scale=MUL ** -0.5).then_inc(c_done, 1)
                act.wait_ge(c_done, START + 1)
                with act.Fori(0, NG) as g:
                    def squares(j):
                        n = g * GT + j
                        b = 3 * (j % 2)
                        act.wait_ge(k_mm, START + n + 1)
                        act.wait_ge(d_mm, START + (n - 1 if j > 1 else g * GT))
                        act.wait_ge(var_done, START + (n - 1 if j > 1 else g * GT))
                        nc.scalar.activation(kc[:, j % 2, :], bank[b][0:RT, :], ACT.Copy).then_inc(k_done, 1)
                        nc.scalar.activation(sq[:, j % 2, 0:INNER], bank[b][0:RT, :], ACT.Square)
                        act.wait_ge(v_mm, START + n + 1)
                        nc.scalar.activation(sq[:, j % 2, INNER:], bank[b + 1][0:RT, :], ACT.Square).then_inc(sq_done, 1)
                        act.wait_ge(h_mm, START + n + 1)
                        act.wait_ge(h_stored, START + g * 16)
                        nc.scalar.activation(h_rows[:, j, :], bank[b + 2][0:RT, 0:D], ACT.Copy,
                                             scale=z8[:, bass.ds(n, 1)]).then_inc(h_done, 1)

                    def deviation(j):
                        n = g * GT + j
                        act.wait_ge(var_done, START + n + 1)
                        nc.scalar.activation(var[:, j % 2, :], var[:, j % 2, :], ACT.Sqrt, bias=eps_t[:, :], scale=1.0 / DH1)\
                          .then_inc(std_done, 1)
                    squares(0)
                    for j in range(GT):
                        if j + 1 < GT:
                            squares(j + 1)
                        deviation(j)

            @block.vector
            def _(dve):
                dve.wait_ge(w_in, START + NW)
                heads = wkv[:, :, :].rearrange("p k (h d) -> p (k h) d", d=DH1)
                means = mean[:, :, :].rearrange("p k h -> p (k h)")
                nc.vector.tensor_reduce(means, heads, AX, ALU.add).then_inc(wc_done, 1)
                dve.wait_ge(wc_done, START + 1)
                nc.vector.tensor_scalar(means, means, 1.0 / DH1, None, ALU.mult).then_inc(wc_done, 1)
                dve.wait_ge(wc_done, START + 2)
                nc.vector.tensor_tensor(heads, heads, means.rearrange("p (h o) -> p h o", o=1)
                                        .broadcast_to((128, KD * 2 * HEADS1, DH1)), ALU.subtract).then_inc(wc_done, 1)
                with dve.Fori(0, NG) as g:
                    def variance(j):
                        n = g * GT + j
                        dve.wait_ge(sq_done, START + n + 1)
                        dve.wait_ge(rr_done, START + (n - 1 if j > 1 else g * GT))
                        nc.vector.tensor_reduce(var[:, j % 2, :], sq[:, j % 2, :].rearrange("p (h d) -> p h d", d=DH1),
                                                AX, ALU.add).then_inc(var_done, 1)

                    def scaled(j):
                        n = g * GT + j
                        b = 3 * (j % 2)
                        dve.wait_ge(std_done, START + n + 1)
                        nc.vector.reciprocal(var[:, j % 2, :], var[:, j % 2, :]).then_inc(r_done, 1)
                        dve.wait_ge(r_done, START + n + 1)
                        dve.wait_ge(d_mm, START + (n - 1 if j > 1 else g * GT))
                        nc.vector.tensor_tensor(rr[:, j % 2, :], var[:, j % 2, 0:HEADS1], var[:, j % 2, HEADS1:],
                                                ALU.mult).then_inc(rr_done, 1)
                        dve.wait_ge(rr_done, START + n + 1)
                        nc.vector.tensor_tensor(
                            vs[:, j % 2, :].rearrange("p (h d) -> p h d", d=DH1),
                            bank[b + 1][0:RT, :].rearrange("p (h d) -> p h d", d=DH1),
                            rr[:, j % 2, :].rearrange("p (h o) -> p h o", o=1).broadcast_to((RT, HEADS1, DH1)),
                            ALU.mult).then_inc(v_done, 1)
                    variance(0)
                    for j in range(GT):
                        if j + 1 < GT:
                            variance(j + 1)
                        scaled(j)
                dve.wait_ge(dots_mm, START + 1)
                dve.wait_ge(const_done, START + 4)
                for f in range(KI):
                    for h in range(128 // DH1):
                        s = slice(h * DH1, (h + 1) * DH1)
                        ins = nc.vector.tensor_scalar(dots[s, f, s], acc[s, f * 128 + h * DH1:f * 128 + (h + 1) * DH1],
                                                      1.0 / N, None, ALU.mult)
                ins.then_inc(bd_done, 1)
                dve.wait_ge(m_mm, START + 1)
                for f in range(KI):
                    ins = nc.vector.tensor_copy(m_s[:, f, :], bank[f][:, 0:D])
                ins.then_inc(m_done, 1)
                dve.wait_ge(c_mm, START + 1)
                for c in range(KD):
                    nc.vector.tensor_copy(wcomb[:, c, :], bank[4 + c][:, 0:D])


def edge_convolution(nc, A, sems, sb, bank, tables, xt, wcomb, x_rows, h_dram):
    src_t, rel0, base_row, rounds_t, iota_w = tables
    (w_in, scaled, acc_zero, tab, hid_mm, hid_done, w_mm, sum_mm, added, staged, u_mm, mix_mm, t_done, b_done,
     x_done, passed, *more) = sems(*("c_" + s for s in (
         "w_in scaled acc_zero tab hid_mm hid w_mm sum_mm added staged u_mm mix_mm t b x passed "
         "ea_a ea_b idx_a idx_b eq_a eq_b hot_a hot_b prod_a prod_b").split()),
                                  *(f"c_gathered{j}" for j in range(ITC)))
    ea_in, idx_ready, eq_done, hot_done, p_done = (more[2 * k:2 * k + 2] for k in range(5))
    gathered = more[10:]
    c_s, c_x = float(np.float32(np.sin(np.pi / 8.0))), float(np.float32(np.cos(np.pi / 8.0)))
    SC = c_s * MUL ** -0.5
    LIN = c_x * 64 ** -0.5 * 16.0 ** -0.5 * (2 * MUL) ** -0.5
    NB = 5
    HE = HALF * EC
    with ExitStack() as ctx:
        acc = sb(ctx, "acc", [128, NB, NP])
        rel = sb(ctx, "rel", [EC, NCH])
        base = sb(ctx, "base", [1, NCH], I32)
        idx = sb(ctx, "idx", [EC, 2, HALF], I32)
        rows = [sb(ctx, f"rows{j}", [EC, D]) for j in range(ITC)]
        ea4 = sb(ctx, "ea4", [EC, NCH, 4])
        ea8 = sb(ctx, "ea8", [8, 2, HE])
        fw0 = sb(ctx, "fw0", [8, 64])
        fw1 = sb(ctx, "fw1", [64, 4 * MUL])
        hid = sb(ctx, "hid", [64, 2, HE])
        eq = sb(ctx, "eq", [EC, 2, HALF, W])
        hot = sb(ctx, "hot", [EC, 2, HALF, 4, W])
        prod = sb(ctx, "prod", [EC, HALF, NB * 128])
        wsc = sb(ctx, "wsc", [128, KD, D])
        wl2 = sb(ctx, "wl2", [128, 3, 128])
        z = sb(ctx, "z", [RT, NT])
        bout = sb(ctx, "bout", [RT, D])
        stage = sb(ctx, "stage", [128, NB, GC])
        stage_x = sb(ctx, "stage_x", [128, KD, GC])
        t_rows = sb(ctx, "t_rows", [RT, GT, D])
        p_hid, p_w, p_sum = bank[0:2], bank[2:4], bank[4:6]
        NW = 16 * 7

        def begin(eng, tag):
            rounds = eng.value_load(rounds_t[0:1, 0:1], min_val=1, max_val=NP // W)
            reg = eng.alloc_register(f"c_its_{tag}")
            eng.reg_mov(reg, 0)
            return rounds, reg

        def count(eng, reg):
            return eng.snap(reg, min_val=0, max_val=NIT * (NP // W))

        with nc.Block() as block:
            @block.sync
            def _(sp):
                for t, name in ((fw0, "L1_gnn_fc_w0"), (fw1, "fw1"), (ea4, "ea4"), (z, "z_rows")):
                    sp.dma_start(t[:], A[name]).then_inc(w_in, 16)
                sp.dma_start(wsc[:, :, :], A["wsc"].rearrange("(k p) n -> p k n", p=128)).then_inc(w_in, 16)
                sp.dma_start(wl2[:, :, :], A["wl2"].rearrange("(k p) n -> p k n", p=128)).then_inc(w_in, 16)
                sp.dma_start(bout[:, :], A["L1_mix_b_out"].rearrange("(o n) -> o n", o=1).broadcast_to((RT, D))).then_inc(w_in, 16)
                rounds, reg = begin(sp, "sp")
                with sp.Fori(0, rounds) as r:
                    with sp.Fori(0, NIT) as i:
                        its = count(sp, reg)
                        for b in range(2):
                            sp.wait_ge(hid_mm, START + (its + i) * 2)
                            sp.dma_start(ea8[:, b, :], A["ea8"][:, bass.ds((i * 2 + b) * HE, HE)]).then_inc(ea_in[b], 16)
                    sp.reg_add(reg, reg, NIT)

            @block.gpsimd
            def _(pool):
                rounds, reg = begin(pool, "pool")
                nc.gpsimd.memset(acc[:, :, :], 0.0).then_inc(acc_zero, 1)
                with pool.Fori(0, rounds) as r:
                    with pool.Fori(0, NIT) as i:
                        its = count(pool, reg)
                        for b in range(2):
                            wait_alone(pool, p_done[b], (its + i) * HALF, passed)
                            nc.gpsimd.tensor_copy(idx[:, b, :], src_t[:, bass.ds(i * ITC + b * HALF, HALF)])\
                              .then_inc(idx_ready[b], 1)
                            wait_alone(pool, idx_ready[b], its + i + 1, passed)
                            for j in range(HALF):
                                nc.gpsimd.indirect_dma_start(
                                    out=rows[b * HALF + j][:, :], out_offset=None, in_=h_dram,
                                    in_offset=bass.IndirectOffsetOnAxis(ap=idx[:, b, j:j + 1], axis=0),
                                ).then_inc(gathered[b * HALF + j], 16)
                    pool.reg_add(reg, reg, NIT)
                with pool.Fori(0, NG) as g:
                    cols = bass.ds(g * GC, GC)
                    pool.wait_ge(added, START + count(pool, reg) * ITC)
                    pool.wait_ge(mix_mm, START + g * GT)
                    nc.gpsimd.tensor_copy(stage[:, :, :], acc[:, :, cols]).then_inc(staged, 1)
                    nc.gpsimd.tensor_copy(stage_x[:, :, :], xt[:, :, cols]).then_inc(staged, 1)

            @block.tensor
            def _(pe):
                rounds, reg = begin(pe, "pe")
                pe.wait_ge(w_in, START + NW)
                with pe.Fori(0, rounds) as r:
                    with pe.Fori(0, NIT) as i:
                        its = count(pe, reg)
                        n = its + i

                        def hidden(b):
                            pe.wait_ge(ea_in[b], START + n * 16 + 16)
                            pe.wait_ge(hid_done, START + (n * 2 + b if b else n * 2))
                            nc.tensor.matmul(p_hid[b][0:64, 0:HE], fw0[:, :], ea8[:, b, :], start=True, stop=True)\
                              .then_inc(hid_mm, 1)

                        def weights(c):
                            b, j = divmod(c, HALF)
                            pe.wait_ge(hid_done, START + n * 2 + b + 1)
                            for q in range(2):
                                pe.wait_ge(p_done[q], START + n * HALF + min(max(c - 1 - q * HALF, 0), HALF))
                            nc.tensor.matmul(p_w[c % 2][0:EC, 0:4 * MUL], hid[:, b, j * EC:(j + 1) * EC], fw1[:, :],
                                             start=True, stop=True).then_inc(w_mm, 1)

                        def sums(c):
                            b, j = divmod(c, HALF)
                            pe.wait_ge(hot_done[b], START + n + 1)
                            pe.wait_ge(p_done[b], START + n * HALF + j + 1)
                            pe.wait_ge(added, START + n * ITC + max(c - 1, 0))
                            for m in range(NB):
                                ins = nc.tensor.matmul(p_sum[c % 2][:, m * W:(m + 1) * W], prod[:, j, m * 128:(m + 1) * 128],
                                                       hot[:, b, j, max(m - 1, 0), :], start=True, stop=True)
                            ins.then_inc(sum_mm, 1)
                        hidden(0)
                        hidden(1)
                        weights(0)
                        for c in range(ITC):
                            if c + 1 < ITC:
                                weights(c + 1)
                            sums(c)
                    pe.reg_add(reg, reg, NIT)
                pe.wait_ge(scaled, START + 3)
                with pe.Fori(0, NG) as g:
                    pe.wait_ge(staged, START + g * 2 + 2)
                    for j in range(GT):
                        n = g * GT + j
                        rows_j = slice(j * RT, (j + 1) * RT)
                        u, m = bank[2 * (j % 2)], bank[2 * (j % 2) + 1]
                        pe.wait_ge(x_done, START + (n - 1 if j > 1 else g * GT))
                        for k in range(KD):
                            nc.tensor.matmul(u[0:RT, 0:D], stage_x[:, k, rows_j], wsc[:, k, :], start=(k == 0), stop=False,
                                             skip_group_check=True)
                        for q in range(NB):
                            if q < 2:
                                to, w = u[0:RT, q * 128:(q + 1) * 128], wl2[:, q, :]
                            else:
                                step = MUL * (q - 1)
                                to = u[0:RT, 0:2 * step].rearrange("p (a b) -> p a b", a=2)[:, :, 0:MUL]
                                w = wl2[:, 2, :].rearrange("p (a b) -> p a b", a=2)
                            ins = nc.tensor.matmul(to, stage[:, q, rows_j], w, start=False, stop=(q == NB - 1),
                                                   skip_group_check=True)
                        ins.then_inc(u_mm, 1)
                        for k in range(KD):
                            ins = nc.tensor.matmul(m[0:RT, 0:D], stage_x[:, k, rows_j], wcomb[:, k, :],
                                                   start=(k == 0), stop=(k == KD - 1))
                        ins.then_inc(mix_mm, 1)

            @block.scalar
            def _(act):
                rounds, reg = begin(act, "act")
                act.wait_ge(w_in, START + NW)
                nc.scalar.activation(wsc[:, :, :], wsc[:, :, :], ACT.Copy, scale=SC).then_inc(scaled, 1)
                nc.scalar.activation(wl2[:, 0:2, :], wl2[:, 0:2, :], ACT.Copy, scale=LIN).then_inc(scaled, 1)
                nc.scalar.activation(wl2[0:MUL, 2, :], wl2[0:MUL, 2, :], ACT.Copy, scale=LIN)
                nc.scalar.activation(wl2[MUL:, 2, :], wl2[MUL:, 2, :], ACT.Copy, scale=LIN * 3.0 ** -0.5).then_inc(scaled, 1)
                with act.Fori(0, rounds) as r:
                    with act.Fori(0, NIT) as i:
                        its = count(act, reg)
                        n = its + i
                        for b in range(2):
                            act.wait_ge(hid_mm, START + n * 2 + b + 1)
                            act.wait_ge(w_mm, START + n * ITC)
                            nc.scalar.activation(hid[:, b, :], p_hid[b][0:64, 0:HE], ACT.Silu, scale=8.0 ** -0.5)\
                              .then_inc(hid_done, 1)
                        for b in range(2):
                            act.wait_ge(eq_done[b], START + n + 1)
                            act.wait_ge(sum_mm, START + n * ITC)
                            for j in range(HALF):
                                for m in range(4):
                                    ins = nc.scalar.activation(
                                        hot[:, b, j, m, :], eq[:, b, j, :], ACT.Copy,
                                        scale=ea4[:, bass.ds(i * ITC + b * HALF + j, 1), m:m + 1].rearrange("p a b -> p (a b)"))
                            ins.then_inc(hot_done[b], 1)
                    act.reg_add(reg, reg, NIT)

            @block.vector
            def _(dve):
                rounds, reg = begin(dve, "dve")
                tabs = dve.alloc_register("c_tabs")
                dve.reg_mov(tabs, 2)
                dve.wait_ge(w_in, START + NW)
                nc.vector.tensor_copy(rel[:, :], rel0[:, :]).then_inc(tab, 1)
                nc.vector.tensor_copy(base[:, :], base_row[:, :]).then_inc(tab, 1)
                dve.wait_ge(acc_zero, START + 1)
                with dve.Fori(0, rounds) as r:
                    wait_alone(dve, tab, dve.snap(tabs, min_val=0, max_val=1 << 20), passed)
                    with dve.Fori(0, NIT) as i:
                        its = count(dve, reg)
                        n = its + i
                        for b in range(2):
                            dve.wait_ge(hot_done[b], START + n)
                            nc.vector.tensor_tensor(
                                eq[:, b, :, :],
                                iota_w[:, :].rearrange("p (o w) -> p o w", o=1).broadcast_to((EC, HALF, W)),
                                rel[:, bass.ds(i * ITC + b * HALF, HALF)].rearrange("p (c o) -> p c o", o=1)
                                .broadcast_to((EC, HALF, W)), ALU.is_equal).then_inc(eq_done[b], 1)
                        at = [dve.value_load(base[0:1, bass.ds(i * ITC + c, 1)], min_val=0, max_val=TOPBASE)
                              for c in range(ITC)]

                        def products(c):
                            b, j = divmod(c, HALF)
                            dve.wait_ge(gathered[c], n * 16 + 16)
                            dve.wait_ge(w_mm, START + n * ITC + c + 1)
                            dve.wait_ge(sum_mm, START + n * ITC + max(c - 3, 0))
                            w = [p_w[c % 2][0:EC, m * MUL:(m + 1) * MUL].rearrange("p (o u) -> p o u", o=1) for m in range(4)]
                            xs0 = rows[c][:, 0:MUL].rearrange("p (o u) -> p o u", o=1)
                            xs1 = rows[c][:, MUL:D].rearrange("p (c u) -> p c u", c=3)
                            three = (EC, 3, MUL)
                            bd = prod[:, j, 2 * 128:].rearrange("p (c h u) -> p c h u", c=3, h=2)
                            mul = nc.vector.tensor_tensor
                            mul(prod[:, j, 0:MUL], rows[c][:, 0:MUL], p_w[c % 2][0:EC, 0:MUL], ALU.mult)
                            mul(prod[:, j, MUL:D].rearrange("p (c u) -> p c u", c=3), xs1, w[2].broadcast_to(three), ALU.mult)
                            mul(bd[:, :, 0, :], xs0.broadcast_to(three), w[1].broadcast_to(three), ALU.mult)
                            mul(bd[:, :, 1, :], xs1, w[3].broadcast_to(three), ALU.mult).then_inc(p_done[b], 1)

                        def add(c):
                            dve.wait_ge(sum_mm, START + n * ITC + c + 1)
                            dve.wait_ge(added, START + n * ITC + c)
                            win = acc[:, :, bass.ds(at[c], W)]
                            nc.vector.tensor_tensor(win, win, p_sum[c % 2][:, 0:NB * W].rearrange("p (k w) -> p k w", k=NB),
                                                    ALU.add).then_inc(added, 1)
                        products(0)
                        for c in range(ITC):
                            if c + 1 < ITC:
                                products(c + 1)
                            add(c)
                    dve.reg_add(reg, reg, NIT)
                    nc.vector.tensor_scalar(rel[:, :], rel[:, :], float(W), None, ALU.subtract).then_inc(tab, 1)
                    nc.vector.tensor_scalar(base[:, :], base[:, :], float(W), float(TOPBASE), ALU.add, ALU.min).then_inc(tab, 1)
                    dve.reg_add(tabs, tabs, 2)
                with dve.Fori(0, NG) as g:
                    for j in range(GT):
                        n = g * GT + j
                        u, m = bank[2 * (j % 2)], bank[2 * (j % 2) + 1]
                        row = x_rows[:, bass.ds(n, 1), :].rearrange("p a d -> p (a d)")
                        zt = z[:, bass.ds(n, 1)]
                        dve.wait_ge(mix_mm, START + n + 1)
                        nc.vector.tensor_tensor(t_rows[:, j, :], m[0:RT, 0:D], bout[:, :], ALU.add).then_inc(t_done, 1)
                        dve.wait_ge(t_done, START + n + 1)
                        nc.vector.tensor_tensor(t_rows[:, j, :], t_rows[:, j, :], row, ALU.add).then_inc(b_done, 1)
                        dve.wait_ge(b_done, START + n + 1)
                        dve.wait_ge(u_mm, START + n + 1)
                        nc.vector.scalar_tensor_tensor(out=row[:, 0:MUL], in0=u[0:RT, 0:MUL], scalar=zt, in1=t_rows[:, j, 0:MUL],
                                                       op0=ALU.mult, op1=ALU.add)
                        nc.vector.scalar_tensor_tensor(out=row[:, MUL:D].rearrange("p (u c) -> p u c", c=3),
                                                       in0=u[0:RT, MUL:D].rearrange("p (c u) -> p u c", c=3), scalar=zt,
                                                       in1=t_rows[:, j, MUL:D].rearrange("p (u c) -> p u c", c=3),
                                                       op0=ALU.mult, op1=ALU.add).then_inc(x_done, 1)


def expert_swiglu(nc, A, sems, sb, bank, xt, x_rows):
    h1_mm, h3_mm, s_done, g_done, y_part, y_mm, y_done, passed, *w_in = sems(*("e1_" + s for s in (
        "h1_mm h3_mm s g y_part y_mm y passed w_a w_b").split()))
    NH = len(HCH)
    with ExitStack() as ctx:
        gates = sb(ctx, "gates", [RT, NT, 8])
        route(nc, "r1", A, sems, sb, bank, xt, gates, False, E1, ("rw1",), ())
        w13 = [sb(ctx, f"w13_{b}", [128, 2, KD, HID1]) for b in range(2)]
        w2 = [sb(ctx, f"w2_{b}", [128, NH, D]) for b in range(2)]
        s_t = sb(ctx, "s_t", [128, 2, GC])
        h_t = sb(ctx, "h_t", [128, 2, GC])
        FULL = HID1 // 128
        REST = HID1 - FULL * 128
        with nc.Block() as block:
            @block.sync
            def _(sp):
                with sp.Fori(0, E1 // 2) as p:
                    for b in range(2):
                        e = p * 2 + b
                        sp.wait_ge(y_mm, START + (e * NG * GT if b == 0 else p * (2 * NG * GT)))
                        if b == 1:
                            pass
                        for m, name in enumerate(("w1_1", "w3_1")):
                            sp.dma_start(w13[b][:, m, :, :], A[name][bass.ds(e, 1), :, :].rearrange("o (k p) n -> p (o k) n", p=128))\
                              .then_inc(w_in[b], 16)
                        sp.dma_start(w2[b][:, 0:FULL, :], A["w2_1"][bass.ds(e, 1), 0:FULL * 128, :]
                                     .rearrange("o (k p) n -> p (o k) n", p=128)).then_inc(w_in[b], 16)
                        sp.dma_start(w2[b][0:REST, FULL, :], A["w2_1"][bass.ds(e, 1), FULL * 128:HID1, :]
                                     .rearrange("o p n -> p (o n)")).then_inc(w_in[b], 16)

            @block.tensor
            def _(pe):
                with pe.Fori(0, E1 // 2) as p:
                    for b in range(2):
                        wait_alone(pe, w_in[b], p * 64 + 64, passed)
                        with pe.Fori(0, NG) as g:
                            q = (p * 2 + b) * NG + g
                            cols = bass.ds(g * GC, GC)

                            def up(h):
                                o, sz = HCH[h]
                                wait_alone(pe, g_done, q * NH + max(h - 1, 0), passed)
                                for m, done in ((0, h1_mm), (1, h3_mm)):
                                    for k in range(KD):
                                        ins = nc.tensor.matmul(bank[2 * (h % 2) + m][0:sz, 0:GC], w13[b][:, m, k, o:o + sz],
                                                               xt[:, k, cols], start=(k == 0), stop=(k == KD - 1))
                                    ins.then_inc(done, 1)

                            def down(h):
                                sz = HCH[h][1]
                                pe.wait_ge(g_done, START + q * NH + h + 1)
                                if h == 0:
                                    pe.wait_ge(y_done, START + q * GT)
                                for j in range(GT):
                                    ins = nc.tensor.matmul(bank[4 + j][0:RT, 0:D], h_t[0:sz, h % 2, j * RT:(j + 1) * RT],
                                                           w2[b][0:sz, h, :], start=(h == 0), stop=(h == NH - 1))
                                    if h == NH - 1:
                                        ins.then_inc(y_mm, 1)
                                if h < NH - 1:
                                    ins.then_inc(y_part, 1)
                            up(0)
                            for h in range(NH):
                                if h + 1 < NH:
                                    up(h + 1)
                                down(h)

            @block.scalar
            def _(act):
                with act.Fori(0, E1 * NG) as q:
                    for h, (o, sz) in enumerate(HCH):
                        act.wait_ge(h1_mm, START + q * NH + h + 1)
                        act.wait_ge(g_done, START + q * NH + max(h - 1, 0))
                        nc.scalar.activation(s_t[0:sz, h % 2, :], bank[2 * (h % 2)][0:sz, 0:GC], ACT.Silu).then_inc(s_done, 1)

            @block.vector
            def _(dve):
                with dve.Fori(0, E1) as e:
                    with dve.Fori(0, NG) as g:
                        q = e * NG + g
                        for h, (o, sz) in enumerate(HCH):
                            dve.wait_ge(s_done, START + q * NH + h + 1)
                            dve.wait_ge(h3_mm, START + q * NH + h + 1)
                            dve.wait_ge(y_part, START + q * (NH - 1) + max(h - 1, 0))
                            if h < 2:
                                dve.wait_ge(y_mm, START + q * GT)
                            nc.vector.tensor_tensor(h_t[0:sz, h % 2, :], s_t[0:sz, h % 2, :], bank[2 * (h % 2) + 1][0:sz, 0:GC],
                                                    ALU.mult).then_inc(g_done, 1)
                        for j in range(GT):
                            t = g * GT + j
                            dve.wait_ge(y_mm, START + q * GT + j + 1)
                            row = x_rows[:, bass.ds(t, 1), :].rearrange("p a d -> p (a d)")
                            nc.vector.scalar_tensor_tensor(
                                out=row, in0=bank[4 + j][0:RT, 0:D],
                                scalar=gates[:, bass.ds(t, 1), bass.ds(e, 1)].rearrange("p a b -> p (a b)"),
                                in1=row, op0=ALU.mult, op1=ALU.add).then_inc(y_done, 1)



def layouts(i):
    c = np.ascontiguousarray
    src, dst = np.asarray(i["src"]), np.asarray(i["dst"])
    x = np.zeros((NP, D), np.float32)
    x[:N] = i["x"]
    z = np.zeros((NP,), np.float32)
    z[:N] = np.asarray(i["node_vec1"])[:, 0]
    pad8 = np.zeros((128, 8), np.float32)
    pad8[:, :E0] = i["L0_ffn_router_w2"]
    vec = np.concatenate([np.arange(MUL)] + [MUL + 3 * np.arange(MUL) + k for k in range(3)])
    qkv = np.asarray(i["L1_mix_w_qkv"])[vec]
    none = np.zeros((128, 128), np.float32)
    l0, l1 = np.asarray(i["L1_gnn_W_lin2_0"]), np.asarray(i["L1_gnn_W_lin2_1"])

    def diag(p, q):
        m = np.zeros((2 * MUL, 2 * MUL), np.float32)
        m[:MUL, :MUL], m[MUL:, MUL:] = p, q
        return m

    a = {
        "x_rows": c(x.reshape(NT, RT, D).transpose(1, 0, 2)),
        "src_t": c(src.reshape(NCH, EC).T),
        "dst_t": c(dst.reshape(NCH, EC).T),
        "dst_c": c(dst.reshape(NCH // HALF, HALF, EC)),
        "wkv0": c(np.concatenate([i["L0_mix_wk"], i["L0_mix_wv"]], axis=1)),
        "wq0": i["L0_mix_wq"], "wo0": i["L0_mix_wo"],
        "w1_0": c(np.asarray(i["L0_gnn_W1"]).T), "w2_0": c(np.asarray(i["L0_gnn_W2"]).T),
        "wih_0": c(np.asarray(i["L0_gnn_W_ih"]).T), "whh_0": c(np.asarray(i["L0_gnn_W_hh"]).T),
        "rw2_0": pad8,
        "z_rows": c(z.reshape(NT, RT).T),
        "ea4": c(np.asarray(i["edge_attr_4"]).reshape(NCH, EC, 4).transpose(1, 0, 2)),
        "ea8": c(np.asarray(i["edge_attr_8"]).T),
        "wlin": np.concatenate([diag(i["L1_gnn_W_lin1_0"], i["L1_gnn_W_lin1_1"]),
                                diag(i["L1_gnn_W_lin1_1"], i["L1_gnn_W_lin1_1"])]),
        "wsc": np.concatenate([np.concatenate([diag(i["L1_gnn_W_sc0"], i["L1_gnn_W_sc1"]), none], axis=1),
                               np.concatenate([none, diag(i["L1_gnn_W_sc1"], i["L1_gnn_W_sc1"])], axis=1)]),
        "wl2": np.concatenate([diag(l0[:MUL], l1[MUL:]), diag(l1[MUL:], l1[MUL:]),
                               diag(l1[:MUL], l0[MUL:])[:, np.r_[MUL:2 * MUL, 0:MUL]]]),
        "fw1": np.asarray(i["L1_gnn_fc_w1"]),
        "wkv1": c(qkv[:, INNER:]), "wq1_t": c(qkv[:, :INNER].T),
        "rw1": c(np.asarray(i["L1_ffn_router_w"]).T),
        "w1_1": c(np.asarray(i["L1_ffn_w1"]).transpose(0, 2, 1)),
        "w3_1": c(np.asarray(i["L1_ffn_w3"]).transpose(0, 2, 1)),
        "w2_1": c(np.asarray(i["L1_ffn_w2"]).transpose(0, 2, 1)),
    }
    for name in ("L0_mix_bq", "L0_mix_bo", "L0_gnn_b1", "L0_gnn_b_ih", "L0_gnn_b_hh"):
        a[name + "_t"] = np.asarray(i[name]).reshape(-1, 128).T
    for name in ("L0_ffn_expert_b1", "L0_ffn_expert_b2"):
        a[name + "_t"] = np.asarray(i[name]).reshape(E0, KD, 128).transpose(2, 0, 1)
    for name in ("L0_mix_bk", "L0_mix_bv", "L0_gnn_b2",
                 "L0_ffn_router_w1", "L0_ffn_router_b1", "L0_ffn_router_b2", "L0_ffn_expert_w1", "L0_ffn_expert_w2",
                 "L0_ffn_expert_w3", "L0_ffn_expert_b3",
                 "L1_gnn_fc_w0", "L1_mix_w_out", "L1_mix_b_out"):
        a[name] = i[name]
    return {k: np.ascontiguousarray(v) for k, v in a.items()}


def kernel(**inputs):
    import concourse.bacc as _bacc
    from concourse.bass_utils import run_bass_kernel_spmd as _run

    nc = _bacc.Bacc("TRN2", target_bir_lowering=False, num_devices=1)
    arrays = {f"in_{k}": v for k, v in layouts(inputs).items()}
    args = {k[3:]: nc.dram_tensor(k, v.shape, mybir.dt.from_np(v.dtype), kind="ExternalInput").ap()
            for k, v in arrays.items()}
    out = nc.dram_tensor("out_0", (N, D), F32, kind="ExternalOutput").ap()
    build(nc, args, out)
    r = _run(nc, [arrays], core_ids=[0])
    return r.results[0]["out_0"]
```

```python
from contextlib import ExitStack

import numpy as np

import concourse.bass as bass
from concourse import mybir

F32 = mybir.dt.float32
BF16 = mybir.dt.bfloat16
I16 = mybir.dt.int16
I32 = mybir.dt.int32
U32 = mybir.dt.uint32
ALU = mybir.AluOpType
ACT = mybir.ActivationFunctionType
AX = mybir.AxisListType.X

N, D = 3125, 256
RT, NT = 100, 32
GT, NG = 4, 8
GC = RT * GT
NP = RT * NT
LASTROWS = N - RT * (NT - 1)
KD = D // 128
EC, NCH = 125, 400
UC = 4
NU = NCH // UC
ITC = 2 * UC
NIT = NU // 2
UE = UC * EC
W = 80
MAXROUNDS = -(-N // W)
NW_COLS = NP + W
PC = 2
NPAIR = NCH // PC
KT = NP // 128
AB = 7
AC = -(-N // AB)
TB = (9, 8, 8)
HB = 5
HN = NP // (KT // HB)
PARTS = 3
EXACT = 256
STEPS = 6
EPS = 1e-5
HEADS0, DH0 = 8, 32
HEADS1, DH1 = 8, 64
INNER = HEADS1 * DH1
E0, E1, HID1 = 6, 8, 682
HCH = [(k * 128, min(128, HID1 - k * 128)) for k in range((HID1 + 127) // 128)]
MUL = 64
NEG = -1e30
START = 16


def wait_alone(eng, sem, value, passed):
    eng.wait_ge(sem, START + value)
    eng.sem_inc(passed, 1)


def build(nc, A, out, debug=None):
    top = ExitStack()
    names = [0]

    held = []

    def sems(*wanted):
        got = [nc.alloc_semaphore(name=n) for n in wanted]
        engines = (nc.gpsimd, nc.sync, nc.scalar, nc.vector, nc.tensor)
        for n, (sem, name) in enumerate(zip(got, wanted)):
            if "gathered" not in name:
                engines[n % len(engines)].sem_inc(sem, START)
        nc.all_engine_barrier()
        held.extend(got)
        return got

    def phase(f, *args):
        f(nc, *args)
        if held:
            nc.clear_and_free_semaphores(held)
            held.clear()
            nc.all_engine_barrier()

    def sb(ctx, name, shape, dt=F32):
        names[0] += 1
        return ctx.enter_context(nc.sbuf_tensor(f"{name}_{names[0]}", shape, dt))

    with top:
        x_rows = sb(top, "x_rows", [RT, NT, D])
        ident = sb(top, "ident", [128, 128])
        iota_w = sb(top, "iota_w", [EC, W])
        src_t = sb(top, "src_t", [EC, NCH], I32)
        rel0 = sb(top, "rel0", [EC, NCH])
        base_row = sb(top, "base_row", [1, NU], I32)
        rounds_t = sb(top, "rounds_t", [1, 1], I32)
        eps_t = sb(top, "eps_t", [128, 1])
        crowded_t = sb(top, "crowded_t", [1, 1], I32)
        bank = [top.enter_context(nc.psum_tensor(f"bank{k}", [128, 512], F32)) for k in range(8)]
        h_dram = nc.dram_tensor("h_dram", (NP, D), F32).ap()
        base_dram = nc.dram_tensor("base_dram", (NU,), F32).ap()
        span_dram = nc.dram_tensor("span_dram", (NU,), F32).ap()

        a_dram = nc.dram_tensor("a_dram", (NG, 128, KT, GC), BF16).ap()
        pair_dram = [nc.dram_tensor(f"pair_{e}_dram", (NPAIR,), F32).ap() for e in ("lo", "hi")]
        range_dram = nc.dram_tensor("range_dram", (NT, 2), I32).ap()

        phase(setup, A, sems, sb, x_rows, ident, iota_w, src_t, rel0, base_row, rounds_t, eps_t,
              base_dram, span_dram)
        tables = (src_t, rel0, base_row, rounds_t, iota_w)

        with ExitStack() as ctx:
            nf = sb(ctx, "nf", [128, KD, NP])
            phase(norm_transpose, "n0", sems, sb, x_rows, ident, eps_t, bank, nf, False)
            with ExitStack() as ctx_mix:
                mix = sb(ctx_mix, "mix", [128, KD, NP])
                phase(linear_attention, A, sems, sb, bank, nf, mix)
                phase(add_transposed, "mix", sems, bank, sb, ident, x_rows, mix)
            phase(adjacency, A, sems, sb, bank, ident, src_t, a_dram, pair_dram, range_dram, crowded_t)
            phase(gated_graph, A, sems, sb, bank, nf, a_dram, crowded_t)
            phase(gated_graph_by_edges, A, sems, sb, bank, tables, nf, h_dram, crowded_t)
            phase(add_transposed, "gnn", sems, bank, sb, ident, x_rows, nf)
        if debug == "l0a":
            return store_rows(nc, sems, x_rows, out)
        with ExitStack() as ctx:
            xt = sb(ctx, "xt", [128, KD, NP])
            phase(norm_transpose, "n1", sems, sb, x_rows, ident, eps_t, bank, xt, False)
            phase(expert_mlp, A, sems, sb, bank, xt, x_rows)
        if debug == "l0":
            return store_rows(nc, sems, x_rows, out)

        with ExitStack() as ctx:
            xt = sb(ctx, "xt", [128, KD, NP])
            wcomb = sb(ctx, "wcomb", [128, KD, D])
            phase(norm_transpose, "n2", sems, sb, x_rows, ident, eps_t, bank, xt, True)
            phase(galerkin_and_nodes, A, sems, sb, bank, xt, wcomb, h_dram)
            phase(edge_convolution, A, sems, sb, bank, tables, ident, xt, wcomb, x_rows, h_dram)
        if debug == "l1a":
            return store_rows(nc, sems, x_rows, out)
        with ExitStack() as ctx:
            xt = sb(ctx, "xt", [128, KD, NP])
            phase(norm_transpose, "n3", sems, sb, x_rows, ident, eps_t, bank, xt, False)
            phase(expert_swiglu, A, sems, sb, bank, xt, x_rows)
        store_rows(nc, sems, x_rows, out)


def store_rows(nc, sems, x_rows, out):
    stored, = sems("out_stored")
    with nc.Block() as block:
        @block.sync
        def _(sp):
            sp.dma_start(out[0:RT * (NT - 1), :].rearrange("(t p) d -> p t d", p=RT),
                         x_rows[:, 0:NT - 1, :]).then_inc(stored, 16)
            sp.dma_start(out[RT * (NT - 1):N, :], x_rows[0:LASTROWS, NT - 1, :]).then_inc(stored, 16)
            sp.wait_ge(stored, START + 32)


def setup(nc, A, sems, sb, x_rows, ident, iota_w, src_t, rel0, base_row, rounds_t, eps_t,
          base_dram, span_dram):
    (x_in, edges_in, ident_zero, ident_done, iota_done, conv, mm_done, mm_stored, bc_loaded,
     tab) = sems("x_in", "edges_in", "ident_zero", "ident_done", "iota_done", "conv", "mm_done",
                 "mm_stored", "bc_loaded", "tab")
    with ExitStack() as ctx:
        dst_t = sb(ctx, "dst_t", [EC, NCH], I32)
        dst_f = sb(ctx, "dst_f", [EC, NCH])
        dst_c = sb(ctx, "dst_c", [NU, UE], I32)
        dst_cf = sb(ctx, "dst_cf", [NU, UE])
        lo = sb(ctx, "lo", [NU, 1])
        hi = sb(ctx, "hi", [NU, 1])
        span = sb(ctx, "span", [NU, 1])
        base_bc = sb(ctx, "base_bc", [EC, NU])
        span_row = sb(ctx, "span_row", [1, NU])
        widest = sb(ctx, "widest", [1, 1])
        starts_i = sb(ctx, "starts_i", [1, MAXROUNDS], I32)
        starts = sb(ctx, "starts", [1, MAXROUNDS])
        needed = sb(ctx, "needed", [1, MAXROUNDS])
        iota_i = sb(ctx, "iota_i", [EC, W], I32)
        with nc.Block() as block:
            @block.sync
            def _(sp):
                sp.dma_start(dst_t[:, :], A["dst_t"]).then_inc(edges_in, 16)
                sp.dma_start(dst_c[:, :], A["dst_c"]).then_inc(edges_in, 16)
                sp.dma_start(src_t[:, :], A["src_t"]).then_inc(edges_in, 16)
                sp.dma_start(x_rows[:, :, :], A["x_rows"]).then_inc(x_in, 16)
                sp.wait_ge(mm_done, START + 1)
                sp.dma_start(base_dram.rearrange("(p j) -> p j", j=1), lo[:, :]).then_inc(mm_stored, 16)
                sp.dma_start(span_dram.rearrange("(p j) -> p j", j=1), span[:, :]).then_inc(mm_stored, 16)
                sp.wait_ge(mm_stored, START + 32)
                sp.dma_start(base_bc[:, :], base_dram.rearrange("(o c) -> o c", o=1).broadcast_to((EC, NU)))\
                  .then_inc(bc_loaded, 16)
                sp.dma_start(span_row[:, :], span_dram.rearrange("(o c) -> o c", o=1)).then_inc(bc_loaded, 16)
                sp.wait_ge(x_in, START + 16)

            @block.gpsimd
            def _(pool):
                nc.gpsimd.memset(ident[:, :], 0.0).then_inc(ident_zero, 1)
                nc.gpsimd.iota(iota_i[:, :], pattern=[[1, W]], base=0, channel_multiplier=0).then_inc(iota_done, 1)
                nc.gpsimd.iota(starts_i[:, :], pattern=[[W, MAXROUNDS]], base=0, channel_multiplier=0).then_inc(iota_done, 1)
                pool.wait_ge(ident_zero, START + 1)
                nc.gpsimd.affine_select(out=ident[:, :], in_=ident[:, :], compare_op=ALU.not_equal, fill=1.0,
                                        base=0, pattern=[[-1, 128]], channel_multiplier=1).then_inc(ident_done, 1)

            @block.vector
            def _(dve):
                nc.vector.memset(eps_t[:, :], EPS)
                dve.wait_ge(iota_done, START + 2)
                nc.vector.tensor_copy(iota_w[:, :], iota_i[:, :])
                nc.vector.tensor_copy(starts[:, :], starts_i[:, :]).then_inc(conv, 1)
                dve.wait_ge(edges_in, START + 48)
                nc.vector.tensor_copy(dst_f[:, :], dst_t[:, :]).then_inc(conv, 1)
                nc.vector.tensor_copy(dst_cf[:, :], dst_c[:, :]).then_inc(conv, 1)
                dve.wait_ge(conv, START + 3)
                nc.vector.tensor_reduce(lo[:, :], dst_cf[:, :], AX, ALU.min).then_inc(conv, 1)
                nc.vector.tensor_reduce(hi[:, :], dst_cf[:, :], AX, ALU.max).then_inc(conv, 1)
                dve.wait_ge(conv, START + 5)
                nc.vector.tensor_tensor(span[:, :], hi[:, :], lo[:, :], ALU.subtract).then_inc(mm_done, 1)
                dve.wait_ge(bc_loaded, START + 32)
                unit_base = base_bc[:, :].rearrange("p (u o) -> p u o", o=1).broadcast_to((EC, NU, UC))
                nc.vector.tensor_tensor(rel0[:, :].rearrange("p (u c) -> p u c", c=UC),
                                        dst_f[:, :].rearrange("p (u c) -> p u c", c=UC), unit_base, ALU.subtract)
                nc.vector.tensor_copy(base_row[:, :], base_bc[0:1, :])
                nc.vector.tensor_reduce(widest[:, :], span_row[:, :], AX, ALU.max).then_inc(tab, 1)
                dve.wait_ge(tab, START + 1)
                nc.vector.tensor_scalar(needed[:, :], starts[:, :], widest[:, :], None, ALU.is_le).then_inc(tab, 1)
                dve.wait_ge(tab, START + 2)
                nc.vector.tensor_reduce(widest[:, :], needed[:, :], AX, ALU.add).then_inc(tab, 1)
                dve.wait_ge(tab, START + 3)
                nc.vector.tensor_copy(rounds_t[:, :], widest[:, :])


def norm_transpose(nc, tag, sems, sb, x_rows, ident, eps_t, bank, xt, by_vector):
    stat_done, aggr_done, std_done, rstd_done, *tiles = sems(
        *(f"{tag}_{s}" for s in ("stat", "aggr", "std", "rstd")),
        *(f"{tag}_{s}{j}" for s in ("normed", "turned", "copied") for j in range(GT)))
    normed, turned, copied = tiles[:GT], tiles[GT:2 * GT], tiles[2 * GT:]
    with ExitStack() as ctx:
        stat = sb(ctx, "stat", [RT, NT, 6])
        mv = sb(ctx, "mv", [RT, NT, 2])
        std = sb(ctx, "std", [RT, NT])
        rstd = sb(ctx, "rstd", [RT, NT])
        xn = sb(ctx, "xn", [RT, GT, D])
        with nc.Block() as block:
            @block.vector
            def _(dve):
                with dve.Fori(0, NT) as t:
                    nc.vector.bn_stats(stat[:, bass.ds(t, 1), :], x_rows[:, bass.ds(t, 1), :]).then_inc(stat_done, 1)
                dve.wait_ge(stat_done, START + NT)
                for t in range(NT):
                    ins = nc.vector.bn_aggr(mv[:, t, :], stat[:, t, :])
                ins.then_inc(aggr_done, 1)
                dve.wait_ge(std_done, START + 1)
                nc.vector.reciprocal(rstd[:, :], std[:, :]).then_inc(rstd_done, 1)
                dve.wait_ge(rstd_done, START + 1)
                with dve.Fori(0, NG) as g:
                    for j in range(GT):
                        t = g * GT + j
                        dve.wait_ge(turned[j], START + g)
                        def norm(o, i):
                            return nc.vector.tensor_scalar(o, i, mv[:, bass.ds(t, 1), 0:1].rearrange("p a b -> p (a b)"),
                                                           rstd[:, bass.ds(t, 1)], ALU.subtract, ALU.mult)
                        row = x_rows[:, bass.ds(t, 1), :].rearrange("p a d -> p (a d)")
                        if by_vector:
                            norm(xn[:, j, 0:MUL], row[:, 0:MUL])
                            ins = norm(xn[:, j, MUL:D].rearrange("p (c u) -> p u c", c=3),
                                       row[:, MUL:D].rearrange("p (u c) -> p u c", c=3))
                        else:
                            ins = norm(xn[:, j, :], row)
                        ins.then_inc(normed[j], 1)

            @block.tensor
            def _(pe):
                with pe.Fori(0, NG) as g:
                    for j in range(GT):
                        pe.wait_ge(normed[j], START + g + 1)
                        pe.wait_ge(copied[j], START + g)
                        for k in range(KD):
                            ins = nc.tensor.transpose(bank[j][:, k * RT:(k + 1) * RT], xn[:, j, k * 128:(k + 1) * 128],
                                                      ident[0:RT, 0:RT])
                        ins.then_inc(turned[j], 1)

            @block.scalar
            def _(act):
                act.wait_ge(aggr_done, START + 1)
                nc.scalar.activation(std[:, :], mv[:, :, 1], ACT.Sqrt, bias=eps_t[0:RT, :], scale=1.0).then_inc(std_done, 1)
                with act.Fori(0, NG) as g:
                    for j in range(GT):
                        act.wait_ge(turned[j], START + g + 1)
                        nc.scalar.activation(xt[:, :, bass.ds(g * GC + j * RT, RT)],
                                             bank[j][:, 0:KD * RT].rearrange("p (k r) -> p k r", k=KD),
                                             ACT.Copy).then_inc(copied[j], 1)


def linear_attention(nc, A, sems, sb, bank, xt, mix):
    (w_in, mask_done, staged, kv_mm, kb_done, km_done, ke_done, kf_done, acc_mm, v_done, zero_mm,
     bd_done, q_mm, qm_done, qe_done, qr_done, qf_done, nd_mm, dn_done, rec_done, o_done, out_mm,
     mix_done) = sems(*("a0_" + s for s in (
         "w_in mask staged kv_mm kb km ke kf acc_mm v zero bd q_mm qm qe qr qf nd_mm dn rec o out_mm mix").split()))
    NH = 128 // DH0
    with ExitStack() as ctx:
        wkv = sb(ctx, "wkv", [128, KD, 2 * D])
        wq = sb(ctx, "wq", [128, KD, D])
        wo = sb(ctx, "wo", [128, KD, D])
        bk_bc = sb(ctx, "bk_bc", [RT, D])
        bv_bc = sb(ctx, "bv_bc", [RT, D])
        bq = sb(ctx, "bq", [128, KD])
        bo = sb(ctx, "bo", [128, KD])
        row_bias = sb(ctx, "row_bias", [RT, 2])
        stage = sb(ctx, "stage", [128, KD, GC])
        kb = sb(ctx, "kb", [RT, GT, D])
        km = sb(ctx, "km", [RT, GT, D])
        ke = sb(ctx, "ke", [RT, GT, D])
        vb = sb(ctx, "vb", [RT, GT, D])
        ones = sb(ctx, "ones", [RT, 128])
        zeros = sb(ctx, "zeros", [1, 512])
        kv_bd = sb(ctx, "kv_bd", [128, KD, 128])
        ks_bd = sb(ctx, "ks_bd", [128, KD, 128])
        qm = sb(ctx, "qm", [128, KD, GC])
        qr = sb(ctx, "qr", [128, KD, GC])
        dn = sb(ctx, "dn", [128, KD, GC])
        o_t = sb(ctx, "o_t", [128, KD, GC])
        acc = bank[4]
        with nc.Block() as block:
            @block.sync
            def _(sp):
                for t, name in ((wkv, "wkv0"), (wq, "wq0"), (wo, "wo0")):
                    sp.dma_start(t[:, :, :], A[name].rearrange("(k p) n -> p k n", p=128)).then_inc(w_in, 16)
                for t, name in ((bk_bc, "L0_mix_bk"), (bv_bc, "L0_mix_bv")):
                    sp.dma_start(t[:, :], A[name].rearrange("(o n) -> o n", o=1).broadcast_to((RT, D))).then_inc(w_in, 16)
                for t, name in ((bq, "L0_mix_bq_t"), (bo, "L0_mix_bo_t")):
                    sp.dma_start(t[:, :], A[name]).then_inc(w_in, 16)

            @block.gpsimd
            def _(pool):
                nc.gpsimd.memset(ones[:, :], 1.0).then_inc(mask_done, 1)
                nc.gpsimd.memset(zeros[:, :], 0.0).then_inc(mask_done, 1)
                nc.gpsimd.memset(row_bias[:, :], 0.0).then_inc(mask_done, 1)
                nc.gpsimd.memset(kv_bd[:, :, :], 0.0).then_inc(mask_done, 1)
                nc.gpsimd.memset(ks_bd[:, :, :], 0.0).then_inc(mask_done, 1)
                pool.wait_ge(mask_done, START + 5)
                nc.gpsimd.affine_select(out=row_bias[:, 1:2], in_=row_bias[:, 1:2], compare_op=ALU.is_ge, fill=NEG,
                                        base=LASTROWS - 1, pattern=[[0, 1]], channel_multiplier=-1).then_inc(mask_done, 1)
                with pool.Fori(0, NG) as g:
                    pool.wait_ge(kv_mm, START + g * GT)
                    nc.gpsimd.tensor_copy(stage[:, :, :], xt[:, :, bass.ds(g * GC, GC)]).then_inc(staged, 1)

            @block.tensor
            def _(pe):
                pe.wait_ge(w_in, START + 16 * 7)
                pe.wait_ge(mask_done, START + 6)
                nc.tensor.matmul(acc[:, :], zeros[:, 0:128], zeros[:, :], start=True, stop=False, skip_group_check=True)
                with pe.Fori(0, NG) as g:
                    pe.wait_ge(staged, START + g + 1)
                    for j in range(GT):
                        pe.wait_ge(v_done, START + g * GT)
                        for k in range(KD):
                            ins = nc.tensor.matmul(bank[j][0:RT, :], stage[:, k, j * RT:(j + 1) * RT], wkv[:, k, :],
                                                   start=(k == 0), stop=(k == KD - 1))
                        ins.then_inc(kv_mm, 1)
                    for j in range(GT):
                        pe.wait_ge(kf_done, START + g * GT + j + 1)
                        pe.wait_ge(v_done, START + g * GT + j + 1)
                        for k in range(KD):
                            f = slice(k * 128, (k + 1) * 128)
                            nc.tensor.matmul(acc[:, k * 256:k * 256 + 128], km[:, j, f], vb[:, j, f],
                                             start=False, stop=False, skip_group_check=True)
                            ins = nc.tensor.matmul(acc[:, k * 256 + 128:k * 256 + 256], km[:, j, f], ones[:, :],
                                                   start=False, stop=False, skip_group_check=True)
                        ins.then_inc(acc_mm, 1)
                nc.tensor.matmul(acc[:, :], zeros[:, 0:128], zeros[:, :], start=False, stop=True,
                                 skip_group_check=True).then_inc(zero_mm, 1)
                pe.wait_ge(bd_done, START + 1)
                with pe.Fori(0, NG) as g:
                    cols = bass.ds(g * GC, GC)
                    pe.wait_ge(qr_done, START + g * KD)
                    for f in range(KD):
                        for k in range(KD):
                            ins = nc.tensor.matmul(bank[f][:, 0:GC], wq[:, k, f * 128:(f + 1) * 128], xt[:, k, cols],
                                                   start=(k == 0), stop=(k == KD - 1))
                        ins.then_inc(q_mm, 1)
                    pe.wait_ge(o_done, START + g)
                    for f in range(KD):
                        pe.wait_ge(qf_done, START + g * KD + f + 1)
                        nc.tensor.matmul(bank[2 + f][:, 0:GC], kv_bd[:, f, :], qr[:, f, :], start=True, stop=True)
                        ins = nc.tensor.matmul(bank[5 + f][:, 0:GC], ks_bd[:, f, :], qr[:, f, :], start=True, stop=True)
                        ins.then_inc(nd_mm, 1)
                    pe.wait_ge(o_done, START + g + 1)
                    pe.wait_ge(mix_done, START + g * KD)
                    for f in range(KD):
                        b = (4, 7)[f]
                        for k in range(KD):
                            ins = nc.tensor.matmul(bank[b][:, 0:GC], wo[:, k, f * 128:(f + 1) * 128], o_t[:, k, :],
                                                   start=(k == 0), stop=(k == KD - 1))
                        ins.then_inc(out_mm, 1)

            @block.vector
            def _(dve):
                dve.wait_ge(w_in, START + 16 * 7)
                dve.wait_ge(mask_done, START + 6)

                def keys(g, last):
                    for j in range(GT):
                        n = g * GT + j
                        dve.wait_ge(kv_mm, START + n + 1)
                        dve.wait_ge(acc_mm, START + g * GT)
                        pad = 1 if last and j == GT - 1 else 0
                        nc.vector.scalar_tensor_tensor(out=kb[:, j, :], in0=bank[j][0:RT, 0:D],
                                                       scalar=row_bias[:, pad:pad + 1], in1=bk_bc[:, :],
                                                       op0=ALU.add, op1=ALU.add).then_inc(kb_done, 1)
                        nc.vector.tensor_tensor(vb[:, j, :], bank[j][0:RT, D:2 * D], bv_bc[:, :], ALU.add).then_inc(v_done, 1)
                        dve.wait_ge(kb_done, START + n + 1)
                        nc.vector.tensor_scalar(km[:, j, :], kb[:, j, :], 0.0, None, ALU.min).then_inc(km_done, 1)
                    for j in range(GT):
                        n = g * GT + j
                        dve.wait_ge(ke_done, START + n + 1)
                        nc.vector.scalar_tensor_tensor(out=km[:, j, :], in0=kb[:, j, :], scalar=0.0, in1=ke[:, j, :],
                                                       op0=ALU.max, op1=ALU.add).then_inc(kf_done, 1)
                with dve.Fori(0, NG - 1) as g:
                    keys(g, False)
                keys(NG - 1, True)
                dve.wait_ge(zero_mm, START + 1)
                for f in range(KD):
                    for h in range(NH):
                        s = slice(h * DH0, (h + 1) * DH0)
                        nc.vector.tensor_copy(kv_bd[s, f, s], acc[s, f * 256 + h * DH0:f * 256 + (h + 1) * DH0])
                        ins = nc.vector.tensor_copy(ks_bd[s, f, s], acc[s, f * 256 + 128:f * 256 + 128 + DH0])
                ins.then_inc(bd_done, 1)
                with dve.Fori(0, NG) as g:
                    for f in range(KD):
                        n = g * KD + f
                        dve.wait_ge(q_mm, START + n + 1)
                        nc.vector.tensor_scalar(qm[:, f, :], bank[f][:, 0:GC], bq[:, f:f + 1], 0.0, ALU.add, ALU.min)\
                          .then_inc(qm_done, 1)
                    for f in range(KD):
                        n = g * KD + f
                        dve.wait_ge(qe_done, START + n + 1)
                        dve.wait_ge(qr_done, START + n + 1)
                        nc.vector.tensor_tensor(qr[:, f, :], qr[:, f, :], qm[:, f, :], ALU.add).then_inc(qf_done, 1)
                    for f in range(KD):
                        n = g * KD + f
                        dve.wait_ge(nd_mm, START + n + 1)
                        nc.vector.tensor_scalar(dn[:, f, :], bank[5 + f][:, 0:GC], 1e-6, None, ALU.add).then_inc(dn_done, 1)
                        dve.wait_ge(dn_done, START + n + 1)
                        nc.vector.reciprocal(dn[:, f, :], dn[:, f, :]).then_inc(rec_done, 1)
                        dve.wait_ge(rec_done, START + n + 1)
                        dve.wait_ge(out_mm, START + g * KD)
                        ins = nc.vector.tensor_tensor(o_t[:, f, :], bank[2 + f][:, 0:GC], dn[:, f, :], ALU.mult)
                    ins.then_inc(o_done, 1)

            @block.scalar
            def _(act):
                with act.Fori(0, NG * GT // GT) as g:
                    for j in range(GT):
                        act.wait_ge(km_done, START + g * GT + j + 1)
                        act.wait_ge(kf_done, START + g * GT)
                        nc.scalar.activation(ke[:, j, :], km[:, j, :], ACT.Exp).then_inc(ke_done, 1)
                act.wait_ge(w_in, START + 16 * 7)
                with act.Fori(0, NG) as g:
                    for f in range(KD):
                        n = g * KD + f
                        act.wait_ge(nd_mm, START + g * KD)
                        act.wait_ge(q_mm, START + n + 1)
                        act.wait_ge(qm_done, START + n + 1)
                        nc.scalar.activation(qr[:, f, :], bank[f][:, 0:GC], ACT.Relu, bias=bq[:, f:f + 1], scale=1.0)\
                          .then_inc(qr_done, 1)
                        nc.scalar.activation(qm[:, f, :], qm[:, f, :], ACT.Exp).then_inc(qe_done, 1)
                    for f in range(KD):
                        n = g * KD + f
                        act.wait_ge(out_mm, START + n + 1)
                        nc.scalar.activation(mix[:, f, bass.ds(g * GC, GC)], bank[(4, 7)[f]][:, 0:GC], ACT.Identity,
                                             bias=bo[:, f:f + 1], scale=1.0).then_inc(mix_done, 1)


def adjacency(nc, A, sems, sb, bank, ident, src_t, a_dram, pair_dram, range_dram, crowded_t):
    (edges_in, iota_done, step, pairs_out, pairs_in, range_out, range_in, tile_iota, zeros, hot_0, hot_1, used_0, used_1,
     acc_mm, rows_a, rows_d, turned, cols_0, cols_1, cols_2, squared, stored, bad_mm, passed) = sems(*("a_" + s for s in (
         "edges_in iota step pairs_out pairs_in range_out range_in tile_iota zeros hot_0 hot_1 used_0 used_1 "
         "acc_mm rows_a rows_d turned cols_0 cols_1 cols_2 squared stored bad_mm passed").split()))
    hot_done, used, cols_done = (hot_0, hot_1), (used_0, used_1), (cols_0, cols_1, cols_2)
    DVE_BANKS = 3
    ACT_COLS = (AB - DVE_BANKS) * AC
    with ExitStack() as ctx:
        dst_t = sb(ctx, "dst_t", [EC, NCH], I32)
        dst_f = sb(ctx, "dst_f", [EC, NCH])
        src_f = sb(ctx, "src_f", [EC, NCH])
        dst_p = sb(ctx, "dst_p", [NU, NPAIR // NU, PC * EC], I32)
        dst_pf = sb(ctx, "dst_pf", [NU, NPAIR // NU, PC * EC])
        ends = sb(ctx, "ends", [NU, 2, NPAIR // NU])
        ends_bc = sb(ctx, "ends_bc", [NT, 2, NPAIR])
        up_i = sb(ctx, "up_i", [NT, NPAIR], I32)
        up = sb(ctx, "up", [NT, NPAIR])
        down = sb(ctx, "down", [NT, NPAIR])
        tile_i = sb(ctx, "tile_i", [NT, 2], I32)
        tile_at = sb(ctx, "tile_at", [NT, 2])
        meets = sb(ctx, "meets", [NT, NPAIR])
        first = sb(ctx, "first", [NT, 1])
        last = sb(ctx, "last", [NT, 1])
        range_i = sb(ctx, "range_i", [NT, 2], I32)
        ranges = sb(ctx, "ranges", [1, NT, 2], I32)
        iota_i = sb(ctx, "iota_i", [EC, RT], I32)
        iota_t = sb(ctx, "iota_t", [EC, RT])
        iota_s = sb(ctx, "iota_s", [EC, AB * AC], I16)
        hot_dst = sb(ctx, "hot_dst", [EC, PC, RT], BF16)
        hot_src = [sb(ctx, f"hot_src{c}", [EC, AB * AC], BF16) for c in range(PC)]
        nil = sb(ctx, "nil", [1, AC], BF16)
        ident_b = sb(ctx, "ident_b", [RT, RT], BF16)
        a_rows = sb(ctx, "a_rows", [RT, NP], BF16)
        squares = sb(ctx, "squares", [RT, NP], BF16)
        a_cols = sb(ctx, "a_cols", [128, KT, GC], BF16)
        square_sum = sb(ctx, "square_sum", [RT, NT])
        bad = sb(ctx, "bad", [RT, NT])
        bad_row = sb(ctx, "bad_row", [RT, 1])
        ones = sb(ctx, "ones", [RT, 1])
        p_acc = bank[0:AB]
        p_t = [bank[(AB + i) % 8][:, :].bitcast(BF16) for i in range(len(TB))]
        ORDER = [(len(TB) - 1 + m) % AB for m in range(AB)]
        p_bad = bank[0]

        def tile_range(eng, t):
            return [eng.value_load(ranges[0:1, bass.ds(t, 1), k:k + 1].rearrange("p a b -> p (a b)"), min_val=k,
                                   max_val=NPAIR - 1 + k) for k in range(2)]

        def cols(eng, t, j, i):
            at, m = sum(TB[:i]), TB[i]
            eng.wait_ge(turned, START + t * len(TB) + i + 1)
            to, read = a_cols[:, at:at + m, j * RT:(j + 1) * RT], p_t[i][:, 0:m * RT].rearrange("p (k r) -> p k r", k=m)
            ins = nc.vector.tensor_copy(to, read) if i == 1 else nc.scalar.activation(to, read, ACT.Copy)
            ins.then_inc(cols_done[i], 1)

        with nc.Block() as block:
            @block.sync
            def _(sp):
                sp.dma_start(dst_p[:, :, :], A["dst_c"].rearrange("u (q e) -> u q e", e=PC * EC)).then_inc(edges_in, 16)
                sp.dma_start(dst_t[:, :], A["dst_t"]).then_inc(edges_in, 16)
                sp.wait_ge(step, START + 3)
                for k in range(2):
                    sp.dma_start(pair_dram[k].rearrange("(u q) -> u q", u=NU), ends[:, k, :]).then_inc(pairs_out, 16)
                sp.wait_ge(pairs_out, START + 32)
                for k in range(2):
                    sp.dma_start(ends_bc[:, k, :], pair_dram[k].rearrange("(o c) -> o c", o=1).broadcast_to((NT, NPAIR)))\
                      .then_inc(pairs_in, 16)
                sp.wait_ge(step, START + 13)
                sp.dma_start(range_dram, range_i[:, :]).then_inc(range_out, 16)
                sp.wait_ge(range_out, START + 16)
                sp.dma_start(ranges[:, :, :], range_dram.rearrange("(o t) k -> o t k", o=1)).then_inc(range_in, 16)
                with sp.Fori(0, NG) as g:
                    for i in range(len(TB)):
                        sp.wait_ge(cols_done[i], START + g * GT + GT)
                    sp.dma_start(a_dram[bass.ds(g, 1), :, :, :].rearrange("o p k c -> (o p) k c"), a_cols[:, :, :])\
                      .then_inc(stored, 16)
                sp.wait_ge(stored, START + NG * 16)

            @block.gpsimd
            def _(pool):
                nc.gpsimd.iota(up_i[:, :], pattern=[[1, NPAIR]], base=1, channel_multiplier=0)
                nc.gpsimd.iota(tile_i[:, :], pattern=[[RT, 2]], base=0, channel_multiplier=RT)
                nc.gpsimd.iota(iota_i[:, :], pattern=[[1, RT]], base=0, channel_multiplier=0)
                nc.gpsimd.iota(iota_s[:, :], pattern=[[1, AB * AC]], base=0, channel_multiplier=0).then_inc(iota_done, 1)
                nc.gpsimd.memset(nil[:, :], 0.0)
                nc.gpsimd.memset(ones[:, :], 1.0)
                nc.gpsimd.memset(a_rows[:, :], 0.0).then_inc(zeros, 1)

            @block.vector
            def _(dve):
                n = [0]

                def then(ins):
                    ins.then_inc(step, 1)
                    n[0] += 1
                    dve.wait_ge(step, START + n[0])
                dve.wait_ge(edges_in, START + 32)
                dve.wait_ge(iota_done, START + 1)
                nc.vector.tensor_copy(dst_f[:, :], dst_t[:, :])
                nc.vector.tensor_copy(src_f[:, :], src_t[:, :])
                nc.vector.tensor_copy(ident_b[:, :], ident[0:RT, 0:RT])
                nc.vector.tensor_copy(iota_t[:, :], iota_i[:, :]).then_inc(tile_iota, 1)
                nc.vector.tensor_copy(up[:, :], up_i[:, :])
                nc.vector.tensor_copy(tile_at[:, :], tile_i[:, :])
                then(nc.vector.tensor_copy(dst_pf[:, :, :], dst_p[:, :, :]))
                then(nc.vector.tensor_reduce(ends[:, 0, :], dst_pf[:, :, :], AX, ALU.min))
                then(nc.vector.tensor_reduce(ends[:, 1, :], dst_pf[:, :, :], AX, ALU.max))
                dve.wait_ge(pairs_in, START + 32)
                then(nc.vector.tensor_scalar(down[:, :], up[:, :], -1.0, float(NPAIR + 1), ALU.mult, ALU.add))
                then(nc.vector.tensor_scalar(meets[:, :], ends_bc[:, 0, :], tile_at[:, 1:2], None, ALU.is_lt))
                then(nc.vector.scalar_tensor_tensor(out=meets[:, :], in0=ends_bc[:, 1, :], scalar=tile_at[:, 0:1],
                                                    in1=meets[:, :], op0=ALU.is_ge, op1=ALU.mult))
                nc.vector.tensor_tensor(up[:, :], up[:, :], meets[:, :], ALU.mult)
                then(nc.vector.tensor_tensor(down[:, :], down[:, :], meets[:, :], ALU.mult))
                nc.vector.tensor_reduce(last[:, :], up[:, :], AX, ALU.max)
                then(nc.vector.tensor_reduce(first[:, :], down[:, :], AX, ALU.max))
                then(nc.vector.tensor_scalar(first[:, :], first[:, :], -1.0, float(NPAIR), ALU.mult, ALU.add))
                then(nc.vector.tensor_scalar(first[:, :], first[:, :], float(NPAIR - 1), None, ALU.min))
                then(nc.vector.scalar_tensor_tensor(out=last[:, :], in0=first[:, :], scalar=1.0, in1=last[:, :],
                                                    op0=ALU.add, op1=ALU.max))
                then(nc.vector.tensor_copy(range_i[:, 0:1], first[:, :]))
                then(nc.vector.tensor_copy(range_i[:, 1:2], last[:, :]))
                dve.wait_ge(range_in, START + 16)
                dve.wait_ge(zeros, START + 1)
                visits = dve.alloc_register("a_visits_dve")
                dve.reg_mov(visits, 0)
                with dve.Fori(0, NG) as g:
                    for j in range(GT):
                        t = g * GT + j
                        lo, hi = tile_range(dve, t)
                        wait_alone(dve, tile_iota, t + 1, passed)
                        with dve.Fori(lo, hi) as u:
                            v = dve.snap(visits, min_val=0, max_val=NT * NPAIR)
                            for c in range(PC):
                                col = bass.ds(u * PC + c, 1)
                                dve.wait_ge(used[c], START + v)
                                nc.vector.tensor_scalar(hot_dst[:, c, :], iota_t[:, :], dst_f[:, col], None, ALU.is_equal)
                                nc.vector.tensor_scalar(hot_src[c][:, :], iota_s[:, :], src_f[:, col], None, ALU.is_equal)\
                                  .then_inc(hot_done[c], 1)
                            dve.reg_add(visits, visits, 1)
                        nc.vector.tensor_scalar(iota_t[:, :], iota_t[:, :], float(RT), None, ALU.add).then_inc(tile_iota, 1)
                        dve.wait_ge(acc_mm, START + t + 1)
                        dve.wait_ge(turned, START + t * len(TB))
                        dve.wait_ge(squared, START + t)
                        for m in range(AB - DVE_BANKS, AB):
                            ins = nc.vector.tensor_copy(a_rows[:, m * AC:(m + 1) * AC], p_acc[m][0:RT, 0:AC])
                        ins.then_inc(rows_d, 1)
                        dve.wait_ge(stored, START + g * 16)
                        cols(dve, t, j, 1)
                dve.wait_ge(squared, START + NT)
                then(nc.vector.tensor_scalar(bad[:, :], square_sum[:, :], float(EXACT * EXACT), None, ALU.is_ge))
                then(nc.vector.tensor_reduce(bad_row[:, :], bad[:, :], AX, ALU.max))
                dve.wait_ge(bad_mm, START + 1)
                then(nc.vector.tensor_scalar(bad[0:1, 0:1], p_bad[0:1, 0:1], 0.5, None, ALU.is_ge))
                then(nc.vector.tensor_copy(crowded_t[:, :], bad[0:1, 0:1]))

            @block.tensor
            def _(pe):
                pe.wait_ge(range_in, START + 16)
                pe.wait_ge(zeros, START + 1)
                visits = pe.alloc_register("a_visits_pe")
                pe.reg_mov(visits, 0)

                def turn(t):
                    pe.wait_ge(rows_a, START + t + 1)
                    pe.wait_ge(rows_d, START + t + 1)
                    pe.wait_ge(cols_done[0], START + t)
                    at = 0
                    for i, m in enumerate(TB):
                        for k in range(m):
                            ins = nc.tensor.transpose(p_t[i][:, k * RT:(k + 1) * RT], a_rows[:, (at + k) * 128:(at + k + 1) * 128],
                                                      ident_b[:, :])
                        ins.then_inc(turned, 1)
                        at += m

                def counts(t):
                    lo, hi = tile_range(pe, t)
                    for m in ORDER:
                        if m < len(TB) - 1:
                            pe.wait_ge(cols_done[1 + m], START + t)
                        nc.tensor.matmul(p_acc[m][0:RT, 0:AC], nil[:, 0:RT], nil[:, :], start=True, stop=False,
                                         skip_group_check=True)
                    with pe.Fori(lo, hi) as u:
                        v = pe.snap(visits, min_val=0, max_val=NT * NPAIR)
                        for c in range(PC):
                            pe.wait_ge(hot_done[c], START + v + 1)
                            for m in ORDER:
                                ins = nc.tensor.matmul(p_acc[m][0:RT, 0:AC], hot_dst[:, c, :],
                                                       hot_src[c][:, m * AC:(m + 1) * AC], start=False, stop=False,
                                                       skip_group_check=True)
                            ins.then_inc(used[c], 1)
                        pe.reg_add(visits, visits, 1)
                    for m in range(AB):
                        ins = nc.tensor.matmul(p_acc[m][0:RT, 0:1], nil[:, 0:RT], nil[:, 0:1], start=False, stop=True,
                                               skip_group_check=True)
                    ins.then_inc(acc_mm, 1)
                with pe.Fori(0, NT) as t:
                    counts(t)
                    turn(t)
                pe.wait_ge(step, START + 15)
                nc.tensor.matmul(p_bad[0:1, 0:1], bad_row[:, :], ones[:, :], start=True, stop=True).then_inc(bad_mm, 1)

            @block.scalar
            def _(act):
                act.wait_ge(zeros, START + 1)

                with act.Fori(0, NG) as g:
                    for j in range(GT):
                        t = g * GT + j
                        act.wait_ge(acc_mm, START + t + 1)
                        act.wait_ge(turned, START + t * len(TB))
                        act.wait_ge(squared, START + t)
                        for m in range(AB - DVE_BANKS):
                            ins = nc.scalar.activation(a_rows[:, m * AC:(m + 1) * AC], p_acc[m][0:RT, 0:AC], ACT.Copy)
                        ins.then_inc(rows_a, 1)
                        act.wait_ge(stored, START + g * 16)
                        cols(act, t, j, 0)
                        cols(act, t, j, 2)
                        act.wait_ge(rows_a, START + t + 1)
                        act.wait_ge(rows_d, START + t + 1)
                        act.wait_ge(squared, START + t)
                        nc.scalar.activation(squares[:, :], a_rows[:, :], ACT.Square,
                                             accum_out=square_sum[:, bass.ds(t, 1)]).then_inc(squared, 1)


def gated_graph(nc, A, sems, sb, bank, nf, a_dram, crowded_t):
    (w_in, bias_done, t1_mm, t1_done, h_mm, h_done, part_1, rest_1, part_2, part_3, a_in_0, a_in_1, ah_mm, msg_done,
     r_mm, hn_mm, xn_mm, z_mm, r_done, hn_used, t_done, n_done, z_done, blend, nf_done, passed) = sems(*("d_" + s for s in (
         "w_in bias t1_mm t1 h_mm h part_1 rest_1 part_2 part_3 a_in_0 a_in_1 ah_mm msg "
         "r_mm hn_mm xn_mm z_mm r hn_used t n z blend nf passed").split()))
    a_in = (a_in_0, a_in_1)
    NH = KT // HB
    HH = HN // 2
    with ExitStack() as ctx:
        w1 = sb(ctx, "w1", [128, KD, D])
        w2 = sb(ctx, "w2", [128, KD, D])
        wih = sb(ctx, "wih", [128, KD, 3 * D])
        whh = sb(ctx, "whh", [128, KD, 3 * D])
        b1 = sb(ctx, "b1", [128, KD])
        b2_bc = sb(ctx, "b2_bc", [128, D])
        bih = sb(ctx, "bih", [128, 3 * KD])
        bhh = sb(ctx, "bhh", [128, 3 * KD])
        bsum = sb(ctx, "bsum", [128, 3 * KD])
        t1 = sb(ctx, "t1", [128, KD, HN])
        h = sb(ctx, "h", [128, HB, D])
        parts = sb(ctx, "parts", [128, PARTS, KT, D], BF16)
        stage = sb(ctx, "stage", [128, 2, HB, D], BF16)
        a_cols = [sb(ctx, f"a_cols{b}", [128, KT, GC], BF16) for b in range(2)]
        msg = sb(ctx, "msg", [128, KD, GC])
        r_t = sb(ctx, "r_t", [128, KD, GC])
        t_t = sb(ctx, "t_t", [128, KD, GC])
        n_t = sb(ctx, "n_t", [128, KD, GC])
        z_t = sb(ctx, "z_t", [128, KD, GC])
        d_t = sb(ctx, "d_t", [128, KD, GC])
        p_t1, p_h = bank[0:4], bank[4:8]
        p_msg, (p_r, p_hn, p_xn, p_z) = bank[0:2], bank[2:6]

        with nc.Block() as block:
            @block.sync
            def _(sp):
                crowded = sp.value_load(crowded_t[0:1, 0:1], min_val=0, max_val=1)
                with sp.If(crowded < 1):
                    for w, name in ((w1, "w1_0"), (w2, "w2_0"), (wih, "wih_0"), (whh, "whh_0")):
                        sp.dma_start(w[:, :, :], A[name].rearrange("(k p) n -> p k n", p=128)).then_inc(w_in, 16)
                    for w, name in ((b1, "L0_gnn_b1_t"), (bih, "L0_gnn_b_ih_t"), (bhh, "L0_gnn_b_hh_t")):
                        sp.dma_start(w[:, :], A[name]).then_inc(w_in, 16)
                    sp.dma_start(b2_bc[:, :], A["L0_gnn_b2"].rearrange("(o n) -> o n", o=1).broadcast_to((128, D)))\
                      .then_inc(w_in, 16)
                    with sp.Fori(0, STEPS) as s:
                        with sp.Fori(0, NG // 2) as i:
                            for b in range(2):
                                n = s * NG + i * 2 + b
                                sp.wait_ge(ah_mm, START + n * KD - 2 * KD + KD)
                                sp.dma_start(a_cols[b][:, :, :], a_dram[bass.ds(i * 2 + b, 1), :, :, :]
                                             .rearrange("o p k c -> (o p) k c")).then_inc(a_in[b], 16)

            @block.gpsimd
            def _(pool):
                crowded = pool.value_load(crowded_t[0:1, 0:1], min_val=0, max_val=1)
                with pool.If(crowded < 1):
                    with pool.Fori(0, STEPS * NH) as q:
                        pool.wait_ge(part_1, START + q + 1)
                        nc.gpsimd.tensor_tensor(h[:, :, :], h[:, :, :], stage[:, 0, :, :], ALU.subtract).then_inc(rest_1, 1)
                        pool.wait_ge(part_2, START + q + 1)
                        nc.gpsimd.tensor_tensor(h[:, :, :], h[:, :, :], stage[:, 1, :, :], ALU.subtract).then_inc(rest_1, 1)

            @block.tensor
            def _(pe):
                crowded = pe.value_load(crowded_t[0:1, 0:1], min_val=0, max_val=1)
                with pe.If(crowded < 1):
                    pe.wait_ge(w_in, START + 16 * 8)
                    with pe.Fori(0, STEPS) as s:
                        wait_alone(pe, nf_done, s * NG, passed)
                        wait_alone(pe, z_done, s * NG * KD, passed)
                        with pe.Fori(0, NH) as i:
                            q = s * NH + i
                            for f in range(KD):
                                for half in range(2):
                                    pe.wait_ge(t1_done, START + q * 4)
                                    for k in range(KD):
                                        ins = nc.tensor.matmul(p_t1[f * 2 + half][:, 0:HH], w1[:, k, f * 128:(f + 1) * 128],
                                                               nf[:, k, bass.ds(i * HN + half * HH, HH)],
                                                               start=(k == 0), stop=(k == KD - 1))
                                    ins.then_inc(t1_mm, 1)
                            pe.wait_ge(t1_done, START + q * 4 + 4)
                            for j in range(HB):
                                pe.wait_ge(h_done, START + q * HB + max(j - 3, 0))
                                for k in range(KD):
                                    ins = nc.tensor.matmul(p_h[j % 4][:, 0:D], t1[:, k, j * 128:(j + 1) * 128], w2[:, k, :],
                                                           start=(k == 0), stop=(k == KD - 1))
                                ins.then_inc(h_mm, 1)
                        wait_alone(pe, h_done, (s * NH + NH) * HB, passed)
                        with pe.Fori(0, NG // 2) as i:
                            for b in range(2):
                                n = s * NG + i * 2 + b
                                pe.wait_ge(a_in[b], START + (s * (NG // 2) + i) * 16 + 16)
                                for f in range(KD):
                                    pe.wait_ge(msg_done, START + n * KD + f - 1)
                                    for k in range(KT):
                                        if k % HB == 0:
                                            pe.wait_ge(part_3, START + s * NH + k // HB + 1)
                                        for m in range(PARTS):
                                            ins = nc.tensor.matmul(p_msg[f][:, 0:GC], parts[:, m, k, f * 128:(f + 1) * 128],
                                                                   a_cols[b][:, k, :], start=(k == 0 and m == 0),
                                                                   stop=(k == KT - 1 and m == PARTS - 1))
                                    ins.then_inc(ah_mm, 1)
                                cols = bass.ds((i * 2 + b) * GC, GC)

                                def gate(out_p, part, f, start, src, stop):
                                    w = whh if src is nf else wih
                                    for k in range(KD):
                                        x = nf[:, k, cols] if src is nf else msg[:, k, :]
                                        ins = nc.tensor.matmul(out_p[:, 0:GC], w[:, k, part * D + f * 128:part * D + (f + 1) * 128], x,
                                                               start=(start and k == 0), stop=(stop and k == KD - 1))
                                    return ins
                                for f in range(KD):
                                    q = n * KD + f
                                    pe.wait_ge(hn_used, START + q)
                                    gate(p_hn, 2, f, True, nf, True).then_inc(hn_mm, 1)
                                    pe.wait_ge(r_done, START + q)
                                    gate(p_r, 0, f, True, nf, False)
                                    pe.wait_ge(msg_done, START + n * KD + KD)
                                    gate(p_r, 0, f, False, msg, True).then_inc(r_mm, 1)
                                    pe.wait_ge(t_done, START + q)
                                    gate(p_xn, 2, f, True, msg, True).then_inc(xn_mm, 1)
                                    pe.wait_ge(z_done, START + q)
                                    gate(p_z, 1, f, True, nf, False)
                                    gate(p_z, 1, f, False, msg, True).then_inc(z_mm, 1)

            @block.vector
            def _(dve):
                crowded = dve.value_load(crowded_t[0:1, 0:1], min_val=0, max_val=1)
                with dve.If(crowded < 1):
                    dve.wait_ge(w_in, START + 16 * 8)
                    nc.vector.tensor_tensor(bsum[:, :], bih[:, :], bhh[:, :], ALU.add).then_inc(bias_done, 1)
                    with dve.Fori(0, STEPS) as s:
                        with dve.Fori(0, NH) as i:
                            q = s * NH + i
                            dve.wait_ge(part_3, START + q)
                            for j in range(HB):
                                dve.wait_ge(h_mm, START + q * HB + j + 1)
                                nc.vector.tensor_tensor(h[:, j, :], p_h[j % 4][:, 0:D], b2_bc[:, :], ALU.add).then_inc(h_done, 1)
                            block_i = bass.ds(i * HB, HB)
                            dve.wait_ge(h_done, START + q * HB + HB)
                            nc.vector.tensor_copy(stage[:, 0, :, :], h[:, :, :]).then_inc(part_1, 1)
                            dve.wait_ge(part_1, START + q + 1)
                            nc.vector.tensor_copy(parts[:, 0, block_i, :], stage[:, 0, :, :])
                            dve.wait_ge(rest_1, START + q * 2 + 1)
                            nc.vector.tensor_copy(stage[:, 1, :, :], h[:, :, :]).then_inc(part_2, 1)
                            dve.wait_ge(part_2, START + q + 1)
                            nc.vector.tensor_copy(parts[:, 1, block_i, :], stage[:, 1, :, :])
                            dve.wait_ge(rest_1, START + q * 2 + 2)
                            nc.vector.tensor_copy(parts[:, 2, block_i, :], h[:, :, :]).then_inc(part_3, 1)
                        with dve.Fori(0, NG) as g:
                            cols = bass.ds(g * GC, GC)
                            for f in range(KD):
                                q = (s * NG + g) * KD + f
                                dve.wait_ge(hn_mm, START + q + 1)
                                dve.wait_ge(r_done, START + q + 1)
                                nc.vector.scalar_tensor_tensor(out=t_t[:, f, :], in0=p_hn[:, 0:GC],
                                                               scalar=bhh[:, 2 * KD + f:2 * KD + f + 1], in1=r_t[:, f, :],
                                                               op0=ALU.add, op1=ALU.mult).then_inc(hn_used, 1)
                                dve.wait_ge(hn_used, START + q + 1)
                                dve.wait_ge(xn_mm, START + q + 1)
                                nc.vector.tensor_tensor(t_t[:, f, :], t_t[:, f, :], p_xn[:, 0:GC], ALU.add).then_inc(t_done, 1)
                            q = s * NG + g
                            dve.wait_ge(n_done, START + q * KD + KD)
                            dve.wait_ge(z_done, START + q * KD + KD)
                            nc.vector.tensor_tensor(d_t[:, :, :], nf[:, :, cols], n_t[:, :, :], ALU.subtract).then_inc(blend, 1)
                            dve.wait_ge(blend, START + q * 2 + 1)
                            nc.vector.tensor_tensor(d_t[:, :, :], d_t[:, :, :], z_t[:, :, :], ALU.mult).then_inc(blend, 1)
                            dve.wait_ge(blend, START + q * 2 + 2)
                            nc.vector.tensor_tensor(nf[:, :, cols], d_t[:, :, :], n_t[:, :, :], ALU.add).then_inc(nf_done, 1)

            @block.scalar
            def _(act):
                crowded = act.value_load(crowded_t[0:1, 0:1], min_val=0, max_val=1)
                with act.If(crowded < 1):
                    act.wait_ge(w_in, START + 16 * 8)
                    act.wait_ge(bias_done, START + 1)
                    with act.Fori(0, STEPS) as s:
                        with act.Fori(0, NH) as i:
                            q = s * NH + i
                            act.wait_ge(h_mm, START + q * HB)
                            for f in range(KD):
                                for half in range(2):
                                    act.wait_ge(t1_mm, START + q * 4 + f * 2 + half + 1)
                                    nc.scalar.activation(t1[:, f, half * HH:(half + 1) * HH], p_t1[f * 2 + half][:, 0:HH],
                                                         ACT.Relu, bias=b1[:, f:f + 1], scale=1.0).then_inc(t1_done, 1)
                        with act.Fori(0, NG) as g:
                            n = s * NG + g
                            act.wait_ge(z_mm, START + n * KD)
                            for f in range(KD):
                                act.wait_ge(ah_mm, START + n * KD + f + 1)
                                nc.scalar.activation(msg[:, f, :], p_msg[f][:, 0:GC], ACT.Copy).then_inc(msg_done, 1)
                            for f in range(KD):
                                q = n * KD + f
                                act.wait_ge(r_mm, START + q + 1)
                                act.wait_ge(hn_used, START + q)
                                nc.scalar.activation(r_t[:, f, :], p_r[:, 0:GC], ACT.Sigmoid, bias=bsum[:, f:f + 1], scale=1.0)\
                                  .then_inc(r_done, 1)
                                act.wait_ge(t_done, START + q + 1)
                                act.wait_ge(nf_done, START + n)
                                nc.scalar.activation(n_t[:, f, :], t_t[:, f, :], ACT.Tanh,
                                                     bias=bih[:, 2 * KD + f:2 * KD + f + 1], scale=1.0).then_inc(n_done, 1)
                                act.wait_ge(z_mm, START + q + 1)
                                nc.scalar.activation(z_t[:, f, :], p_z[:, 0:GC], ACT.Sigmoid, bias=bsum[:, KD + f:KD + f + 1],
                                                     scale=1.0).then_inc(z_done, 1)


def gated_graph_by_edges(nc, A, sems, sb, bank, tables, nf, h_dram, crowded_t):
    src_t, rel0, base_row, rounds_t, iota_w = tables
    (w_in, bias_done, t1_mm, t1_done, h_mm, h_done, h_stored, acc_zero, tab, hot_a, hot_b, sum_a, sum_b,
     added, idx_a, idx_b, r_mm, hn_mm, xn_mm, z_mm, r_done, hn_used, t_done, n_done, z_done, blend,
     nf_done, passed, *gathered) = sems(*("g_" + s for s in (
         "w_in bias t1_mm t1 h_mm h h_stored acc_zero tab hot_a hot_b sum_a sum_b added idx_a idx_b "
         "r_mm hn_mm xn_mm z_mm r hn_used t n z blend nf passed").split()),
                              *(f"g_gathered{j}" for j in range(ITC)))
    hot_ready, summed, idx_ready = (hot_a, hot_b), (sum_a, sum_b), (idx_a, idx_b)
    with ExitStack() as ctx:
        w1 = sb(ctx, "w1", [128, KD, D])
        w2 = sb(ctx, "w2", [128, KD, D])
        wih = sb(ctx, "wih", [128, KD, 3 * D])
        whh = sb(ctx, "whh", [128, KD, 3 * D])
        b1 = sb(ctx, "b1", [128, KD])
        b2_bc = sb(ctx, "b2_bc", [RT, D])
        bih = sb(ctx, "bih", [128, 3 * KD])
        bhh = sb(ctx, "bhh", [128, 3 * KD])
        bsum = sb(ctx, "bsum", [128, 3 * KD])
        msg = sb(ctx, "msg", [128, KD, NW_COLS])
        rel = sb(ctx, "rel", [EC, NCH])
        base = sb(ctx, "base", [1, NU], I32)
        idx = sb(ctx, "idx", [EC, 2, UC], I32)
        rows = [sb(ctx, f"rows{j}", [EC, D]) for j in range(ITC)]
        hot = sb(ctx, "hot", [EC, 2, UC, W])
        t1 = sb(ctx, "t1", [128, KD, GC])
        h_rows = sb(ctx, "h_rows", [RT, GT, D])
        r_t = sb(ctx, "r_t", [128, KD, GC])
        t_t = sb(ctx, "t_t", [128, KD, GC])
        n_t = sb(ctx, "n_t", [128, KD, GC])
        z_t = sb(ctx, "z_t", [128, KD, GC])
        d_t = sb(ctx, "d_t", [128, KD, GC])
        p_sum = bank[0:2]
        p_r, p_hn, p_xn, p_z = bank[2:6]
        p_t1 = bank[6:8]
        p_h = (p_r, p_hn, p_xn, p_z)

        def begin(eng, tag):
            rounds = eng.value_load(rounds_t[0:1, 0:1], min_val=1, max_val=MAXROUNDS)
            reg = eng.alloc_register(f"g_its_{tag}")
            eng.reg_mov(reg, 0)
            return rounds, reg

        def count(eng, reg):
            return eng.snap(reg, min_val=0, max_val=STEPS * NIT * MAXROUNDS)

        with nc.Block() as block:
            @block.sync
            def _(sp):
                crowded = sp.value_load(crowded_t[0:1, 0:1], min_val=0, max_val=1)
                with sp.If(crowded > 0):
                    for t, name in ((w1, "w1_0"), (w2, "w2_0"), (wih, "wih_0"), (whh, "whh_0")):
                        sp.dma_start(t[:, :, :], A[name].rearrange("(k p) n -> p k n", p=128)).then_inc(w_in, 16)
                    for t, name in ((b1, "L0_gnn_b1_t"), (bih, "L0_gnn_b_ih_t"), (bhh, "L0_gnn_b_hh_t")):
                        sp.dma_start(t[:, :], A[name]).then_inc(w_in, 16)
                    sp.dma_start(b2_bc[:, :], A["L0_gnn_b2"].rearrange("(o n) -> o n", o=1).broadcast_to((RT, D))).then_inc(w_in, 16)
                    with sp.Fori(0, STEPS) as s:
                        with sp.Fori(0, NG) as g:
                            sp.wait_ge(h_done, START + (s * NG + g) * GT + GT)
                            sp.dma_start(h_dram[bass.ds(g * GC, GC), :].rearrange("(j p) d -> p j d", p=RT),
                                         h_rows[:, :, :]).then_inc(h_stored, 16)
                            wait_alone(sp, h_stored, (s * NG + g) * 16 + 16, passed)

            @block.gpsimd
            def _(pool):
                crowded = pool.value_load(crowded_t[0:1, 0:1], min_val=0, max_val=1)
                with pool.If(crowded > 0):
                    rounds, reg = begin(pool, "pool")
                    with pool.Fori(0, STEPS) as s:
                        wait_alone(pool, z_mm, s * NG * KD, passed)
                        nc.gpsimd.memset(msg[:, :, :], 0.0).then_inc(acc_zero, 1)
                        wait_alone(pool, h_stored, s * NG * 16 + NG * 16, passed)
                        with pool.Fori(0, rounds) as r:
                            with pool.Fori(0, NIT) as i:
                                its = count(pool, reg)
                                for b in range(2):
                                    wait_alone(pool, summed[b], its + i, passed)
                                    nc.gpsimd.tensor_copy(idx[:, b, :], src_t[:, bass.ds(i * ITC + b * UC, UC)])\
                                      .then_inc(idx_ready[b], 1)
                                    wait_alone(pool, idx_ready[b], its + i + 1, passed)
                                    for j in range(UC):
                                        nc.gpsimd.indirect_dma_start(
                                            out=rows[b * UC + j][:, :], out_offset=None, in_=h_dram,
                                            in_offset=bass.IndirectOffsetOnAxis(ap=idx[:, b, j:j + 1], axis=0),
                                        ).then_inc(gathered[b * UC + j], 16)
                            pool.reg_add(reg, reg, NIT)

            @block.tensor
            def _(pe):
                crowded = pe.value_load(crowded_t[0:1, 0:1], min_val=0, max_val=1)
                with pe.If(crowded > 0):
                    rounds, reg = begin(pe, "pe")
                    pe.wait_ge(w_in, START + 16 * 8)
                    with pe.Fori(0, STEPS) as s:
                        wait_alone(pe, nf_done, s * NG, passed)
                        with pe.Fori(0, NG) as g:
                            q = s * NG + g
                            cols = bass.ds(g * GC, GC)
                            for f in range(KD):
                                pe.wait_ge(t1_done, START + q * KD)
                                for k in range(KD):
                                    ins = nc.tensor.matmul(p_t1[f][:, 0:GC], w1[:, k, f * 128:(f + 1) * 128], nf[:, k, cols],
                                                           start=(k == 0), stop=(k == KD - 1))
                                ins.then_inc(t1_mm, 1)
                            pe.wait_ge(t1_done, START + q * KD + KD)
                            pe.wait_ge(h_done, START + q * GT)
                            for j in range(GT):
                                for k in range(KD):
                                    ins = nc.tensor.matmul(p_h[j][0:RT, 0:D],
                                                           t1[:, k, j * RT:(j + 1) * RT], w2[:, k, :],
                                                           start=(k == 0), stop=(k == KD - 1))
                                ins.then_inc(h_mm, 1)
                        with pe.Fori(0, rounds) as r:
                            with pe.Fori(0, NIT) as i:
                                its = count(pe, reg)
                                for b in range(2):
                                    pe.wait_ge(hot_ready[b], START + its + i + 1)
                                    pe.wait_ge(added, START + (its + i) * 2)
                                    for j in range(UC):
                                        pe.wait_ge(gathered[b * UC + j], (its + i) * 16 + 16)
                                        for k in range(KD):
                                            ins = nc.tensor.matmul(p_sum[b][:, k * W:(k + 1) * W],
                                                                   rows[b * UC + j][:, k * 128:(k + 1) * 128],
                                                                   hot[:, b, j, :], start=(j == 0 and k == 0), stop=(j == UC - 1),
                                                                   skip_group_check=True)
                                    ins.then_inc(summed[b], 1)
                            pe.reg_add(reg, reg, NIT)
                        wait_alone(pe, added, count(pe, reg) * 2, passed)
                        with pe.Fori(0, NG) as g:
                            cols = bass.ds(g * GC, GC)
                            for f in range(KD):
                                q = (s * NG + g) * KD + f

                                def gate(out_p, n, parts):
                                    ws = [(w, src, k) for w, src in parts for k in range(KD)]
                                    for m, (w, src, k) in enumerate(ws):
                                        ins = nc.tensor.matmul(out_p[:, 0:GC], w[:, k, n * D + f * 128:n * D + (f + 1) * 128],
                                                               src[:, k, cols], start=(m == 0), stop=(m == len(ws) - 1))
                                    return ins
                                pe.wait_ge(r_done, START + q)
                                gate(p_r, 0, ((wih, msg), (whh, nf))).then_inc(r_mm, 1)
                                pe.wait_ge(hn_used, START + q)
                                gate(p_hn, 2, ((whh, nf),)).then_inc(hn_mm, 1)
                                pe.wait_ge(t_done, START + q)
                                gate(p_xn, 2, ((wih, msg),)).then_inc(xn_mm, 1)
                                pe.wait_ge(z_done, START + q)
                                gate(p_z, 1, ((wih, msg), (whh, nf))).then_inc(z_mm, 1)

            @block.vector
            def _(dve):
                crowded = dve.value_load(crowded_t[0:1, 0:1], min_val=0, max_val=1)
                with dve.If(crowded > 0):
                    rounds, reg = begin(dve, "dve")
                    tabs = dve.alloc_register("g_tabs")
                    dve.reg_mov(tabs, 0)
                    dve.wait_ge(w_in, START + 16 * 8)
                    nc.vector.tensor_tensor(bsum[:, :], bih[:, :], bhh[:, :], ALU.add).then_inc(bias_done, 1)
                    with dve.Fori(0, STEPS) as s:
                        nc.vector.tensor_copy(rel[:, :], rel0[:, :]).then_inc(tab, 1)
                        nc.vector.tensor_copy(base[:, :], base_row[:, :]).then_inc(tab, 1)
                        dve.reg_add(tabs, tabs, 2)
                        with dve.Fori(0, NG) as g:
                            q = s * NG + g
                            dve.wait_ge(h_stored, START + q * 16)
                            for j in range(GT):
                                dve.wait_ge(h_mm, START + q * GT + j + 1)
                                nc.vector.tensor_tensor(h_rows[:, j, :], p_h[j][0:RT, 0:D],
                                                        b2_bc[:, :], ALU.add).then_inc(h_done, 1)
                        wait_alone(dve, acc_zero, s + 1, passed)
                        with dve.Fori(0, rounds) as r:
                            wait_alone(dve, tab, dve.snap(tabs, min_val=0, max_val=1 << 20), passed)
                            with dve.Fori(0, NIT) as i:
                                its = count(dve, reg)
                                for b in range(2):
                                    dve.wait_ge(summed[b], START + its + i)
                                    nc.vector.tensor_tensor(
                                        hot[:, b, :, :],
                                        iota_w[:, :].rearrange("p (o w) -> p o w", o=1).broadcast_to((EC, UC, W)),
                                        rel[:, bass.ds(i * ITC + b * UC, UC)].rearrange("p (c o) -> p c o", o=1)
                                        .broadcast_to((EC, UC, W)), ALU.is_equal).then_inc(hot_ready[b], 1)
                                for b in range(2):
                                    at = dve.value_load(base[0:1, bass.ds(i * 2 + b, 1)], min_val=0, max_val=NP)
                                    dve.wait_ge(summed[b], START + its + i + 1)
                                    dve.wait_ge(added, START + (its + i) * 2 + b)
                                    win = msg[:, :, bass.ds(at, W)]
                                    nc.vector.tensor_tensor(win, win, p_sum[b][:, 0:KD * W].rearrange("p (k w) -> p k w", k=KD),
                                                            ALU.add).then_inc(added, 1)
                            dve.reg_add(reg, reg, NIT)
                            nc.vector.tensor_scalar(rel[:, :], rel[:, :], float(W), None, ALU.subtract).then_inc(tab, 1)
                            nc.vector.tensor_scalar(base[:, :], base[:, :], float(W), float(NP), ALU.add, ALU.min)\
                              .then_inc(tab, 1)
                            dve.reg_add(tabs, tabs, 2)
                        with dve.Fori(0, NG) as g:
                            cols = bass.ds(g * GC, GC)
                            for f in range(KD):
                                q = (s * NG + g) * KD + f
                                dve.wait_ge(hn_mm, START + q + 1)
                                dve.wait_ge(r_done, START + q + 1)
                                nc.vector.scalar_tensor_tensor(out=t_t[:, f, :], in0=p_hn[:, 0:GC],
                                                               scalar=bhh[:, 2 * KD + f:2 * KD + f + 1], in1=r_t[:, f, :],
                                                               op0=ALU.add, op1=ALU.mult).then_inc(hn_used, 1)
                                dve.wait_ge(hn_used, START + q + 1)
                                dve.wait_ge(xn_mm, START + q + 1)
                                nc.vector.tensor_tensor(t_t[:, f, :], t_t[:, f, :], p_xn[:, 0:GC], ALU.add).then_inc(t_done, 1)
                            q = s * NG + g
                            dve.wait_ge(n_done, START + q * KD + KD)
                            dve.wait_ge(z_done, START + q * KD + KD)
                            nc.vector.tensor_tensor(d_t[:, :, :], nf[:, :, cols], n_t[:, :, :], ALU.subtract).then_inc(blend, 1)
                            dve.wait_ge(blend, START + q * 2 + 1)
                            nc.vector.tensor_tensor(d_t[:, :, :], d_t[:, :, :], z_t[:, :, :], ALU.mult).then_inc(blend, 1)
                            dve.wait_ge(blend, START + q * 2 + 2)
                            nc.vector.tensor_tensor(nf[:, :, cols], d_t[:, :, :], n_t[:, :, :], ALU.add).then_inc(nf_done, 1)

            @block.scalar
            def _(act):
                crowded = act.value_load(crowded_t[0:1, 0:1], min_val=0, max_val=1)
                with act.If(crowded > 0):
                    act.wait_ge(w_in, START + 16 * 8)
                    act.wait_ge(bias_done, START + 1)
                    with act.Fori(0, STEPS) as s:
                        with act.Fori(0, NG) as g:
                            q = s * NG + g
                            act.wait_ge(h_mm, START + q * GT)
                            for f in range(KD):
                                act.wait_ge(t1_mm, START + q * KD + f + 1)
                                nc.scalar.activation(t1[:, f, :], p_t1[f][:, 0:GC], ACT.Relu, bias=b1[:, f:f + 1], scale=1.0)\
                                  .then_inc(t1_done, 1)
                        with act.Fori(0, NG) as g:
                            for f in range(KD):
                                q = (s * NG + g) * KD + f
                                act.wait_ge(r_mm, START + q + 1)
                                act.wait_ge(hn_used, START + q)
                                nc.scalar.activation(r_t[:, f, :], p_r[:, 0:GC], ACT.Sigmoid, bias=bsum[:, f:f + 1], scale=1.0)\
                                  .then_inc(r_done, 1)
                                act.wait_ge(t_done, START + q + 1)
                                act.wait_ge(nf_done, START + s * NG + g)
                                nc.scalar.activation(n_t[:, f, :], t_t[:, f, :], ACT.Tanh,
                                                     bias=bih[:, 2 * KD + f:2 * KD + f + 1], scale=1.0).then_inc(n_done, 1)
                                act.wait_ge(z_mm, START + q + 1)
                                nc.scalar.activation(z_t[:, f, :], p_z[:, 0:GC], ACT.Sigmoid, bias=bsum[:, KD + f:KD + f + 1],
                                                     scale=1.0).then_inc(z_done, 1)


def add_transposed(nc, tag, sems, bank, sb, ident, x_rows, a_t):
    staged, turned, added = sems(*(f"{tag}_{s}" for s in ("staged", "turned", "added")))
    with ExitStack() as ctx:
        s_t = sb(ctx, "s_t", [128, KD, GC])
        with nc.Block() as block:
            @block.gpsimd
            def _(pool):
                with pool.Fori(0, NG) as g:
                    pool.wait_ge(turned, START + g * GT)
                    nc.gpsimd.tensor_copy(s_t[:, :, :], a_t[:, :, bass.ds(g * GC, GC)]).then_inc(staged, 1)

            @block.tensor
            def _(pe):
                with pe.Fori(0, NG) as g:
                    pe.wait_ge(staged, START + g + 1)
                    pe.wait_ge(added, START + g * GT)
                    for j in range(GT):
                        for k in range(KD):
                            ins = nc.tensor.transpose(bank[j][0:RT, k * 128:(k + 1) * 128], s_t[:, k, j * RT:(j + 1) * RT],
                                                      ident[:, :])
                        ins.then_inc(turned, 1)

            @block.vector
            def _(dve):
                with dve.Fori(0, NG) as g:
                    for j in range(GT):
                        dve.wait_ge(turned, START + g * GT + j + 1)
                        row = x_rows[:, bass.ds(g * GT + j, 1), :].rearrange("p a d -> p (a d)")
                        nc.vector.tensor_tensor(row, row, bank[j][0:RT, 0:D], ALU.add).then_inc(added, 1)


def route(nc, tag, A, sems, sb, bank, xt, gates, hidden, count, w_names, b_names):
    (w_in, hid_mm, hid_done, lg_mm, lg_done, step, ex_done, staged, top_done, gate_done) = sems(*(f"{tag}_{s}" for s in (
        "w_in hid_mm hid lg_mm lg step exp staged top gate").split()))
    nw = len(w_names) + len(b_names)
    with ExitStack() as ctx:
        w1 = sb(ctx, "rw1", [128, KD, 128 if hidden else 8])
        w2 = sb(ctx, "rw2", [128, 8])
        b1 = sb(ctx, "rb1", [128, 1])
        b2 = sb(ctx, "rb2", [RT, 8])
        rh = sb(ctx, "rh", [128, KD, GC])
        lg = sb(ctx, "lg", [RT, NT, 8])
        pr = sb(ctx, "pr", [RT, NT, 8])
        mx = sb(ctx, "mx", [RT, NT])
        best = sb(ctx, "best", [RT, NT, 8])
        at = sb(ctx, "at", [RT, NT, 8], U32)
        at_f = sb(ctx, "at_f", [RT, NT, 8])
        iota_i = sb(ctx, "iota8i", [RT, 8], I32)
        iota_f = sb(ctx, "iota8", [RT, 8])
        wt = sb(ctx, "wt", [RT, NT, 2])
        one = sb(ctx, "one", [RT, NT, 8])
        with nc.Block() as block:
            @block.sync
            def _(sp):
                sp.wait_ge(step, START + 1)
                sp.dma_start(w1[:, :, :], A[w_names[0]].rearrange("(k p) n -> p k n", p=128)).then_inc(w_in, 16)
                if hidden:
                    sp.dma_start(w2[:, :], A[w_names[1]]).then_inc(w_in, 16)
                    sp.dma_start(b1[:, :], A[b_names[0]].rearrange("(p o) -> p o", o=1)).then_inc(w_in, 16)
                    sp.dma_start(b2[:, 0:count], A[b_names[1]].rearrange("(o n) -> o n", o=1).broadcast_to((RT, count)))\
                      .then_inc(w_in, 16)

            @block.gpsimd
            def _(pool):
                nc.gpsimd.iota(iota_i[:, :], pattern=[[1, 8]], base=0, channel_multiplier=0).then_inc(staged, 1)
                if not hidden:
                    with pool.Fori(0, NG) as g:
                        pool.wait_ge(lg_mm, START + g)
                        nc.gpsimd.tensor_copy(rh[:, :, :], xt[:, :, bass.ds(g * GC, GC)]).then_inc(hid_done, 1)

            @block.tensor
            def _(pe):
                pe.wait_ge(w_in, START + 16 * nw)
                with pe.Fori(0, NG) as g:
                    if hidden:
                        pe.wait_ge(hid_done, START + g)
                        for k in range(KD):
                            ins = nc.tensor.matmul(bank[0][:, 0:GC], w1[:, k, :], xt[:, k, bass.ds(g * GC, GC)],
                                                   start=(k == 0), stop=(k == KD - 1))
                        ins.then_inc(hid_mm, 1)
                    pe.wait_ge(hid_done, START + g + 1)
                    pe.wait_ge(lg_done, START + g)
                    for j in range(GT):
                        for k in range(1 if hidden else KD):
                            ins = nc.tensor.matmul(bank[1][0:RT, j * 8:j * 8 + 8], rh[:, k, j * RT:(j + 1) * RT],
                                                   w2[:, :] if hidden else w1[:, k, :],
                                                   start=(k == 0), stop=(hidden or k == KD - 1))
                    ins.then_inc(lg_mm, 1)

            @block.scalar
            def _(act):
                if hidden:
                    act.wait_ge(w_in, START + 16 * nw)
                    with act.Fori(0, NG) as g:
                        act.wait_ge(hid_mm, START + g + 1)
                        act.wait_ge(lg_mm, START + g)
                        nc.scalar.activation(rh[:, 0, :], bank[0][:, 0:GC], ACT.Relu, bias=b1[:, :], scale=1.0)\
                          .then_inc(hid_done, 1)
                act.wait_ge(step, START + 3)
                nc.scalar.activation(pr[:, :, :], lg[:, :, :], ACT.Exp).then_inc(ex_done, 1)
                if hidden:
                    act.wait_ge(step, START + 6)
                    nc.scalar.activation(wt[:, :, 1], mx[:, :], ACT.Exp).then_inc(ex_done, 1)

            @block.vector
            def _(dve):
                n = [0]

                def then(ins):
                    n[0] += 1
                    ins.then_inc(step, 1)
                    dve.wait_ge(step, START + n[0])

                def per_node(a):
                    return a.rearrange("p (t o) -> p t o", o=1).broadcast_to((RT, NT, 8))
                then(nc.vector.memset(b2[:, :], NEG if count < 8 else 0.0))
                if hidden:
                    dve.wait_ge(w_in, START + 16 * nw)
                with dve.Fori(0, NG) as g:
                    dve.wait_ge(lg_mm, START + g + 1)
                    nc.vector.tensor_tensor(lg[:, bass.ds(g * GT, GT), :],
                                            bank[1][0:RT, 0:GT * 8].rearrange("p (j e) -> p j e", j=GT),
                                            b2[:, :].rearrange("p (o e) -> p o e", o=1).broadcast_to((RT, GT, 8)),
                                            ALU.add).then_inc(lg_done, 1)
                dve.wait_ge(lg_done, START + NG)
                then(nc.vector.tensor_reduce(mx[:, :], lg[:, :, :], AX, ALU.max))
                then(nc.vector.tensor_tensor(lg[:, :, :], lg[:, :, :], per_node(mx[:, :]), ALU.subtract))
                dve.wait_ge(ex_done, START + 1)
                then(nc.vector.tensor_reduce(mx[:, :], pr[:, :, :], AX, ALU.add))
                then(nc.vector.reciprocal(mx[:, :], mx[:, :]))
                nc.vector.tensor_tensor(pr[:, :, :], pr[:, :, :], per_node(mx[:, :]), ALU.mult).then_inc(top_done, 1)
                dve.wait_ge(top_done, START + 1)
                for t in range(NT):
                    nc.vector.max(best[:, t, :], pr[:, t, :]).then_inc(top_done, 1)
                dve.wait_ge(top_done, START + NT + 1)
                for t in range(NT):
                    nc.vector.max_index(at[:, t, :], best[:, t, :], pr[:, t, :]).then_inc(top_done, 1)
                if hidden:
                    then(nc.vector.tensor_tensor(mx[:, :], best[:, :, 1], best[:, :, 0], ALU.subtract))
                    dve.wait_ge(ex_done, START + 2)
                    then(nc.vector.tensor_scalar(mx[:, :], wt[:, :, 1], 1.0, None, ALU.add))
                    then(nc.vector.reciprocal(wt[:, :, 0], mx[:, :]))
                    then(nc.vector.tensor_tensor(wt[:, :, 1], wt[:, :, 1], wt[:, :, 0], ALU.mult))
                else:
                    then(nc.vector.tensor_tensor(mx[:, :], best[:, :, 1], best[:, :, 0], ALU.add))
                    then(nc.vector.tensor_scalar(mx[:, :], mx[:, :], 1e-9, None, ALU.add))
                    then(nc.vector.reciprocal(mx[:, :], mx[:, :]))
                    nc.vector.tensor_tensor(wt[:, :, 0], best[:, :, 0], mx[:, :], ALU.mult)
                    then(nc.vector.tensor_tensor(wt[:, :, 1], best[:, :, 1], mx[:, :], ALU.mult))
                dve.wait_ge(top_done, START + 2 * NT + 1)
                dve.wait_ge(staged, START + 1)
                nc.vector.tensor_copy(iota_f[:, :], iota_i[:, :])
                then(nc.vector.tensor_copy(at_f[:, :, :], at[:, :, :]))
                every = iota_f[:, :].rearrange("p (o e) -> p o e", o=1).broadcast_to((RT, NT, 8))
                for c, to in ((0, gates), (1, one)):
                    then(nc.vector.tensor_tensor(to[:, :, :], every, at_f[:, :, c:c + 1].broadcast_to((RT, NT, 8)), ALU.is_equal))
                    then(nc.vector.tensor_tensor(to[:, :, :], to[:, :, :], wt[:, :, c:c + 1].broadcast_to((RT, NT, 8)), ALU.mult))
                nc.vector.tensor_tensor(gates[:, :, :], gates[:, :, :], one[:, :, :], ALU.add)


def expert_mlp(nc, A, sems, sb, bank, xt, x_rows):
    w_in, ones_done, h1_mm, h1_done, h2_mm, h2_done, y_mm, y_done = sems(*("e0_" + s for s in (
        "w_in ones h1_mm h1 h2_mm h2 y_mm y").split()))
    with ExitStack() as ctx:
        gates = sb(ctx, "gates", [RT, NT, 8])
        route(nc, "r0", A, sems, sb, bank, xt, gates, True, E0, ("L0_ffn_router_w1", "rw2_0"),
              ("L0_ffn_router_b1", "L0_ffn_router_b2"))
        w = [sb(ctx, f"ew{i}", [128, E0, KD, D]) for i in range(3)]
        b1 = sb(ctx, "eb1", [128, E0, KD])
        b2 = sb(ctx, "eb2", [128, E0, KD])
        b3 = sb(ctx, "eb3", [1, E0, D])
        ones = sb(ctx, "ones", [1, RT])
        h1 = sb(ctx, "h1", [128, 2, KD, GC])
        h2 = sb(ctx, "h2", [128, 2, KD, GC])
        with nc.Block() as block:
            @block.sync
            def _(sp):
                for t, name in zip(w, ("L0_ffn_expert_w1", "L0_ffn_expert_w2", "L0_ffn_expert_w3")):
                    for e in range(E0):
                        sp.dma_start(t[:, e, :, :], A[name][e].rearrange("(k p) n -> p k n", p=128)).then_inc(w_in, 16)
                for t, name in ((b1, "L0_ffn_expert_b1_t"), (b2, "L0_ffn_expert_b2_t")):
                    sp.dma_start(t[:, :, :], A[name]).then_inc(w_in, 16)
                sp.dma_start(b3[:, :, :], A["L0_ffn_expert_b3"].rearrange("(o e) n -> o e n", o=1)).then_inc(w_in, 16)
            NW = 16 * (3 * E0 + 3)

            @block.tensor
            def _(pe):
                pe.wait_ge(w_in, START + NW)
                pe.wait_ge(ones_done, START + 1)
                with pe.Fori(0, NG) as g:
                    cols = bass.ds(g * GC, GC)

                    def layer1(e):
                        pe.wait_ge(h1_done, START + (g * E0 + e) * KD)
                        for f in range(KD):
                            for k in range(KD):
                                ins = nc.tensor.matmul(bank[f][:, 0:GC], w[0][:, e, k, f * 128:(f + 1) * 128], xt[:, k, cols],
                                                       start=(k == 0), stop=(k == KD - 1))
                            ins.then_inc(h1_mm, 1)

                    def layer2(e):
                        pe.wait_ge(h1_done, START + (g * E0 + e) * KD + KD)
                        pe.wait_ge(h2_done, START + (g * E0 + e) * KD)
                        for f in range(KD):
                            for k in range(KD):
                                ins = nc.tensor.matmul(bank[2 + f][:, 0:GC], w[1][:, e, k, f * 128:(f + 1) * 128],
                                                       h1[:, e % 2, k, :], start=(k == 0), stop=(k == KD - 1))
                            ins.then_inc(h2_mm, 1)

                    def layer3(e):
                        pe.wait_ge(h2_done, START + (g * E0 + e) * KD + KD)
                        pe.wait_ge(y_done, START + (g * E0 + e) * GT)
                        for j in range(GT):
                            o = bank[4 + j][0:RT, 0:D]
                            for k in range(KD):
                                nc.tensor.matmul(o, h2[:, e % 2, k, j * RT:(j + 1) * RT], w[2][:, e, k, :],
                                                 start=(k == 0), stop=False)
                            nc.tensor.matmul(o, ones[:, :], b3[:, e, :], start=False, stop=True).then_inc(y_mm, 1)
                    layer1(0)
                    for e in range(E0):
                        layer2(e)
                        if e + 1 < E0:
                            layer1(e + 1)
                        layer3(e)

            @block.scalar
            def _(act):
                act.wait_ge(w_in, START + NW)
                with act.Fori(0, NG) as g:
                    def relu(e, mm, b, bias, to, done):
                        for f in range(KD):
                            act.wait_ge(mm, START + (g * E0 + e) * KD + f + 1)
                            nc.scalar.activation(to[:, e % 2, f, :], b[f][:, 0:GC], ACT.Relu, bias=bias[:, e, f:f + 1],
                                                 scale=1.0).then_inc(done, 1)
                    relu(0, h1_mm, bank[0:2], b1, h1, h1_done)
                    for e in range(E0):
                        relu(e, h2_mm, bank[2:4], b2, h2, h2_done)
                        if e + 1 < E0:
                            relu(e + 1, h1_mm, bank[0:2], b1, h1, h1_done)

            @block.vector
            def _(dve):
                nc.vector.memset(ones[:, :], 1.0).then_inc(ones_done, 1)
                with dve.Fori(0, NG) as g:
                    for e in range(E0):
                        for j in range(GT):
                            n = (g * E0 + e) * GT + j
                            t = g * GT + j
                            dve.wait_ge(y_mm, START + n + 1)
                            if e:
                                dve.wait_ge(y_done, START + n - GT + 1)
                            row = x_rows[:, bass.ds(t, 1), :].rearrange("p a d -> p (a d)")
                            nc.vector.scalar_tensor_tensor(
                                out=row, in0=bank[4 + j][0:RT, 0:D],
                                scalar=gates[:, bass.ds(t, 1), e:e + 1].rearrange("p a b -> p (a b)"),
                                in1=row, op0=ALU.mult, op1=ALU.add).then_inc(y_done, 1)


def galerkin_and_nodes(nc, A, sems, sb, bank, xt, wcomb, h_dram):
    (w_in, const_done, wc_done, staged, k_mm, v_mm, h_mm, k_done, sq_done, var_done, std_done, r_done, rr_done,
     v_done, h_done, h_stored, d_mm, dots_mm, bd_done, m_mm, m_done, c_mm, c_done) = sems(*("m_" + s for s in (
         "w_in const wc staged k_mm v_mm h_mm k sq var std r rr v h h_stored d_mm dots_mm bd m_mm m c_mm c").split()))
    KI = INNER // 128
    with ExitStack() as ctx:
        wkv = sb(ctx, "wkv1", [128, KD, 2 * INNER])
        mean = sb(ctx, "mean", [128, KD, 2 * HEADS1])
        wq_t = sb(ctx, "wq_t", [128, KI, D])
        wout = sb(ctx, "wout", [128, KI, D])
        wlin = sb(ctx, "wlin", [128, KD, 128])
        z = sb(ctx, "z", [RT, NT])
        z8 = sb(ctx, "z8", [RT, NT])
        zeros = sb(ctx, "zeros", [1, 512])
        stage = sb(ctx, "stage", [128, KD, GC])
        kc = sb(ctx, "kc", [RT, 2, INNER])
        sq = sb(ctx, "sq", [RT, 2, 2 * INNER])
        var = sb(ctx, "var", [RT, 2, 2 * HEADS1])
        rr = sb(ctx, "rr", [RT, 2, HEADS1])
        vs = sb(ctx, "vs", [RT, 2, INNER])
        h_rows = sb(ctx, "h_rows", [RT, GT, D])
        dots = sb(ctx, "dots", [128, KI, 128])
        m_s = sb(ctx, "m_s", [128, KI, D])
        eps_t = sb(ctx, "eps", [RT, 1])
        acc = bank[6]
        NW = 16 * 5

        def last(j, f):
            return f

        with nc.Block() as block:
            @block.sync
            def _(sp):
                sp.dma_start(wkv[:, :, :], A["wkv1"].rearrange("(k p) n -> p k n", p=128)).then_inc(w_in, 16)
                sp.dma_start(wq_t[:, :, :], A["wq1_t"].rearrange("(k p) n -> p k n", p=128)).then_inc(w_in, 16)
                sp.dma_start(wout[:, :, :], A["L1_mix_w_out"].rearrange("(k p) n -> p k n", p=128)).then_inc(w_in, 16)
                sp.dma_start(wlin[:, :, :], A["wlin"].rearrange("(k p) n -> p k n", p=128)).then_inc(w_in, 16)
                sp.dma_start(z[:, :], A["z_rows"]).then_inc(w_in, 16)
                with sp.Fori(0, NG) as g:
                    sp.wait_ge(h_done, START + g * GT + GT)
                    sp.dma_start(h_dram[bass.ds(g * GC, GC), :].rearrange("(j p) d -> p j d", p=RT),
                                 h_rows[:, :, :]).then_inc(h_stored, 16)
                sp.wait_ge(h_stored, START + NG * 16)

            @block.gpsimd
            def _(pool):
                nc.gpsimd.memset(zeros[:, :], 0.0).then_inc(const_done, 1)
                nc.gpsimd.memset(dots[:, :, :], 0.0).then_inc(const_done, 1)
                nc.gpsimd.memset(eps_t[:, :], EPS).then_inc(const_done, 1)
                nc.gpsimd.memset(xt[:, :, N:NP], 0.0).then_inc(const_done, 1)
                pool.wait_ge(const_done, START + 4)
                with pool.Fori(0, NG) as g:
                    pool.wait_ge(h_mm, START + g * GT)
                    nc.gpsimd.tensor_copy(stage[:, :, :], xt[:, :, bass.ds(g * GC, GC)]).then_inc(staged, 1)

            @block.tensor
            def _(pe):
                pe.wait_ge(w_in, START + NW)
                pe.wait_ge(const_done, START + 4)
                pe.wait_ge(wc_done, START + 3)
                nc.tensor.matmul(acc[:, :], zeros[:, 0:128], zeros[:, :], start=True, stop=False, skip_group_check=True)
                with pe.Fori(0, NG) as g:
                    pe.wait_ge(staged, START + g + 1)

                    def maps(j):
                        n = g * GT + j
                        b = 3 * (j % 2)
                        rows = slice(j * RT, (j + 1) * RT)
                        pe.wait_ge(sq_done, START + (n if j > 1 else g * GT))
                        pe.wait_ge(v_done, START + (n - 1 if j > 1 else g * GT))
                        pe.wait_ge(h_done, START + (n - 1 if j > 1 else g * GT))
                        for k in range(KD):
                            ins = nc.tensor.matmul(bank[b][0:RT, :], stage[:, k, rows], wkv[:, k, 0:INNER],
                                                   start=(k == 0), stop=(k == KD - 1))
                        ins.then_inc(k_mm, 1)
                        for k in range(KD):
                            ins = nc.tensor.matmul(bank[b + 1][0:RT, :], stage[:, k, rows], wkv[:, k, INNER:],
                                                   start=(k == 0), stop=(k == KD - 1))
                        ins.then_inc(v_mm, 1)
                        for k in range(KD):
                            ins = nc.tensor.matmul(bank[b + 2][0:RT, k * 128:(k + 1) * 128], stage[:, k, rows], wlin[:, k, :],
                                                   start=True, stop=True)
                        ins.then_inc(h_mm, 1)

                    def sums(j):
                        n = g * GT + j
                        pe.wait_ge(k_done, START + n + 1)
                        pe.wait_ge(v_done, START + n + 1)
                        for f in range(KI):
                            s = slice(f * 128, (f + 1) * 128)
                            ins = nc.tensor.matmul(acc[:, s], vs[:, j % 2, s], kc[:, j % 2, s], start=False, stop=False,
                                                   skip_group_check=True)
                        ins.then_inc(d_mm, 1)
                    maps(0)
                    for j in range(GT):
                        if j + 1 < GT:
                            maps(j + 1)
                        sums(j)
                nc.tensor.matmul(acc[:, :], zeros[:, 0:128], zeros[:, :], start=False, stop=True,
                                 skip_group_check=True).then_inc(dots_mm, 1)
                pe.wait_ge(bd_done, START + 1)
                for f in range(KI):
                    ins = nc.tensor.matmul(bank[f][:, 0:D], dots[:, f, :], wout[:, f, :], start=True, stop=True)
                ins.then_inc(m_mm, 1)
                pe.wait_ge(m_done, START + 1)
                for c in range(KD):
                    for f in range(KI):
                        ins = nc.tensor.matmul(bank[4 + c][:, 0:D], wq_t[:, f, c * 128:(c + 1) * 128], m_s[:, f, :],
                                               start=(f == 0), stop=(f == KI - 1))
                ins.then_inc(c_mm, 1)

            @block.scalar
            def _(act):
                act.wait_ge(w_in, START + NW)
                act.wait_ge(const_done, START + 4)
                nc.scalar.activation(z8[:, :], z[:, :], ACT.Copy, scale=MUL ** -0.5).then_inc(c_done, 1)
                act.wait_ge(c_done, START + 1)
                with act.Fori(0, NG) as g:
                    def squares(j):
                        n = g * GT + j
                        b = 3 * (j % 2)
                        act.wait_ge(k_mm, START + n + 1)
                        act.wait_ge(d_mm, START + (n - 1 if j > 1 else g * GT))
                        act.wait_ge(var_done, START + (n - 1 if j > 1 else g * GT))
                        nc.scalar.activation(kc[:, j % 2, :], bank[b][0:RT, :], ACT.Copy).then_inc(k_done, 1)
                        nc.scalar.activation(sq[:, j % 2, 0:INNER], bank[b][0:RT, :], ACT.Square)
                        act.wait_ge(v_mm, START + n + 1)
                        nc.scalar.activation(sq[:, j % 2, INNER:], bank[b + 1][0:RT, :], ACT.Square).then_inc(sq_done, 1)
                        act.wait_ge(h_mm, START + n + 1)
                        act.wait_ge(h_stored, START + g * 16)
                        nc.scalar.activation(h_rows[:, j, :], bank[b + 2][0:RT, 0:D], ACT.Copy,
                                             scale=z8[:, bass.ds(n, 1)]).then_inc(h_done, 1)

                    def deviation(j):
                        n = g * GT + j
                        act.wait_ge(var_done, START + n + 1)
                        nc.scalar.activation(var[:, j % 2, :], var[:, j % 2, :], ACT.Sqrt, bias=eps_t[:, :], scale=1.0 / DH1)\
                          .then_inc(std_done, 1)
                    squares(0)
                    for j in range(GT):
                        if j + 1 < GT:
                            squares(j + 1)
                        deviation(j)

            @block.vector
            def _(dve):
                dve.wait_ge(w_in, START + NW)
                heads = wkv[:, :, :].rearrange("p k (h d) -> p (k h) d", d=DH1)
                means = mean[:, :, :].rearrange("p k h -> p (k h)")
                nc.vector.tensor_reduce(means, heads, AX, ALU.add).then_inc(wc_done, 1)
                dve.wait_ge(wc_done, START + 1)
                nc.vector.tensor_scalar(means, means, 1.0 / DH1, None, ALU.mult).then_inc(wc_done, 1)
                dve.wait_ge(wc_done, START + 2)
                nc.vector.tensor_tensor(heads, heads, means.rearrange("p (h o) -> p h o", o=1)
                                        .broadcast_to((128, KD * 2 * HEADS1, DH1)), ALU.subtract).then_inc(wc_done, 1)
                with dve.Fori(0, NG) as g:
                    def variance(j):
                        n = g * GT + j
                        dve.wait_ge(sq_done, START + n + 1)
                        dve.wait_ge(rr_done, START + (n - 1 if j > 1 else g * GT))
                        nc.vector.tensor_reduce(var[:, j % 2, :], sq[:, j % 2, :].rearrange("p (h d) -> p h d", d=DH1),
                                                AX, ALU.add).then_inc(var_done, 1)

                    def scaled(j):
                        n = g * GT + j
                        b = 3 * (j % 2)
                        dve.wait_ge(std_done, START + n + 1)
                        nc.vector.reciprocal(var[:, j % 2, :], var[:, j % 2, :]).then_inc(r_done, 1)
                        dve.wait_ge(r_done, START + n + 1)
                        dve.wait_ge(d_mm, START + (n - 1 if j > 1 else g * GT))
                        nc.vector.tensor_tensor(rr[:, j % 2, :], var[:, j % 2, 0:HEADS1], var[:, j % 2, HEADS1:],
                                                ALU.mult).then_inc(rr_done, 1)
                        dve.wait_ge(rr_done, START + n + 1)
                        nc.vector.tensor_tensor(
                            vs[:, j % 2, :].rearrange("p (h d) -> p h d", d=DH1),
                            bank[b + 1][0:RT, :].rearrange("p (h d) -> p h d", d=DH1),
                            rr[:, j % 2, :].rearrange("p (h o) -> p h o", o=1).broadcast_to((RT, HEADS1, DH1)),
                            ALU.mult).then_inc(v_done, 1)
                    variance(0)
                    for j in range(GT):
                        if j + 1 < GT:
                            variance(j + 1)
                        scaled(j)
                dve.wait_ge(dots_mm, START + 1)
                dve.wait_ge(const_done, START + 4)
                for f in range(KI):
                    for h in range(128 // DH1):
                        s = slice(h * DH1, (h + 1) * DH1)
                        ins = nc.vector.tensor_scalar(dots[s, f, s], acc[s, f * 128 + h * DH1:f * 128 + (h + 1) * DH1],
                                                      1.0 / N, None, ALU.mult)
                ins.then_inc(bd_done, 1)
                dve.wait_ge(m_mm, START + 1)
                for f in range(KI):
                    ins = nc.vector.tensor_copy(m_s[:, f, :], bank[f][:, 0:D])
                ins.then_inc(m_done, 1)
                dve.wait_ge(c_mm, START + 1)
                for c in range(KD):
                    nc.vector.tensor_copy(wcomb[:, c, :], bank[4 + c][:, 0:D])


def edge_convolution(nc, A, sems, sb, bank, tables, ident, xt, wcomb, x_rows, h_dram):
    src_t, rel0, base_row, rounds_t, iota_w = tables
    (w_in, scaled, acc_zero, tab, ea_in_a, ea_in_b, hid_mm, hid_done, w_mm, eq_done, hot_done, p_done, sum_mm, sum_copied, turned, added, idx_ready,
     staged, u_mm, mix_mm, t_done, b_done, x_done, passed, *gathered) = sems(*("c_" + s for s in (
         "w_in scaled acc_zero tab ea_in_a ea_in_b hid_mm hid w_mm eq hot prod sum_mm sum_copied turned added idx "
         "staged u_mm mix_mm t b x passed").split()),
                                  *(f"c_gathered{j}" for j in range(ITC)))
    ea_in = (ea_in_a, ea_in_b)
    c_s, c_x = float(np.float32(np.sin(np.pi / 8.0))), float(np.float32(np.cos(np.pi / 8.0)))
    SC = c_s * MUL ** -0.5
    LIN = c_x * 64 ** -0.5 * 16.0 ** -0.5 * (2 * MUL) ** -0.5
    NB = 4
    with ExitStack() as ctx:
        acc = sb(ctx, "acc", [128, NB, NW_COLS])
        rel = sb(ctx, "rel", [EC, NCH])
        base = sb(ctx, "base", [1, NU], I32)
        idx = sb(ctx, "idx", [EC, 2, UC], I32)
        rows = [sb(ctx, f"rows{j}", [EC, D]) for j in range(ITC)]
        ea4 = sb(ctx, "ea4", [EC, NCH, 4])
        ea8 = sb(ctx, "ea8", [8, 2, UE])
        fw0 = sb(ctx, "fw0", [8, 64])
        fw1 = sb(ctx, "fw1", [64, 4 * MUL])
        hid = sb(ctx, "hid", [64, 2, UE])
        eq = sb(ctx, "eq", [EC, 2, UC, W])
        hot = sb(ctx, "hot", [EC, 2, UC, 4, W])
        prod = sb(ctx, "prod", [EC, 2, UC, 8 * MUL])
        sum_rows = sb(ctx, "sum_rows", [W, 2, 8 * MUL])
        wsc = sb(ctx, "wsc", [128, KD, D])
        wl2 = sb(ctx, "wl2", [128, 4, 128])
        z = sb(ctx, "z", [RT, NT])
        bout = sb(ctx, "bout", [RT, D])
        stage = sb(ctx, "stage", [128, NB, GC])
        stage_x = sb(ctx, "stage_x", [128, KD, GC])
        t_rows = sb(ctx, "t_rows", [RT, GT, D])
        p_hid, p_t, p_w, p_sum = bank[0], bank[1], bank[2:6], bank[6:8]
        NW = 16 * 7

        def begin(eng, tag):
            rounds = eng.value_load(rounds_t[0:1, 0:1], min_val=1, max_val=MAXROUNDS)
            reg = eng.alloc_register(f"c_its_{tag}")
            eng.reg_mov(reg, 0)
            return rounds, reg

        def count(eng, reg):
            return eng.snap(reg, min_val=0, max_val=NIT * MAXROUNDS)

        with nc.Block() as block:
            @block.sync
            def _(sp):
                for t, name in ((fw0, "L1_gnn_fc_w0"), (fw1, "fw1"), (ea4, "ea4"), (z, "z_rows")):
                    sp.dma_start(t[:], A[name]).then_inc(w_in, 16)
                sp.dma_start(wsc[:, :, :], A["wsc"].rearrange("(k p) n -> p k n", p=128)).then_inc(w_in, 16)
                sp.dma_start(wl2[:, :, :], A["wl2"].rearrange("(k p) n -> p k n", p=128)).then_inc(w_in, 16)
                sp.dma_start(bout[:, :], A["L1_mix_b_out"].rearrange("(o n) -> o n", o=1).broadcast_to((RT, D))).then_inc(w_in, 16)
                rounds, reg = begin(sp, "sp")
                with sp.Fori(0, rounds) as r:
                    with sp.Fori(0, NIT) as i:
                        its = count(sp, reg)
                        for b in range(2):
                            sp.wait_ge(hid_mm, START + (its + i) * 2 + b - 1)
                            sp.dma_start(ea8[:, b, :], A["ea8"][:, bass.ds((i * 2 + b) * UE, UE)]).then_inc(ea_in[b], 16)
                    sp.reg_add(reg, reg, NIT)

            @block.gpsimd
            def _(pool):
                rounds, reg = begin(pool, "pool")
                nc.gpsimd.memset(acc[:, :, :], 0.0).then_inc(acc_zero, 1)
                with pool.Fori(0, rounds) as r:
                    with pool.Fori(0, NIT) as i:
                        its = count(pool, reg)
                        for b in range(2):
                            wait_alone(pool, p_done, ((its + i) * 2 + b) * UC - UC, passed)
                            nc.gpsimd.tensor_copy(idx[:, b, :], src_t[:, bass.ds(i * ITC + b * UC, UC)])\
                              .then_inc(idx_ready, 1)
                            wait_alone(pool, idx_ready, (its + i) * 2 + b + 1, passed)
                            for j in range(UC):
                                nc.gpsimd.indirect_dma_start(
                                    out=rows[b * UC + j][:, :], out_offset=None, in_=h_dram,
                                    in_offset=bass.IndirectOffsetOnAxis(ap=idx[:, b, j:j + 1], axis=0),
                                ).then_inc(gathered[b * UC + j], 16)
                    pool.reg_add(reg, reg, NIT)
                with pool.Fori(0, NG) as g:
                    cols = bass.ds(g * GC, GC)
                    pool.wait_ge(added, START + count(pool, reg) * 2)
                    pool.wait_ge(mix_mm, START + g * GT)
                    nc.gpsimd.tensor_copy(stage[:, :, :], acc[:, :, cols]).then_inc(staged, 1)
                    nc.gpsimd.tensor_copy(stage_x[:, :, :], xt[:, :, cols]).then_inc(staged, 1)

            @block.tensor
            def _(pe):
                rounds, reg = begin(pe, "pe")
                pe.wait_ge(w_in, START + NW)
                def hidden(q, b):
                    pe.wait_ge(ea_in[b], START + (q - b) * 8 + 16)
                    pe.wait_ge(hid_done, START + q)
                    nc.tensor.matmul(p_hid[0:64, 0:UE], fw0[:, :], ea8[:, b, :], start=True, stop=True)\
                      .then_inc(hid_mm, 1)

                def weights(q, b):
                    pe.wait_ge(hid_done, START + q + 1)
                    for j in range(UC):
                        pe.wait_ge(p_done, START + q * UC + j + 1 - UC)
                        nc.tensor.matmul(p_w[j][0:EC, 0:4 * MUL], hid[:, b, j * EC:(j + 1) * EC], fw1[:, :],
                                         start=True, stop=True).then_inc(w_mm, 1)

                def sums(q, b):
                    pe.wait_ge(sum_copied, START + q - 1)
                    to = p_sum[b][0:W, :].rearrange("p (s u) -> p s u", u=MUL)
                    for j in range(UC):
                        pe.wait_ge(hot_done, START + q * UC + j + 1)
                        pe.wait_ge(p_done, START + q * UC + j + 1)
                        p = prod[:, b, j, :].rearrange("p (s u) -> p s u", u=MUL)
                        nc.tensor.matmul(to[:, 0:4, :], hot[:, b, j, 0, :], p[:, 0:4, :], start=(j == 0), stop=False,
                                         skip_group_check=True)
                        for c in range(3):
                            ins = nc.tensor.matmul(to[:, 4 + c:8:3 - c, :], hot[:, b, j, 1 + c, :], p[:, 4:6 + c:1 + c, :],
                                                   start=False, stop=(j == UC - 1 and c == 2), skip_group_check=True)
                        ins.then_inc(sum_mm, 1)

                def turn(q, b):
                    pe.wait_ge(sum_copied, START + q + 1)
                    pe.wait_ge(added, START + q)
                    for m in range(NB):
                        ins = nc.tensor.transpose(p_t[:, m * W:(m + 1) * W], sum_rows[:, b, m * 128:(m + 1) * 128],
                                                  ident[0:W, 0:W])
                    ins.then_inc(turned, 1)

                def step(q, b, ahead=2, behind=True):
                    if ahead > 0:
                        weights(q + 1, 1 - b)
                    if ahead > 1:
                        hidden(q + 2, b)
                    if behind:
                        turn(q - 1, 1 - b)
                    sums(q, b)
                with pe.Fori(0, rounds) as r:
                    first = count(pe, reg) * 2
                    hidden(first, 0)
                    weights(first, 0)
                    hidden(first + 1, 1)
                    step(first, 0, behind=False)
                    with pe.Fori(0, NIT - 2) as i:
                        for b in range(2):
                            step(first + i * 2 + b + 1, 1 - b)
                    step(first + NU - 3, 1)
                    step(first + NU - 2, 0, ahead=1)
                    step(first + NU - 1, 1, ahead=0)
                    turn(first + NU - 1, 1)
                    pe.reg_add(reg, reg, NIT)
                pe.wait_ge(scaled, START + 3)
                with pe.Fori(0, NG) as g:
                    pe.wait_ge(staged, START + g * 2 + 2)
                    for j in range(GT):
                        n = g * GT + j
                        rows_j = slice(j * RT, (j + 1) * RT)
                        u, m = bank[2 * (j % 2)], bank[2 * (j % 2) + 1]
                        pe.wait_ge(x_done, START + (n - 1 if j > 1 else g * GT))
                        for k in range(KD):
                            nc.tensor.matmul(u[0:RT, 0:D], stage_x[:, k, rows_j], wsc[:, k, :], start=(k == 0), stop=False,
                                             skip_group_check=True)
                        for q in range(NB):
                            at, w = MUL * (0, 2, 1, 0)[q], wl2[:, q, :]
                            to = u[0:RT, at:at + 2 * MUL]
                            if q == NB - 1:
                                to = u[0:RT, :].rearrange("p (s u) -> p s u", u=MUL)[:, 0:4:3, :]
                                w = w.rearrange("p (a b) -> p a b", a=2)
                            ins = nc.tensor.matmul(to, stage[:, q, rows_j], w, start=False, stop=(q == NB - 1),
                                                   skip_group_check=True)
                        ins.then_inc(u_mm, 1)
                        for k in range(KD):
                            ins = nc.tensor.matmul(m[0:RT, 0:D], stage_x[:, k, rows_j], wcomb[:, k, :],
                                                   start=(k == 0), stop=(k == KD - 1))
                        ins.then_inc(mix_mm, 1)

            @block.scalar
            def _(act):
                rounds, reg = begin(act, "act")
                act.wait_ge(w_in, START + NW)
                nc.scalar.activation(wsc[:, :, :], wsc[:, :, :], ACT.Copy, scale=SC).then_inc(scaled, 1)
                nc.scalar.activation(wl2[:, 0:3, :], wl2[:, 0:3, :], ACT.Copy, scale=LIN).then_inc(scaled, 1)
                nc.scalar.activation(wl2[0:MUL, 3, :], wl2[0:MUL, 3, :], ACT.Copy, scale=LIN)
                nc.scalar.activation(wl2[MUL:, 3, :], wl2[MUL:, 3, :], ACT.Copy, scale=LIN * 3.0 ** -0.5).then_inc(scaled, 1)

                def silu(q, b):
                    act.wait_ge(hid_mm, START + q + 1)
                    act.wait_ge(w_mm, START + q * UC - UC)
                    nc.scalar.activation(hid[:, b, :], p_hid[0:64, 0:UE], ACT.Silu, scale=8.0 ** -0.5)\
                      .then_inc(hid_done, 1)

                def weighted_hots(q, b, u):
                    act.wait_ge(eq_done, START + q + 1)
                    for j in range(UC):
                        act.wait_ge(sum_mm, START + q * UC + j + 1 - ITC)
                        for m in range(4):
                            ins = nc.scalar.activation(hot[:, b, j, m, :], eq[:, b, j, :], ACT.Copy,
                                                       scale=ea4[:, bass.ds(u * UC + j, 1), m:m + 1].rearrange("p a b -> p (a b)"))
                        ins.then_inc(hot_done, 1)
                def copy(q, b):
                    act.wait_ge(sum_mm, START + q * UC + UC)
                    act.wait_ge(turned, START + q - 1)
                    nc.scalar.activation(sum_rows[:, b, :], p_sum[b][0:W, :], ACT.Copy).then_inc(sum_copied, 1)

                def step(q, b, u, ahead=2):
                    if ahead > 1:
                        silu(q + 2, b)
                    if ahead > 0:
                        weighted_hots(q + 1, 1 - b, u + 1)
                    copy(q, b)
                with act.Fori(0, rounds) as r:
                    first = count(act, reg) * 2
                    silu(first, 0)
                    weighted_hots(first, 0, 0)
                    silu(first + 1, 1)
                    step(first, 0, 0)
                    with act.Fori(0, NIT - 2) as i:
                        for b in range(2):
                            step(first + i * 2 + b + 1, 1 - b, i * 2 + b + 1)
                    step(first + NU - 3, 1, NU - 3)
                    step(first + NU - 2, 0, NU - 2, ahead=1)
                    step(first + NU - 1, 1, NU - 1, ahead=0)
                    act.reg_add(reg, reg, NIT)

            @block.vector
            def _(dve):
                rounds, reg = begin(dve, "dve")
                tabs = dve.alloc_register("c_tabs")
                dve.reg_mov(tabs, 2)
                dve.wait_ge(w_in, START + NW)
                nc.vector.tensor_copy(rel[:, :], rel0[:, :]).then_inc(tab, 1)
                nc.vector.tensor_copy(base[:, :], base_row[:, :]).then_inc(tab, 1)
                dve.wait_ge(acc_zero, START + 1)

                def one_hots(q, b, u):
                    dve.wait_ge(hot_done, START + q * UC - UC)
                    nc.vector.tensor_tensor(
                        eq[:, b, :, :],
                        iota_w[:, :].rearrange("p (o w) -> p o w", o=1).broadcast_to((EC, UC, W)),
                        rel[:, bass.ds(u * UC, UC)].rearrange("p (c o) -> p c o", o=1).broadcast_to((EC, UC, W)),
                        ALU.is_equal).then_inc(eq_done, 1)

                def products(q, b):
                    dve.wait_ge(sum_mm, START + q * UC - UC)
                    for j in range(UC):
                        dve.wait_ge(gathered[b * UC + j], (q - b) * 8 + 16)
                        dve.wait_ge(w_mm, START + q * UC + j + 1)
                        x, p, w = rows[b * UC + j], prod[:, b, j, :], p_w[j][0:EC, :]
                        two, three = (EC, 2, MUL), (EC, 3, MUL)
                        xs0 = x[:, 0:MUL].rearrange("p (o u) -> p o u", o=1).broadcast_to(two)
                        xs1 = x[:, MUL:D].rearrange("p (c u) -> p c u", c=3)
                        w_c = w[:, 2 * MUL:3 * MUL].rearrange("p (o u) -> p o u", o=1).broadcast_to(three)
                        w_d = w[:, 3 * MUL:4 * MUL].rearrange("p (o u) -> p o u", o=1).broadcast_to(three)
                        slots = p.rearrange("p (s u) -> p s u", u=MUL)
                        nc.vector.tensor_tensor(slots[:, 0:5:4, :], xs0, w[:, 0:2 * MUL].rearrange("p (a u) -> p a u", a=2), ALU.mult)
                        nc.vector.tensor_tensor(slots[:, 1:4, :], xs1, w_c, ALU.mult)
                        nc.vector.tensor_tensor(slots[:, 5:8, :], xs1, w_d, ALU.mult).then_inc(p_done, 1)

                def add(q, u):
                    at = dve.value_load(base[0:1, bass.ds(u, 1)], min_val=0, max_val=NP)
                    dve.wait_ge(turned, START + q + 1)
                    dve.wait_ge(added, START + q)
                    win = acc[:, :, bass.ds(at, W)]
                    nc.vector.tensor_tensor(win, win, p_t[:, 0:NB * W].rearrange("p (k w) -> p k w", k=NB),
                                            ALU.add).then_inc(added, 1)
                with dve.Fori(0, rounds) as r:
                    wait_alone(dve, tab, dve.snap(tabs, min_val=0, max_val=1 << 20), passed)
                    first = count(dve, reg) * 2
                    one_hots(first, 0, 0)
                    products(first, 0)
                    one_hots(first + 1, 1, 1)
                    products(first + 1, 1)
                    with dve.Fori(0, NIT - 1) as i:
                        for b in range(2):
                            q, u = first + i * 2 + b, i * 2 + b
                            one_hots(q + 2, b, u + 2)
                            products(q + 2, b)
                            add(q, u)
                    add(first + NU - 2, NU - 2)
                    add(first + NU - 1, NU - 1)
                    dve.reg_add(reg, reg, NIT)
                    nc.vector.tensor_scalar(rel[:, :], rel[:, :], float(W), None, ALU.subtract).then_inc(tab, 1)
                    nc.vector.tensor_scalar(base[:, :], base[:, :], float(W), float(NP), ALU.add, ALU.min).then_inc(tab, 1)
                    dve.reg_add(tabs, tabs, 2)
                with dve.Fori(0, NG) as g:
                    for j in range(GT):
                        n = g * GT + j
                        u, m = bank[2 * (j % 2)], bank[2 * (j % 2) + 1]
                        row = x_rows[:, bass.ds(n, 1), :].rearrange("p a d -> p (a d)")
                        zt = z[:, bass.ds(n, 1)]
                        dve.wait_ge(mix_mm, START + n + 1)
                        nc.vector.tensor_tensor(t_rows[:, j, :], m[0:RT, 0:D], bout[:, :], ALU.add).then_inc(t_done, 1)
                        dve.wait_ge(t_done, START + n + 1)
                        nc.vector.tensor_tensor(t_rows[:, j, :], t_rows[:, j, :], row, ALU.add).then_inc(b_done, 1)
                        dve.wait_ge(b_done, START + n + 1)
                        dve.wait_ge(u_mm, START + n + 1)
                        nc.vector.scalar_tensor_tensor(out=row[:, 0:MUL], in0=u[0:RT, 0:MUL], scalar=zt, in1=t_rows[:, j, 0:MUL],
                                                       op0=ALU.mult, op1=ALU.add)
                        nc.vector.scalar_tensor_tensor(out=row[:, MUL:D].rearrange("p (u c) -> p u c", c=3),
                                                       in0=u[0:RT, MUL:D].rearrange("p (c u) -> p u c", c=3), scalar=zt,
                                                       in1=t_rows[:, j, MUL:D].rearrange("p (u c) -> p u c", c=3),
                                                       op0=ALU.mult, op1=ALU.add).then_inc(x_done, 1)


def expert_swiglu(nc, A, sems, sb, bank, xt, x_rows):
    h1_mm, h3_mm, s_done, g_done, y_part, y_mm, y_done, passed, *w_in = sems(*("e1_" + s for s in (
        "h1_mm h3_mm s g y_part y_mm y passed w_a w_b").split()))
    NH = len(HCH)
    with ExitStack() as ctx:
        gates = sb(ctx, "gates", [RT, NT, 8])
        route(nc, "r1", A, sems, sb, bank, xt, gates, False, E1, ("rw1",), ())
        w13 = [sb(ctx, f"w13_{b}", [128, 2, KD, HID1]) for b in range(2)]
        w2 = [sb(ctx, f"w2_{b}", [128, NH, D]) for b in range(2)]
        s_t = sb(ctx, "s_t", [128, 2, GC])
        h_t = sb(ctx, "h_t", [128, 2, GC])
        FULL = HID1 // 128
        REST = HID1 - FULL * 128
        with nc.Block() as block:
            @block.sync
            def _(sp):
                with sp.Fori(0, E1 // 2) as p:
                    for b in range(2):
                        e = p * 2 + b
                        sp.wait_ge(y_mm, START + (e * NG * GT if b == 0 else p * (2 * NG * GT)))
                        if b == 1:
                            pass
                        for m, name in enumerate(("w1_1", "w3_1")):
                            sp.dma_start(w13[b][:, m, :, :], A[name][bass.ds(e, 1), :, :].rearrange("o (k p) n -> p (o k) n", p=128))\
                              .then_inc(w_in[b], 16)
                        sp.dma_start(w2[b][:, 0:FULL, :], A["w2_1"][bass.ds(e, 1), 0:FULL * 128, :]
                                     .rearrange("o (k p) n -> p (o k) n", p=128)).then_inc(w_in[b], 16)
                        sp.dma_start(w2[b][0:REST, FULL, :], A["w2_1"][bass.ds(e, 1), FULL * 128:HID1, :]
                                     .rearrange("o p n -> p (o n)")).then_inc(w_in[b], 16)

            @block.tensor
            def _(pe):
                with pe.Fori(0, E1 // 2) as p:
                    for b in range(2):
                        wait_alone(pe, w_in[b], p * 64 + 64, passed)
                        with pe.Fori(0, NG) as g:
                            q = (p * 2 + b) * NG + g
                            cols = bass.ds(g * GC, GC)

                            def up(h):
                                o, sz = HCH[h]
                                wait_alone(pe, g_done, q * NH + max(h - 1, 0), passed)
                                for m, done in ((0, h1_mm), (1, h3_mm)):
                                    for k in range(KD):
                                        ins = nc.tensor.matmul(bank[2 * (h % 2) + m][0:sz, 0:GC], w13[b][:, m, k, o:o + sz],
                                                               xt[:, k, cols], start=(k == 0), stop=(k == KD - 1))
                                    ins.then_inc(done, 1)

                            def down(h):
                                sz = HCH[h][1]
                                pe.wait_ge(g_done, START + q * NH + h + 1)
                                if h == 0:
                                    pe.wait_ge(y_done, START + q * GT)
                                for j in range(GT):
                                    ins = nc.tensor.matmul(bank[4 + j][0:RT, 0:D], h_t[0:sz, h % 2, j * RT:(j + 1) * RT],
                                                           w2[b][0:sz, h, :], start=(h == 0), stop=(h == NH - 1))
                                    if h == NH - 1:
                                        ins.then_inc(y_mm, 1)
                                if h < NH - 1:
                                    ins.then_inc(y_part, 1)
                            up(0)
                            for h in range(NH):
                                if h + 1 < NH:
                                    up(h + 1)
                                down(h)

            @block.scalar
            def _(act):
                with act.Fori(0, E1 * NG) as q:
                    for h, (o, sz) in enumerate(HCH):
                        act.wait_ge(h1_mm, START + q * NH + h + 1)
                        act.wait_ge(g_done, START + q * NH + max(h - 1, 0))
                        nc.scalar.activation(s_t[0:sz, h % 2, :], bank[2 * (h % 2)][0:sz, 0:GC], ACT.Silu).then_inc(s_done, 1)

            @block.vector
            def _(dve):
                with dve.Fori(0, E1) as e:
                    with dve.Fori(0, NG) as g:
                        q = e * NG + g
                        for h, (o, sz) in enumerate(HCH):
                            dve.wait_ge(s_done, START + q * NH + h + 1)
                            dve.wait_ge(h3_mm, START + q * NH + h + 1)
                            dve.wait_ge(y_part, START + q * (NH - 1) + max(h - 1, 0))
                            if h < 2:
                                dve.wait_ge(y_mm, START + q * GT)
                            nc.vector.tensor_tensor(h_t[0:sz, h % 2, :], s_t[0:sz, h % 2, :], bank[2 * (h % 2) + 1][0:sz, 0:GC],
                                                    ALU.mult).then_inc(g_done, 1)
                        for j in range(GT):
                            t = g * GT + j
                            dve.wait_ge(y_mm, START + q * GT + j + 1)
                            row = x_rows[:, bass.ds(t, 1), :].rearrange("p a d -> p (a d)")
                            nc.vector.scalar_tensor_tensor(
                                out=row, in0=bank[4 + j][0:RT, 0:D],
                                scalar=gates[:, bass.ds(t, 1), bass.ds(e, 1)].rearrange("p a b -> p (a b)"),
                                in1=row, op0=ALU.mult, op1=ALU.add).then_inc(y_done, 1)



def layouts(i):
    c = np.ascontiguousarray
    src, dst = np.asarray(i["src"]), np.asarray(i["dst"])
    x = np.zeros((NP, D), np.float32)
    x[:N] = i["x"]
    z = np.zeros((NP,), np.float32)
    z[:N] = np.asarray(i["node_vec1"])[:, 0]
    pad8 = np.zeros((128, 8), np.float32)
    pad8[:, :E0] = i["L0_ffn_router_w2"]
    vec = np.concatenate([np.arange(MUL)] + [MUL + 3 * np.arange(MUL) + k for k in range(3)])
    qkv = np.asarray(i["L1_mix_w_qkv"])[vec]
    none = np.zeros((128, 128), np.float32)
    swap = np.r_[MUL:2 * MUL, 0:MUL]
    l0, l1 = np.asarray(i["L1_gnn_W_lin2_0"]), np.asarray(i["L1_gnn_W_lin2_1"])

    def diag(p, q):
        m = np.zeros((2 * MUL, 2 * MUL), np.float32)
        m[:MUL, :MUL], m[MUL:, MUL:] = p, q
        return m

    a = {
        "x_rows": c(x.reshape(NT, RT, D).transpose(1, 0, 2)),
        "src_t": c(src.reshape(NCH, EC).T),
        "dst_t": c(dst.reshape(NCH, EC).T),
        "dst_c": c(dst.reshape(NU, UE)),
        "wkv0": c(np.concatenate([i["L0_mix_wk"], i["L0_mix_wv"]], axis=1)),
        "wq0": i["L0_mix_wq"], "wo0": i["L0_mix_wo"],
        "w1_0": c(np.asarray(i["L0_gnn_W1"]).T), "w2_0": c(np.asarray(i["L0_gnn_W2"]).T),
        "wih_0": c(np.asarray(i["L0_gnn_W_ih"]).T), "whh_0": c(np.asarray(i["L0_gnn_W_hh"]).T),
        "rw2_0": pad8,
        "z_rows": c(z.reshape(NT, RT).T),
        "ea4": c(np.asarray(i["edge_attr_4"]).reshape(NCH, EC, 4).transpose(1, 0, 2)),
        "ea8": c(np.asarray(i["edge_attr_8"]).T),
        "wlin": np.concatenate([diag(i["L1_gnn_W_lin1_0"], i["L1_gnn_W_lin1_1"]),
                                diag(i["L1_gnn_W_lin1_1"], i["L1_gnn_W_lin1_1"])]),
        "wsc": np.concatenate([np.concatenate([diag(i["L1_gnn_W_sc0"], i["L1_gnn_W_sc1"]), none], axis=1),
                               np.concatenate([none, diag(i["L1_gnn_W_sc1"], i["L1_gnn_W_sc1"])], axis=1)]),
        "wl2": np.concatenate([diag(l0[:MUL], l1[MUL:]), diag(l1[MUL:], l1[MUL:]),
                               diag(l1[:MUL], l1[:MUL]), diag(l1[:MUL], l0[MUL:])[:, swap]]),
        "fw1": np.asarray(i["L1_gnn_fc_w1"]),
        "wkv1": c(qkv[:, INNER:]), "wq1_t": c(qkv[:, :INNER].T),
        "rw1": c(np.asarray(i["L1_ffn_router_w"]).T),
        "w1_1": c(np.asarray(i["L1_ffn_w1"]).transpose(0, 2, 1)),
        "w3_1": c(np.asarray(i["L1_ffn_w3"]).transpose(0, 2, 1)),
        "w2_1": c(np.asarray(i["L1_ffn_w2"]).transpose(0, 2, 1)),
    }
    for name in ("L0_mix_bq", "L0_mix_bo", "L0_gnn_b1", "L0_gnn_b_ih", "L0_gnn_b_hh"):
        a[name + "_t"] = np.asarray(i[name]).reshape(-1, 128).T
    for name in ("L0_ffn_expert_b1", "L0_ffn_expert_b2"):
        a[name + "_t"] = np.asarray(i[name]).reshape(E0, KD, 128).transpose(2, 0, 1)
    for name in ("L0_mix_bk", "L0_mix_bv", "L0_gnn_b2",
                 "L0_ffn_router_w1", "L0_ffn_router_b1", "L0_ffn_router_b2", "L0_ffn_expert_w1", "L0_ffn_expert_w2",
                 "L0_ffn_expert_w3", "L0_ffn_expert_b3",
                 "L1_gnn_fc_w0", "L1_mix_w_out", "L1_mix_b_out"):
        a[name] = i[name]
    return {k: np.ascontiguousarray(v) for k, v in a.items()}


def kernel(**inputs):
    import concourse.bacc as _bacc
    from concourse.bass_utils import run_bass_kernel_spmd as _run

    nc = _bacc.Bacc("TRN2", target_bir_lowering=False, num_devices=1)
    arrays = {f"in_{k}": v for k, v in layouts(inputs).items()}
    args = {k[3:]: nc.dram_tensor(k, v.shape, mybir.dt.from_np(v.dtype), kind="ExternalInput").ap()
            for k, v in arrays.items()}
    out = nc.dram_tensor("out_0", (N, D), F32, kind="ExternalOutput").ap()
    build(nc, args, out)
    r = _run(nc, [arrays], core_ids=[0])
    return r.results[0]["out_0"]
```

```python
from contextlib import ExitStack

import numpy as np

import concourse.bass as bass
from concourse import mybir

F32 = mybir.dt.float32
F32R = mybir.dt.float32r
BF16 = mybir.dt.bfloat16
I16 = mybir.dt.int16
I32 = mybir.dt.int32
U32 = mybir.dt.uint32
ALU = mybir.AluOpType
ACT = mybir.ActivationFunctionType
AX = mybir.AxisListType.X

N, D = 3125, 256
RT, NT = 100, 32
GT, NG = 4, 8
GC = RT * GT
NP = RT * NT
LASTROWS = N - RT * (NT - 1)
KD = D // 128
EC, NCH = 125, 400
UC = 4
NU = NCH // UC
ITC = 2 * UC
NIT = NU // 2
UE = UC * EC
W = 80
MAXROUNDS = -(-N // W)
NW_COLS = NP + W
PC = 2
NPAIR = NCH // PC
KT = NP // 128
KB = 5
HB = 5
HN = NP // (KT // HB)
PARTS = 2
EXACT = 256
STEPS = 6
EPS = 1e-5
HEADS0, DH0 = 8, 32
HEADS1, DH1 = 8, 64
INNER = HEADS1 * DH1
E0, E1, HID1 = 6, 8, 682
HCH = [(k * 128, min(128, HID1 - k * 128)) for k in range((HID1 + 127) // 128)]
TOP = 2
NBLK = (NP * TOP + E1 * 127) // 128
NBLK += NBLK % 2
MUL = 64
NEG = -1e30
START = 16


def wait_alone(eng, sem, value, passed):
    eng.wait_ge(sem, START + value)
    eng.sem_inc(passed, 1)


def build(nc, A, out, debug=None):
    top = ExitStack()
    names = [0]

    held = []

    def sems(*wanted):
        got = [nc.alloc_semaphore(name=n) for n in wanted]
        engines = (nc.gpsimd, nc.sync, nc.scalar, nc.vector, nc.tensor)
        for n, (sem, name) in enumerate(zip(got, wanted)):
            if "gathered" not in name:
                engines[n % len(engines)].sem_inc(sem, START)
        nc.all_engine_barrier()
        held.extend(got)
        return got

    def phase(f, *args):
        f(nc, *args)
        if held:
            nc.clear_and_free_semaphores(held)
            held.clear()
            nc.all_engine_barrier()

    def sb(ctx, name, shape, dt=F32):
        names[0] += 1
        return ctx.enter_context(nc.sbuf_tensor(f"{name}_{names[0]}", shape, dt))

    with top:
        x_rows = sb(top, "x_rows", [RT, NT, D])
        ident = sb(top, "ident", [128, 128])
        iota_w = sb(top, "iota_w", [EC, W])
        src_t = sb(top, "src_t", [EC, NCH], I32)
        rel0 = sb(top, "rel0", [EC, NCH])
        base_row = sb(top, "base_row", [1, NU], I32)
        rounds_t = sb(top, "rounds_t", [1, 1], I32)
        eps_t = sb(top, "eps_t", [128, 1])
        crowded_t = sb(top, "crowded_t", [1, 1], I32)
        bank = [top.enter_context(nc.psum_tensor(f"bank{k}", [128, 512], F32)) for k in range(8)]
        h_dram = nc.dram_tensor("h_dram", (NP, D), F32).ap()
        base_dram = nc.dram_tensor("base_dram", (NU,), F32).ap()
        span_dram = nc.dram_tensor("span_dram", (NU,), F32).ap()

        a_dram = nc.dram_tensor("a_dram", (NG, 128, KT, GC), BF16).ap()
        pair_dram = [nc.dram_tensor(f"pair_{e}_dram", (NPAIR,), F32).ap() for e in ("lo", "hi")]
        range_dram = nc.dram_tensor("range_dram", (NT, 2), I32).ap()

        x_slots, y_slots = (nc.dram_tensor(f"{e}_slots", (NBLK * 128, D), F32).ap() for e in "xy")

        phase(setup, A, sems, sb, x_rows, ident, iota_w, src_t, rel0, base_row, rounds_t, eps_t,
              base_dram, span_dram)
        tables = (src_t, rel0, base_row, rounds_t, iota_w)

        with ExitStack() as ctx:
            nf = sb(ctx, "nf", [128, KD, NP])
            phase(norm_transpose, "n0", sems, sb, x_rows, ident, eps_t, bank, nf, False)
            with ExitStack() as ctx_mix:
                mix = sb(ctx_mix, "mix", [128, KD, NP])
                phase(linear_attention, A, sems, sb, bank, nf, mix)
                phase(add_transposed, "mix", sems, bank, sb, ident, x_rows, mix)
            phase(adjacency, A, sems, sb, bank, src_t, a_dram, pair_dram, range_dram, crowded_t, x_slots)
            phase(gated_graph, A, sems, sb, bank, nf, a_dram, crowded_t)
            phase(gated_graph_by_edges, A, sems, sb, bank, tables, nf, h_dram, crowded_t)
            phase(add_transposed, "gnn", sems, bank, sb, ident, x_rows, nf)
        if debug == "l0a":
            return store_rows(nc, sems, x_rows, out)
        with ExitStack() as ctx:
            xt = sb(ctx, "xt", [128, KD, NP])
            phase(norm_transpose, "n1", sems, sb, x_rows, ident, eps_t, bank, xt, False)
            phase(expert_mlp, A, sems, sb, bank, xt, x_rows)
        if debug == "l0":
            return store_rows(nc, sems, x_rows, out)

        with ExitStack() as ctx:
            xt = sb(ctx, "xt", [128, KD, NP])
            wcomb = sb(ctx, "wcomb", [128, KD, D])
            phase(norm_transpose, "n2", sems, sb, x_rows, ident, eps_t, bank, xt, True)
            phase(galerkin_and_nodes, A, sems, sb, bank, xt, wcomb, h_dram)
            phase(edge_convolution, A, sems, sb, bank, tables, ident, xt, wcomb, x_rows, h_dram)
        if debug == "l1a":
            return store_rows(nc, sems, x_rows, out)
        with ExitStack() as ctx:
            mean_var = sb(ctx, "mean_var", [RT, NT, 2])
            rstd = sb(ctx, "rstd", [RT, NT])
            picked = sb(ctx, "picked", [RT, NT, 8])
            weight = sb(ctx, "weight", [RT, NT, TOP])
            slot_i = sb(ctx, "slot_i", [RT, NT, TOP], I32)
            expert_i = sb(ctx, "expert_i", [1, NBLK], I32)
            with ExitStack() as ctx_xt:
                xt = sb(ctx_xt, "xt", [128, KD, NP])
                phase(norm_transpose, "n3", sems, sb, x_rows, ident, eps_t, bank, xt, False, (mean_var, rstd))
                phase(route, "r1", A, sems, sb, bank, xt, False, E1, ("rw1",), (), None, picked, weight)
            with ExitStack() as ctx_w:
                w13 = sb(ctx_w, "w13", [128, E1, 2, KD, HID1])
                w2 = sb(ctx_w, "w2", [128, E1, len(HCH), D])
                phase(dispatch, A, sems, sb, bank, x_rows, mean_var, rstd, picked, slot_i, expert_i, x_slots, w13, w2,
                      ("w1_1", "w3_1", "w2_1"))
                phase(expert_swiglu, sems, sb, bank, ident, expert_i, x_slots, y_slots, w13, w2)
            phase(combine, sems, sb, x_rows, slot_i, weight, y_slots)
        store_rows(nc, sems, x_rows, out)


def store_rows(nc, sems, x_rows, out):
    stored, = sems("out_stored")
    with nc.Block() as block:
        @block.sync
        def _(sp):
            sp.dma_start(out[0:RT * (NT - 1), :].rearrange("(t p) d -> p t d", p=RT),
                         x_rows[:, 0:NT - 1, :]).then_inc(stored, 16)
            sp.dma_start(out[RT * (NT - 1):N, :], x_rows[0:LASTROWS, NT - 1, :]).then_inc(stored, 16)
            sp.wait_ge(stored, START + 32)


def setup(nc, A, sems, sb, x_rows, ident, iota_w, src_t, rel0, base_row, rounds_t, eps_t,
          base_dram, span_dram):
    (x_in, edges_in, ident_zero, ident_done, iota_done, conv, mm_done, mm_stored, bc_loaded,
     tab) = sems("x_in", "edges_in", "ident_zero", "ident_done", "iota_done", "conv", "mm_done",
                 "mm_stored", "bc_loaded", "tab")
    with ExitStack() as ctx:
        dst_t = sb(ctx, "dst_t", [EC, NCH], I32)
        dst_f = sb(ctx, "dst_f", [EC, NCH])
        dst_c = sb(ctx, "dst_c", [NU, UE], I32)
        dst_cf = sb(ctx, "dst_cf", [NU, UE])
        lo = sb(ctx, "lo", [NU, 1])
        hi = sb(ctx, "hi", [NU, 1])
        span = sb(ctx, "span", [NU, 1])
        base_bc = sb(ctx, "base_bc", [EC, NU])
        span_row = sb(ctx, "span_row", [1, NU])
        widest = sb(ctx, "widest", [1, 1])
        starts_i = sb(ctx, "starts_i", [1, MAXROUNDS], I32)
        starts = sb(ctx, "starts", [1, MAXROUNDS])
        needed = sb(ctx, "needed", [1, MAXROUNDS])
        iota_i = sb(ctx, "iota_i", [EC, W], I32)
        with nc.Block() as block:
            @block.sync
            def _(sp):
                sp.dma_start(dst_t[:, :], A["dst_t"]).then_inc(edges_in, 16)
                sp.dma_start(dst_c[:, :], A["dst_c"]).then_inc(edges_in, 16)
                sp.dma_start(src_t[:, :], A["src_t"]).then_inc(edges_in, 16)
                sp.dma_start(x_rows[:, :, :], A["x_rows"]).then_inc(x_in, 16)
                sp.wait_ge(mm_done, START + 1)
                sp.dma_start(base_dram.rearrange("(p j) -> p j", j=1), lo[:, :]).then_inc(mm_stored, 16)
                sp.dma_start(span_dram.rearrange("(p j) -> p j", j=1), span[:, :]).then_inc(mm_stored, 16)
                sp.wait_ge(mm_stored, START + 32)
                sp.dma_start(base_bc[:, :], base_dram.rearrange("(o c) -> o c", o=1).broadcast_to((EC, NU)))\
                  .then_inc(bc_loaded, 16)
                sp.dma_start(span_row[:, :], span_dram.rearrange("(o c) -> o c", o=1)).then_inc(bc_loaded, 16)
                sp.wait_ge(x_in, START + 16)

            @block.gpsimd
            def _(pool):
                nc.gpsimd.memset(ident[:, :], 0.0).then_inc(ident_zero, 1)
                nc.gpsimd.iota(iota_i[:, :], pattern=[[1, W]], base=0, channel_multiplier=0).then_inc(iota_done, 1)
                nc.gpsimd.iota(starts_i[:, :], pattern=[[W, MAXROUNDS]], base=0, channel_multiplier=0).then_inc(iota_done, 1)
                pool.wait_ge(ident_zero, START + 1)
                nc.gpsimd.affine_select(out=ident[:, :], in_=ident[:, :], compare_op=ALU.not_equal, fill=1.0,
                                        base=0, pattern=[[-1, 128]], channel_multiplier=1).then_inc(ident_done, 1)

            @block.vector
            def _(dve):
                nc.vector.memset(eps_t[:, :], EPS)
                dve.wait_ge(iota_done, START + 2)
                nc.vector.tensor_copy(iota_w[:, :], iota_i[:, :])
                nc.vector.tensor_copy(starts[:, :], starts_i[:, :]).then_inc(conv, 1)
                dve.wait_ge(edges_in, START + 48)
                nc.vector.tensor_copy(dst_f[:, :], dst_t[:, :]).then_inc(conv, 1)
                nc.vector.tensor_copy(dst_cf[:, :], dst_c[:, :]).then_inc(conv, 1)
                dve.wait_ge(conv, START + 3)
                nc.vector.tensor_reduce(lo[:, :], dst_cf[:, :], AX, ALU.min).then_inc(conv, 1)
                nc.vector.tensor_reduce(hi[:, :], dst_cf[:, :], AX, ALU.max).then_inc(conv, 1)
                dve.wait_ge(conv, START + 5)
                nc.vector.tensor_tensor(span[:, :], hi[:, :], lo[:, :], ALU.subtract).then_inc(mm_done, 1)
                dve.wait_ge(bc_loaded, START + 32)
                unit_base = base_bc[:, :].rearrange("p (u o) -> p u o", o=1).broadcast_to((EC, NU, UC))
                nc.vector.tensor_tensor(rel0[:, :].rearrange("p (u c) -> p u c", c=UC),
                                        dst_f[:, :].rearrange("p (u c) -> p u c", c=UC), unit_base, ALU.subtract)
                nc.vector.tensor_copy(base_row[:, :], base_bc[0:1, :])
                nc.vector.tensor_reduce(widest[:, :], span_row[:, :], AX, ALU.max).then_inc(tab, 1)
                dve.wait_ge(tab, START + 1)
                nc.vector.tensor_scalar(needed[:, :], starts[:, :], widest[:, :], None, ALU.is_le).then_inc(tab, 1)
                dve.wait_ge(tab, START + 2)
                nc.vector.tensor_reduce(widest[:, :], needed[:, :], AX, ALU.add).then_inc(tab, 1)
                dve.wait_ge(tab, START + 3)
                nc.vector.tensor_copy(rounds_t[:, :], widest[:, :])


def norm_transpose(nc, tag, sems, sb, x_rows, ident, eps_t, bank, xt, by_vector, keep=None):
    stat_done, aggr_done, std_done, rstd_done, *tiles = sems(
        *(f"{tag}_{s}" for s in ("stat", "aggr", "std", "rstd")),
        *(f"{tag}_{s}{j}" for s in ("normed", "turned", "copied") for j in range(GT)))
    normed, turned, copied = tiles[:GT], tiles[GT:2 * GT], tiles[2 * GT:]
    with ExitStack() as ctx:
        stat = sb(ctx, "stat", [RT, NT, 6])
        std = sb(ctx, "std", [RT, NT])
        mv, rstd = keep or (sb(ctx, "mv", [RT, NT, 2]), sb(ctx, "rstd", [RT, NT]))
        xn = sb(ctx, "xn", [RT, GT, D])
        with nc.Block() as block:
            @block.vector
            def _(dve):
                with dve.Fori(0, NT) as t:
                    nc.vector.bn_stats(stat[:, bass.ds(t, 1), :], x_rows[:, bass.ds(t, 1), :]).then_inc(stat_done, 1)
                dve.wait_ge(stat_done, START + NT)
                for t in range(NT):
                    ins = nc.vector.bn_aggr(mv[:, t, :], stat[:, t, :])
                ins.then_inc(aggr_done, 1)
                dve.wait_ge(std_done, START + 1)
                nc.vector.reciprocal(rstd[:, :], std[:, :]).then_inc(rstd_done, 1)
                dve.wait_ge(rstd_done, START + 1)
                with dve.Fori(0, NG) as g:
                    for j in range(GT):
                        t = g * GT + j
                        dve.wait_ge(turned[j], START + g)
                        def norm(o, i):
                            return nc.vector.tensor_scalar(o, i, mv[:, bass.ds(t, 1), 0:1].rearrange("p a b -> p (a b)"),
                                                           rstd[:, bass.ds(t, 1)], ALU.subtract, ALU.mult)
                        row = x_rows[:, bass.ds(t, 1), :].rearrange("p a d -> p (a d)")
                        if by_vector:
                            norm(xn[:, j, 0:MUL], row[:, 0:MUL])
                            ins = norm(xn[:, j, MUL:D].rearrange("p (c u) -> p u c", c=3),
                                       row[:, MUL:D].rearrange("p (u c) -> p u c", c=3))
                        else:
                            ins = norm(xn[:, j, :], row)
                        ins.then_inc(normed[j], 1)

            @block.tensor
            def _(pe):
                with pe.Fori(0, NG) as g:
                    for j in range(GT):
                        pe.wait_ge(normed[j], START + g + 1)
                        pe.wait_ge(copied[j], START + g)
                        for k in range(KD):
                            ins = nc.tensor.transpose(bank[j][:, k * RT:(k + 1) * RT], xn[:, j, k * 128:(k + 1) * 128],
                                                      ident[0:RT, 0:RT])
                        ins.then_inc(turned[j], 1)

            @block.scalar
            def _(act):
                act.wait_ge(aggr_done, START + 1)
                nc.scalar.activation(std[:, :], mv[:, :, 1], ACT.Sqrt, bias=eps_t[0:RT, :], scale=1.0).then_inc(std_done, 1)
                with act.Fori(0, NG) as g:
                    for j in range(GT):
                        act.wait_ge(turned[j], START + g + 1)
                        nc.scalar.activation(xt[:, :, bass.ds(g * GC + j * RT, RT)],
                                             bank[j][:, 0:KD * RT].rearrange("p (k r) -> p k r", k=KD),
                                             ACT.Copy).then_inc(copied[j], 1)


def linear_attention(nc, A, sems, sb, bank, xt, mix):
    (w_in, mask_done, staged, kv_mm, kb_done, km_done, ke_done, kf_done, acc_mm, v_done, zero_mm,
     bd_done, q_mm, qm_done, qe_done, qr_done, qf_done, nd_mm, dn_done, rec_done, o_done, out_mm,
     mix_done) = sems(*("a0_" + s for s in (
         "w_in mask staged kv_mm kb km ke kf acc_mm v zero bd q_mm qm qe qr qf nd_mm dn rec o out_mm mix").split()))
    NH = 128 // DH0
    with ExitStack() as ctx:
        wkv = sb(ctx, "wkv", [128, KD, 2 * D])
        wq = sb(ctx, "wq", [128, KD, D])
        wo = sb(ctx, "wo", [128, KD, D])
        bk_bc = sb(ctx, "bk_bc", [RT, D])
        bv_bc = sb(ctx, "bv_bc", [RT, D])
        bq = sb(ctx, "bq", [128, KD])
        bo = sb(ctx, "bo", [128, KD])
        row_bias = sb(ctx, "row_bias", [RT, 2])
        stage = sb(ctx, "stage", [128, KD, GC])
        kb = sb(ctx, "kb", [RT, GT, D])
        km = sb(ctx, "km", [RT, GT, D])
        ke = sb(ctx, "ke", [RT, GT, D])
        vb = sb(ctx, "vb", [RT, GT, D])
        ones = sb(ctx, "ones", [RT, 128])
        zeros = sb(ctx, "zeros", [1, 512])
        kv_bd = sb(ctx, "kv_bd", [128, KD, 128])
        ks_bd = sb(ctx, "ks_bd", [128, KD, 128])
        qm = sb(ctx, "qm", [128, KD, GC])
        qr = sb(ctx, "qr", [128, KD, GC])
        dn = sb(ctx, "dn", [128, KD, GC])
        o_t = sb(ctx, "o_t", [128, KD, GC])
        acc = bank[4]
        with nc.Block() as block:
            @block.sync
            def _(sp):
                for t, name in ((wkv, "wkv0"), (wq, "wq0"), (wo, "wo0")):
                    sp.dma_start(t[:, :, :], A[name].rearrange("(k p) n -> p k n", p=128)).then_inc(w_in, 16)
                for t, name in ((bk_bc, "L0_mix_bk"), (bv_bc, "L0_mix_bv")):
                    sp.dma_start(t[:, :], A[name].rearrange("(o n) -> o n", o=1).broadcast_to((RT, D))).then_inc(w_in, 16)
                for t, name in ((bq, "L0_mix_bq_t"), (bo, "L0_mix_bo_t")):
                    sp.dma_start(t[:, :], A[name]).then_inc(w_in, 16)

            @block.gpsimd
            def _(pool):
                nc.gpsimd.memset(ones[:, :], 1.0).then_inc(mask_done, 1)
                nc.gpsimd.memset(zeros[:, :], 0.0).then_inc(mask_done, 1)
                nc.gpsimd.memset(row_bias[:, :], 0.0).then_inc(mask_done, 1)
                nc.gpsimd.memset(kv_bd[:, :, :], 0.0).then_inc(mask_done, 1)
                nc.gpsimd.memset(ks_bd[:, :, :], 0.0).then_inc(mask_done, 1)
                pool.wait_ge(mask_done, START + 5)
                nc.gpsimd.affine_select(out=row_bias[:, 1:2], in_=row_bias[:, 1:2], compare_op=ALU.is_ge, fill=NEG,
                                        base=LASTROWS - 1, pattern=[[0, 1]], channel_multiplier=-1).then_inc(mask_done, 1)
                with pool.Fori(0, NG) as g:
                    pool.wait_ge(kv_mm, START + g * GT)
                    nc.gpsimd.tensor_copy(stage[:, :, :], xt[:, :, bass.ds(g * GC, GC)]).then_inc(staged, 1)

            @block.tensor
            def _(pe):
                pe.wait_ge(w_in, START + 16 * 7)
                pe.wait_ge(mask_done, START + 6)
                nc.tensor.matmul(acc[:, :], zeros[:, 0:128], zeros[:, :], start=True, stop=False, skip_group_check=True)
                with pe.Fori(0, NG) as g:
                    pe.wait_ge(staged, START + g + 1)
                    for j in range(GT):
                        pe.wait_ge(v_done, START + g * GT)
                        for k in range(KD):
                            ins = nc.tensor.matmul(bank[j][0:RT, :], stage[:, k, j * RT:(j + 1) * RT], wkv[:, k, :],
                                                   start=(k == 0), stop=(k == KD - 1))
                        ins.then_inc(kv_mm, 1)
                    for j in range(GT):
                        pe.wait_ge(kf_done, START + g * GT + j + 1)
                        pe.wait_ge(v_done, START + g * GT + j + 1)
                        for k in range(KD):
                            f = slice(k * 128, (k + 1) * 128)
                            nc.tensor.matmul(acc[:, k * 256:k * 256 + 128], km[:, j, f], vb[:, j, f],
                                             start=False, stop=False, skip_group_check=True)
                            ins = nc.tensor.matmul(acc[:, k * 256 + 128:k * 256 + 256], km[:, j, f], ones[:, :],
                                                   start=False, stop=False, skip_group_check=True)
                        ins.then_inc(acc_mm, 1)
                nc.tensor.matmul(acc[:, :], zeros[:, 0:128], zeros[:, :], start=False, stop=True,
                                 skip_group_check=True).then_inc(zero_mm, 1)
                pe.wait_ge(bd_done, START + 1)
                with pe.Fori(0, NG) as g:
                    cols = bass.ds(g * GC, GC)
                    pe.wait_ge(qr_done, START + g * KD)
                    for f in range(KD):
                        for k in range(KD):
                            ins = nc.tensor.matmul(bank[f][:, 0:GC], wq[:, k, f * 128:(f + 1) * 128], xt[:, k, cols],
                                                   start=(k == 0), stop=(k == KD - 1))
                        ins.then_inc(q_mm, 1)
                    pe.wait_ge(o_done, START + g)
                    for f in range(KD):
                        pe.wait_ge(qf_done, START + g * KD + f + 1)
                        nc.tensor.matmul(bank[2 + f][:, 0:GC], kv_bd[:, f, :], qr[:, f, :], start=True, stop=True)
                        ins = nc.tensor.matmul(bank[5 + f][:, 0:GC], ks_bd[:, f, :], qr[:, f, :], start=True, stop=True)
                        ins.then_inc(nd_mm, 1)
                    pe.wait_ge(o_done, START + g + 1)
                    pe.wait_ge(mix_done, START + g * KD)
                    for f in range(KD):
                        b = (4, 7)[f]
                        for k in range(KD):
                            ins = nc.tensor.matmul(bank[b][:, 0:GC], wo[:, k, f * 128:(f + 1) * 128], o_t[:, k, :],
                                                   start=(k == 0), stop=(k == KD - 1))
                        ins.then_inc(out_mm, 1)

            @block.vector
            def _(dve):
                dve.wait_ge(w_in, START + 16 * 7)
                dve.wait_ge(mask_done, START + 6)

                def keys(g, last):
                    for j in range(GT):
                        n = g * GT + j
                        dve.wait_ge(kv_mm, START + n + 1)
                        dve.wait_ge(acc_mm, START + g * GT)
                        pad = 1 if last and j == GT - 1 else 0
                        nc.vector.scalar_tensor_tensor(out=kb[:, j, :], in0=bank[j][0:RT, 0:D],
                                                       scalar=row_bias[:, pad:pad + 1], in1=bk_bc[:, :],
                                                       op0=ALU.add, op1=ALU.add).then_inc(kb_done, 1)
                        nc.vector.tensor_tensor(vb[:, j, :], bank[j][0:RT, D:2 * D], bv_bc[:, :], ALU.add).then_inc(v_done, 1)
                        dve.wait_ge(kb_done, START + n + 1)
                        nc.vector.tensor_scalar(km[:, j, :], kb[:, j, :], 0.0, None, ALU.min).then_inc(km_done, 1)
                    for j in range(GT):
                        n = g * GT + j
                        dve.wait_ge(ke_done, START + n + 1)
                        nc.vector.scalar_tensor_tensor(out=km[:, j, :], in0=kb[:, j, :], scalar=0.0, in1=ke[:, j, :],
                                                       op0=ALU.max, op1=ALU.add).then_inc(kf_done, 1)
                with dve.Fori(0, NG - 1) as g:
                    keys(g, False)
                keys(NG - 1, True)
                dve.wait_ge(zero_mm, START + 1)
                for f in range(KD):
                    for h in range(NH):
                        s = slice(h * DH0, (h + 1) * DH0)
                        nc.vector.tensor_copy(kv_bd[s, f, s], acc[s, f * 256 + h * DH0:f * 256 + (h + 1) * DH0])
                        ins = nc.vector.tensor_copy(ks_bd[s, f, s], acc[s, f * 256 + 128:f * 256 + 128 + DH0])
                ins.then_inc(bd_done, 1)
                with dve.Fori(0, NG) as g:
                    for f in range(KD):
                        n = g * KD + f
                        dve.wait_ge(q_mm, START + n + 1)
                        nc.vector.tensor_scalar(qm[:, f, :], bank[f][:, 0:GC], bq[:, f:f + 1], 0.0, ALU.add, ALU.min)\
                          .then_inc(qm_done, 1)
                    for f in range(KD):
                        n = g * KD + f
                        dve.wait_ge(qe_done, START + n + 1)
                        dve.wait_ge(qr_done, START + n + 1)
                        nc.vector.tensor_tensor(qr[:, f, :], qr[:, f, :], qm[:, f, :], ALU.add).then_inc(qf_done, 1)
                    for f in range(KD):
                        n = g * KD + f
                        dve.wait_ge(nd_mm, START + n + 1)
                        nc.vector.tensor_scalar(dn[:, f, :], bank[5 + f][:, 0:GC], 1e-6, None, ALU.add).then_inc(dn_done, 1)
                        dve.wait_ge(dn_done, START + n + 1)
                        nc.vector.reciprocal(dn[:, f, :], dn[:, f, :]).then_inc(rec_done, 1)
                        dve.wait_ge(rec_done, START + n + 1)
                        dve.wait_ge(out_mm, START + g * KD)
                        ins = nc.vector.tensor_tensor(o_t[:, f, :], bank[2 + f][:, 0:GC], dn[:, f, :], ALU.mult)
                    ins.then_inc(o_done, 1)

            @block.scalar
            def _(act):
                with act.Fori(0, NG * GT // GT) as g:
                    for j in range(GT):
                        act.wait_ge(km_done, START + g * GT + j + 1)
                        act.wait_ge(kf_done, START + g * GT)
                        nc.scalar.activation(ke[:, j, :], km[:, j, :], ACT.Exp).then_inc(ke_done, 1)
                act.wait_ge(w_in, START + 16 * 7)
                with act.Fori(0, NG) as g:
                    for f in range(KD):
                        n = g * KD + f
                        act.wait_ge(nd_mm, START + g * KD)
                        act.wait_ge(q_mm, START + n + 1)
                        act.wait_ge(qm_done, START + n + 1)
                        nc.scalar.activation(qr[:, f, :], bank[f][:, 0:GC], ACT.Relu, bias=bq[:, f:f + 1], scale=1.0)\
                          .then_inc(qr_done, 1)
                        nc.scalar.activation(qm[:, f, :], qm[:, f, :], ACT.Exp).then_inc(qe_done, 1)
                    for f in range(KD):
                        n = g * KD + f
                        act.wait_ge(out_mm, START + n + 1)
                        nc.scalar.activation(mix[:, f, bass.ds(g * GC, GC)], bank[(4, 7)[f]][:, 0:GC], ACT.Identity,
                                             bias=bo[:, f:f + 1], scale=1.0).then_inc(mix_done, 1)


def adjacency(nc, A, sems, sb, bank, src_t, a_dram, pair_dram, range_dram, crowded_t, x_slots):
    (edges_in, iota_done, step, pairs_out, pairs_in, range_out, range_in, tile_iota, zeros, hot_0, hot_1, used_0, used_1,
     acc_mm, cols_done, squared, stored, bad_mm, slots_out, passed) = sems(*("a_" + s for s in (
         "edges_in iota step pairs_out pairs_in range_out range_in tile_iota zeros hot_0 hot_1 used_0 used_1 "
         "acc_mm cols squared stored bad_mm slots_out passed").split()))
    hot_done, used = (hot_0, hot_1), (used_0, used_1)
    BANKS = ((3, 4, 0, 1, 2), (3, 4, 5, 6, 7))
    NBANK = len(BANKS[0])
    ORDER = (2, 3, 4, 0, 1)
    with ExitStack() as ctx:
        dst_t = sb(ctx, "dst_t", [EC, NCH], I32)
        dst_f = sb(ctx, "dst_f", [EC, NCH])
        src_f = sb(ctx, "src_f", [EC, NCH])
        dst_p = sb(ctx, "dst_p", [NU, NPAIR // NU, PC * EC], I32)
        dst_pf = sb(ctx, "dst_pf", [NU, NPAIR // NU, PC * EC])
        ends = sb(ctx, "ends", [NU, 2, NPAIR // NU])
        ends_bc = sb(ctx, "ends_bc", [NT, 2, NPAIR])
        up_i = sb(ctx, "up_i", [NT, NPAIR], I32)
        up = sb(ctx, "up", [NT, NPAIR])
        down = sb(ctx, "down", [NT, NPAIR])
        tile_i = sb(ctx, "tile_i", [NT, 2], I32)
        tile_at = sb(ctx, "tile_at", [NT, 2])
        meets = sb(ctx, "meets", [NT, NPAIR])
        first = sb(ctx, "first", [NT, 1])
        last = sb(ctx, "last", [NT, 1])
        range_i = sb(ctx, "range_i", [NT, 2], I32)
        ranges = sb(ctx, "ranges", [1, NT, 2], I32)
        iota_i = sb(ctx, "iota_i", [EC, RT], I32)
        iota_t = sb(ctx, "iota_t", [EC, RT])
        iota_s = sb(ctx, "iota_s", [EC, NP], I16)
        hot_dst = sb(ctx, "hot_dst", [EC, PC, RT], BF16)
        hot_src = [sb(ctx, f"hot_src{c}", [EC, NP], BF16) for c in range(PC)]
        nil = sb(ctx, "nil", [1, KB * RT], BF16)
        squares = sb(ctx, "squares", [128, KT, RT], BF16)
        a_cols = sb(ctx, "a_cols", [128, KT, GC], BF16)
        square_sum = sb(ctx, "square_sum", [128, NT])
        bad = sb(ctx, "bad", [128, NT])
        bad_row = sb(ctx, "bad_row", [128, 1])
        ones = sb(ctx, "ones", [128, 1])
        no_rows = sb(ctx, "no_rows", [128, D])
        p_bad = bank[0]

        def tile_range(eng, t):
            return [eng.value_load(ranges[0:1, bass.ds(t, 1), k:k + 1].rearrange("p a b -> p (a b)"), min_val=k,
                                   max_val=NPAIR - 1 + k) for k in range(2)]

        def cols(j, i):
            return (a_cols[:, i * KB:(i + 1) * KB, j * RT:(j + 1) * RT],
                    bank[BANKS[j % 2][i]][:, 0:KB * RT].rearrange("p (k r) -> p k r", k=KB))

        with nc.Block() as block:
            @block.sync
            def _(sp):
                sp.dma_start(dst_p[:, :, :], A["dst_c"].rearrange("u (q e) -> u q e", e=PC * EC)).then_inc(edges_in, 16)
                sp.dma_start(dst_t[:, :], A["dst_t"]).then_inc(edges_in, 16)
                sp.wait_ge(step, START + 3)
                for k in range(2):
                    sp.dma_start(pair_dram[k].rearrange("(u q) -> u q", u=NU), ends[:, k, :]).then_inc(pairs_out, 16)
                sp.wait_ge(pairs_out, START + 32)
                for k in range(2):
                    sp.dma_start(ends_bc[:, k, :], pair_dram[k].rearrange("(o c) -> o c", o=1).broadcast_to((NT, NPAIR)))\
                      .then_inc(pairs_in, 16)
                sp.wait_ge(step, START + 13)
                sp.dma_start(range_dram, range_i[:, :]).then_inc(range_out, 16)
                sp.wait_ge(range_out, START + 16)
                sp.dma_start(ranges[:, :, :], range_dram.rearrange("(o t) k -> o t k", o=1)).then_inc(range_in, 16)
                sp.wait_ge(zeros, START + 1)
                sp.dma_start(x_slots.rearrange("(b p) d -> p b d", p=128),
                             no_rows[:, :].rearrange("p (o d) -> p o d", o=1).broadcast_to((128, NBLK, D))).then_inc(slots_out, 16)
                with sp.Fori(0, NG) as g:
                    sp.wait_ge(cols_done, START + (g * GT + GT) * NBANK)
                    sp.dma_start(a_dram[bass.ds(g, 1), :, :, :].rearrange("o p k c -> (o p) k c"), a_cols[:, :, :])\
                      .then_inc(stored, 16)
                sp.wait_ge(stored, START + NG * 16)
                sp.wait_ge(slots_out, START + 16)

            @block.gpsimd
            def _(pool):
                nc.gpsimd.iota(up_i[:, :], pattern=[[1, NPAIR]], base=1, channel_multiplier=0)
                nc.gpsimd.iota(tile_i[:, :], pattern=[[RT, 2]], base=0, channel_multiplier=RT)
                nc.gpsimd.iota(iota_i[:, :], pattern=[[1, RT]], base=0, channel_multiplier=0)
                nc.gpsimd.iota(iota_s[:, :], pattern=[[1, NP]], base=0, channel_multiplier=0).then_inc(iota_done, 1)
                nc.gpsimd.memset(nil[:, :], 0.0)
                nc.gpsimd.memset(ones[:, :], 1.0)
                nc.gpsimd.memset(no_rows[:, :], 0.0).then_inc(zeros, 1)

            @block.vector
            def _(dve):
                n = [0]

                def then(ins):
                    ins.then_inc(step, 1)
                    n[0] += 1
                    dve.wait_ge(step, START + n[0])
                dve.wait_ge(edges_in, START + 32)
                dve.wait_ge(iota_done, START + 1)
                nc.vector.tensor_copy(dst_f[:, :], dst_t[:, :])
                nc.vector.tensor_copy(src_f[:, :], src_t[:, :])
                nc.vector.tensor_copy(iota_t[:, :], iota_i[:, :]).then_inc(tile_iota, 1)
                nc.vector.tensor_copy(up[:, :], up_i[:, :])
                nc.vector.tensor_copy(tile_at[:, :], tile_i[:, :])
                then(nc.vector.tensor_copy(dst_pf[:, :, :], dst_p[:, :, :]))
                then(nc.vector.tensor_reduce(ends[:, 0, :], dst_pf[:, :, :], AX, ALU.min))
                then(nc.vector.tensor_reduce(ends[:, 1, :], dst_pf[:, :, :], AX, ALU.max))
                dve.wait_ge(pairs_in, START + 32)
                then(nc.vector.tensor_scalar(down[:, :], up[:, :], -1.0, float(NPAIR + 1), ALU.mult, ALU.add))
                then(nc.vector.tensor_scalar(meets[:, :], ends_bc[:, 0, :], tile_at[:, 1:2], None, ALU.is_lt))
                then(nc.vector.scalar_tensor_tensor(out=meets[:, :], in0=ends_bc[:, 1, :], scalar=tile_at[:, 0:1],
                                                    in1=meets[:, :], op0=ALU.is_ge, op1=ALU.mult))
                nc.vector.tensor_tensor(up[:, :], up[:, :], meets[:, :], ALU.mult)
                then(nc.vector.tensor_tensor(down[:, :], down[:, :], meets[:, :], ALU.mult))
                nc.vector.tensor_reduce(last[:, :], up[:, :], AX, ALU.max)
                then(nc.vector.tensor_reduce(first[:, :], down[:, :], AX, ALU.max))
                then(nc.vector.tensor_scalar(first[:, :], first[:, :], -1.0, float(NPAIR), ALU.mult, ALU.add))
                then(nc.vector.tensor_scalar(first[:, :], first[:, :], float(NPAIR - 1), None, ALU.min))
                then(nc.vector.scalar_tensor_tensor(out=last[:, :], in0=first[:, :], scalar=1.0, in1=last[:, :],
                                                    op0=ALU.add, op1=ALU.max))
                then(nc.vector.tensor_copy(range_i[:, 0:1], first[:, :]))
                then(nc.vector.tensor_copy(range_i[:, 1:2], last[:, :]))
                dve.wait_ge(range_in, START + 16)
                dve.wait_ge(zeros, START + 1)
                visits = dve.alloc_register("a_visits_dve")
                dve.reg_mov(visits, 0)
                with dve.Fori(0, NG) as g:
                    for j in range(GT):
                        t = g * GT + j
                        lo, hi = tile_range(dve, t)
                        wait_alone(dve, tile_iota, t + 1, passed)
                        with dve.Fori(lo, hi) as u:
                            v = dve.snap(visits, min_val=0, max_val=NT * NPAIR)
                            for c in range(PC):
                                col = bass.ds(u * PC + c, 1)
                                dve.wait_ge(used[c], START + v)
                                nc.vector.tensor_scalar(hot_dst[:, c, :], iota_t[:, :], dst_f[:, col], None, ALU.is_equal)
                                nc.vector.tensor_scalar(hot_src[c][:, :], iota_s[:, :], src_f[:, col], None, ALU.is_equal)\
                                  .then_inc(hot_done[c], 1)
                            dve.reg_add(visits, visits, 1)
                        nc.vector.tensor_scalar(iota_t[:, :], iota_t[:, :], float(RT), None, ALU.add).then_inc(tile_iota, 1)
                dve.wait_ge(squared, START + NT)
                then(nc.vector.tensor_scalar(bad[:, :], square_sum[:, :], float(EXACT * EXACT), None, ALU.is_ge))
                then(nc.vector.tensor_reduce(bad_row[:, :], bad[:, :], AX, ALU.max))
                dve.wait_ge(bad_mm, START + 1)
                then(nc.vector.tensor_scalar(bad[0:1, 0:1], p_bad[0:1, 0:1], 0.5, None, ALU.is_ge))
                then(nc.vector.tensor_copy(crowded_t[:, :], bad[0:1, 0:1]))

            @block.tensor
            def _(pe):
                pe.wait_ge(range_in, START + 16)
                pe.wait_ge(zeros, START + 1)
                visits = pe.alloc_register("a_visits_pe")
                pe.reg_mov(visits, 0)

                def counts(t, j):
                    lo, hi = tile_range(pe, t)
                    banks = BANKS[j % 2]
                    pe.wait_ge(cols_done, START + (t - 1) * NBANK)
                    for i in ORDER:
                        if i < 2:
                            pe.wait_ge(cols_done, START + (t - 1) * NBANK + i + 1)
                        nc.tensor.matmul(bank[banks[i]][:, 0:KB * RT], nil[:, 0:128], nil[:, :], start=True, stop=False,
                                         skip_group_check=True)
                    with pe.Fori(lo, hi) as u:
                        v = pe.snap(visits, min_val=0, max_val=NT * NPAIR)
                        for c in range(PC):
                            pe.wait_ge(hot_done[c], START + v + 1)
                            for i in ORDER:
                                for k in range(KB):
                                    at = (i * KB + k) * 128
                                    ins = nc.tensor.matmul(bank[banks[i]][:, k * RT:(k + 1) * RT], hot_src[c][:, at:at + 128],
                                                           hot_dst[:, c, :], start=False, stop=False, skip_group_check=True)
                            ins.then_inc(used[c], 1)
                        pe.reg_add(visits, visits, 1)
                    for i in ORDER:
                        ins = nc.tensor.matmul(bank[banks[i]][:, 0:1], nil[:, 0:128], nil[:, 0:1], start=False, stop=True,
                                               skip_group_check=True)
                    ins.then_inc(acc_mm, 1)
                with pe.Fori(0, NG) as g:
                    for j in range(GT):
                        counts(g * GT + j, j)
                pe.wait_ge(cols_done, START + NT * NBANK)
                pe.wait_ge(step, START + 15)
                nc.tensor.matmul(p_bad[0:1, 0:1], bad_row[:, :], ones[:, :], start=True, stop=True).then_inc(bad_mm, 1)

            @block.scalar
            def _(act):
                act.wait_ge(zeros, START + 1)

                with act.Fori(0, NG) as g:
                    for j in range(GT):
                        t = g * GT + j
                        act.wait_ge(acc_mm, START + t + 1)
                        act.wait_ge(stored, START + g * 16)
                        act.wait_ge(squared, START + t - GT + 1)
                        for i in range(NBANK):
                            to, read = cols(j, i)
                            nc.scalar.activation(to, read, ACT.Copy).then_inc(cols_done, 1)
                        act.wait_ge(cols_done, START + (t + 1) * NBANK)
                        act.wait_ge(squared, START + t)
                        nc.scalar.activation(squares[:, :, :], a_cols[:, :, j * RT:(j + 1) * RT], ACT.Square,
                                             accum_out=square_sum[:, bass.ds(t, 1)]).then_inc(squared, 1)


def gated_graph(nc, A, sems, sb, bank, nf, a_dram, crowded_t):
    (w_in, bias_done, t1_mm, t1_done, h_mm, h_done, high, low, split, a_in, a_done, chunk_mm, msg_done,
     r_mm, hn_mm, xn_mm, z_mm, r_done, hn_used, t_done, n_done, z_done, blend, nf_done, passed) = sems(*("d_" + s for s in (
         "w_in bias t1_mm t1 h_mm h high low split a_in a chunk_mm msg "
         "r_mm hn_mm xn_mm z_mm r hn_used t n z blend nf passed").split()))
    NH = KT // HB
    AHEAD = 2
    HH = HN // 2
    with ExitStack() as ctx:
        w1 = sb(ctx, "w1", [128, KD, D])
        w2 = sb(ctx, "w2", [128, KD, D])
        wih = sb(ctx, "wih", [128, KD, 3 * D])
        whh = sb(ctx, "whh", [128, KD, 3 * D])
        b1 = sb(ctx, "b1", [128, KD])
        b2_bc = sb(ctx, "b2_bc", [128, D])
        bih = sb(ctx, "bih", [128, 3 * KD])
        bhh = sb(ctx, "bhh", [128, 3 * KD])
        bsum = sb(ctx, "bsum", [128, 3 * KD])
        t1 = sb(ctx, "t1", [128, KD, HN])
        h = sb(ctx, "h", [128, HB, D])
        parts = sb(ctx, "parts", [128, PARTS, KT, D], F32R)
        stage = sb(ctx, "stage", [128, HB, D], F32R)
        a_cols = sb(ctx, "a_cols", [128, KT, GC], BF16)
        a_wide = [sb(ctx, f"a_wide{b}", [128, HB, GC], F32R) for b in range(2)]
        msg = sb(ctx, "msg", [128, KD, GC])
        r_t = sb(ctx, "r_t", [128, KD, GC])
        t_t = sb(ctx, "t_t", [128, KD, GC])
        n_t = sb(ctx, "n_t", [128, KD, GC])
        z_t = sb(ctx, "z_t", [128, KD, GC])
        d_t = sb(ctx, "d_t", [128, KD, GC])
        p_t1, p_h = bank[0:4], bank[4:8]
        p_msg, (p_r, p_hn, p_xn, p_z) = bank[0:2], bank[2:6]

        with nc.Block() as block:
            @block.sync
            def _(sp):
                crowded = sp.value_load(crowded_t[0:1, 0:1], min_val=0, max_val=1)
                with sp.If(crowded < 1):
                    for w, name in ((w1, "w1_0"), (w2, "w2_0"), (wih, "wih_0"), (whh, "whh_0")):
                        sp.dma_start(w[:, :, :], A[name].rearrange("(k p) n -> p k n", p=128)).then_inc(w_in, 16)
                    for w, name in ((b1, "L0_gnn_b1_t"), (bih, "L0_gnn_b_ih_t"), (bhh, "L0_gnn_b_hh_t")):
                        sp.dma_start(w[:, :], A[name]).then_inc(w_in, 16)
                    sp.dma_start(b2_bc[:, :], A["L0_gnn_b2"].rearrange("(o n) -> o n", o=1).broadcast_to((128, D)))\
                      .then_inc(w_in, 16)
                    with sp.Fori(0, STEPS) as s:
                        with sp.Fori(0, NG) as g:
                            sp.wait_ge(a_done, START + (s * NG + g) * NH)
                            sp.dma_start(a_cols[:, :, :], a_dram[bass.ds(g, 1), :, :, :].rearrange("o p k c -> (o p) k c"))\
                              .then_inc(a_in, 16)
                    sp.wait_ge(a_done, START + STEPS * NG * NH)
                    sp.dma_start(a_cols[:, :, :], a_dram[0, :, :, :]).then_inc(a_in, 16)

            @block.gpsimd
            def _(pool):
                crowded = pool.value_load(crowded_t[0:1, 0:1], min_val=0, max_val=1)
                with pool.If(crowded < 1):
                    with pool.Fori(0, STEPS) as s:
                        with pool.Fori(0, NH) as i:
                            q = s * NH + i
                            pool.wait_ge(high, START + q + 1)
                            nc.gpsimd.tensor_tensor(parts[:, 1, bass.ds(i * HB, HB), :], h[:, :, :], stage[:, :, :], ALU.subtract)\
                              .then_inc(low, 1)

            @block.tensor
            def _(pe):
                crowded = pe.value_load(crowded_t[0:1, 0:1], min_val=0, max_val=1)
                with pe.If(crowded < 1):
                    pe.wait_ge(w_in, START + 16 * 8)
                    with pe.Fori(0, STEPS) as s:
                        wait_alone(pe, nf_done, s * NG, passed)
                        wait_alone(pe, z_done, s * NG * KD, passed)
                        with pe.Fori(0, NH) as i:
                            q = s * NH + i
                            for f in range(KD):
                                for half in range(2):
                                    pe.wait_ge(t1_done, START + q * 4)
                                    for k in range(KD):
                                        ins = nc.tensor.matmul(p_t1[f * 2 + half][:, 0:HH], w1[:, k, f * 128:(f + 1) * 128],
                                                               nf[:, k, bass.ds(i * HN + half * HH, HH)],
                                                               start=(k == 0), stop=(k == KD - 1))
                                    ins.then_inc(t1_mm, 1)
                            pe.wait_ge(t1_done, START + q * 4 + 4)
                            for j in range(HB):
                                pe.wait_ge(h_done, START + q * HB + max(j - 3, 0))
                                for k in range(KD):
                                    ins = nc.tensor.matmul(p_h[j % 4][:, 0:D], t1[:, k, j * 128:(j + 1) * 128], w2[:, k, :],
                                                           start=(k == 0), stop=(k == KD - 1))
                                ins.then_inc(h_mm, 1)
                        wait_alone(pe, h_done, (s * NH + NH) * HB, passed)
                        with pe.Fori(0, NG // 2) as i:
                            for b in range(2):
                                n = s * NG + i * 2 + b
                                pe.wait_ge(msg_done, START + n * KD)
                                for c in range(NH):
                                    wide = a_wide[(b * NH + c) % 2]
                                    pe.wait_ge(split, START + s * NH + c + 1)
                                    pe.wait_ge(low, START + s * NH + c + 1)
                                    pe.wait_ge(a_done, START + n * NH + c + 1)
                                    for f in range(KD):
                                        for k in range(HB):
                                            for m in range(PARTS):
                                                ins = nc.tensor.matmul(
                                                    p_msg[f][:, 0:GC], parts[:, m, c * HB + k, f * 128:(f + 1) * 128],
                                                    wide[:, k, :], start=(c == 0 and k == 0 and m == 0),
                                                    stop=(c == NH - 1 and k == HB - 1 and m == PARTS - 1))
                                    ins.then_inc(chunk_mm, 1)
                                cols = bass.ds((i * 2 + b) * GC, GC)

                                def gate(out_p, part, f, start, src, stop):
                                    w = whh if src is nf else wih
                                    for k in range(KD):
                                        x = nf[:, k, cols] if src is nf else msg[:, k, :]
                                        ins = nc.tensor.matmul(out_p[:, 0:GC], w[:, k, part * D + f * 128:part * D + (f + 1) * 128], x,
                                                               start=(start and k == 0), stop=(stop and k == KD - 1))
                                    return ins
                                for f in range(KD):
                                    q = n * KD + f
                                    pe.wait_ge(hn_used, START + q)
                                    gate(p_hn, 2, f, True, nf, True).then_inc(hn_mm, 1)
                                    pe.wait_ge(r_done, START + q)
                                    gate(p_r, 0, f, True, nf, False)
                                    pe.wait_ge(msg_done, START + n * KD + KD)
                                    gate(p_r, 0, f, False, msg, True).then_inc(r_mm, 1)
                                    pe.wait_ge(t_done, START + q)
                                    gate(p_xn, 2, f, True, msg, True).then_inc(xn_mm, 1)
                                    pe.wait_ge(z_done, START + q)
                                    gate(p_z, 1, f, True, nf, False)
                                    gate(p_z, 1, f, False, msg, True).then_inc(z_mm, 1)

            @block.vector
            def _(dve):
                crowded = dve.value_load(crowded_t[0:1, 0:1], min_val=0, max_val=1)
                with dve.If(crowded < 1):
                    dve.wait_ge(w_in, START + 16 * 8)
                    nc.vector.tensor_tensor(bsum[:, :], bih[:, :], bhh[:, :], ALU.add).then_inc(bias_done, 1)

                    def widen(n, b, chunks):
                        wait_alone(dve, a_in, n * 16 + 16, passed)
                        for c in chunks:
                            dve.wait_ge(chunk_mm, START + n * NH + c - 1)
                            nc.vector.tensor_copy(a_wide[(b * NH + c) % 2][:, :, :], a_cols[:, c * HB:(c + 1) * HB, :])\
                              .then_inc(a_done, 1)
                    widen(0, 0, range(AHEAD))
                    with dve.Fori(0, STEPS) as s:
                        with dve.Fori(0, NH) as i:
                            q = s * NH + i
                            dve.wait_ge(split, START + q)
                            dve.wait_ge(low, START + q)
                            for j in range(HB):
                                dve.wait_ge(h_mm, START + q * HB + j + 1)
                                nc.vector.tensor_tensor(h[:, j, :], p_h[j % 4][:, 0:D], b2_bc[:, :], ALU.add).then_inc(h_done, 1)
                            dve.wait_ge(h_done, START + q * HB + HB)
                            nc.vector.tensor_copy(stage[:, :, :], h[:, :, :]).then_inc(high, 1)
                            dve.wait_ge(high, START + q + 1)
                            nc.vector.tensor_copy(parts[:, 0, bass.ds(i * HB, HB), :], stage[:, :, :]).then_inc(split, 1)
                        with dve.Fori(0, NG // 2) as i:
                            for b in range(2):
                                g = i * 2 + b
                                cols = bass.ds(g * GC, GC)
                                widen(s * NG + g, b, range(AHEAD, NH))
                                widen(s * NG + g + 1, 1 - b, range(AHEAD))
                                for f in range(KD):
                                    q = (s * NG + g) * KD + f
                                    dve.wait_ge(hn_mm, START + q + 1)
                                    dve.wait_ge(r_done, START + q + 1)
                                    nc.vector.scalar_tensor_tensor(out=t_t[:, f, :], in0=p_hn[:, 0:GC],
                                                                   scalar=bhh[:, 2 * KD + f:2 * KD + f + 1], in1=r_t[:, f, :],
                                                                   op0=ALU.add, op1=ALU.mult).then_inc(hn_used, 1)
                                    dve.wait_ge(hn_used, START + q + 1)
                                    dve.wait_ge(xn_mm, START + q + 1)
                                    nc.vector.tensor_tensor(t_t[:, f, :], t_t[:, f, :], p_xn[:, 0:GC], ALU.add).then_inc(t_done, 1)
                                q = s * NG + g
                                dve.wait_ge(n_done, START + q * KD + KD)
                                dve.wait_ge(z_done, START + q * KD + KD)
                                nc.vector.tensor_tensor(d_t[:, :, :], nf[:, :, cols], n_t[:, :, :], ALU.subtract).then_inc(blend, 1)
                                dve.wait_ge(blend, START + q * 2 + 1)
                                nc.vector.tensor_tensor(d_t[:, :, :], d_t[:, :, :], z_t[:, :, :], ALU.mult).then_inc(blend, 1)
                                dve.wait_ge(blend, START + q * 2 + 2)
                                nc.vector.tensor_tensor(nf[:, :, cols], d_t[:, :, :], n_t[:, :, :], ALU.add).then_inc(nf_done, 1)

            @block.scalar
            def _(act):
                crowded = act.value_load(crowded_t[0:1, 0:1], min_val=0, max_val=1)
                with act.If(crowded < 1):
                    act.wait_ge(w_in, START + 16 * 8)
                    act.wait_ge(bias_done, START + 1)
                    with act.Fori(0, STEPS) as s:
                        with act.Fori(0, NH) as i:
                            q = s * NH + i
                            act.wait_ge(h_mm, START + q * HB)
                            for f in range(KD):
                                for half in range(2):
                                    act.wait_ge(t1_mm, START + q * 4 + f * 2 + half + 1)
                                    nc.scalar.activation(t1[:, f, half * HH:(half + 1) * HH], p_t1[f * 2 + half][:, 0:HH],
                                                         ACT.Relu, bias=b1[:, f:f + 1], scale=1.0).then_inc(t1_done, 1)
                        with act.Fori(0, NG) as g:
                            n = s * NG + g
                            act.wait_ge(z_mm, START + n * KD)
                            for f in range(KD):
                                act.wait_ge(chunk_mm, START + n * NH + NH)
                                nc.scalar.activation(msg[:, f, :], p_msg[f][:, 0:GC], ACT.Copy).then_inc(msg_done, 1)
                            for f in range(KD):
                                q = n * KD + f
                                act.wait_ge(r_mm, START + q + 1)
                                act.wait_ge(hn_used, START + q)
                                nc.scalar.activation(r_t[:, f, :], p_r[:, 0:GC], ACT.Sigmoid, bias=bsum[:, f:f + 1], scale=1.0)\
                                  .then_inc(r_done, 1)
                                act.wait_ge(t_done, START + q + 1)
                                act.wait_ge(nf_done, START + n)
                                nc.scalar.activation(n_t[:, f, :], t_t[:, f, :], ACT.Tanh,
                                                     bias=bih[:, 2 * KD + f:2 * KD + f + 1], scale=1.0).then_inc(n_done, 1)
                                act.wait_ge(z_mm, START + q + 1)
                                nc.scalar.activation(z_t[:, f, :], p_z[:, 0:GC], ACT.Sigmoid, bias=bsum[:, KD + f:KD + f + 1],
                                                     scale=1.0).then_inc(z_done, 1)


def gated_graph_by_edges(nc, A, sems, sb, bank, tables, nf, h_dram, crowded_t):
    src_t, rel0, base_row, rounds_t, iota_w = tables
    (w_in, bias_done, t1_mm, t1_done, h_mm, h_done, h_stored, acc_zero, tab, hot_a, hot_b, sum_a, sum_b,
     added, idx_a, idx_b, r_mm, hn_mm, xn_mm, z_mm, r_done, hn_used, t_done, n_done, z_done, blend,
     nf_done, reset, passed, *gathered) = sems(*("g_" + s for s in (
         "w_in bias t1_mm t1 h_mm h h_stored acc_zero tab hot_a hot_b sum_a sum_b added idx_a idx_b "
         "r_mm hn_mm xn_mm z_mm r hn_used t n z blend nf reset passed").split()),
                              *(f"g_gathered{j}" for j in range(ITC)))
    hot_ready, summed, idx_ready = (hot_a, hot_b), (sum_a, sum_b), (idx_a, idx_b)
    with ExitStack() as ctx:
        w1 = sb(ctx, "w1", [128, KD, D])
        w2 = sb(ctx, "w2", [128, KD, D])
        wih = sb(ctx, "wih", [128, KD, 3 * D])
        whh = sb(ctx, "whh", [128, KD, 3 * D])
        b1 = sb(ctx, "b1", [128, KD])
        b2_bc = sb(ctx, "b2_bc", [RT, D])
        bih = sb(ctx, "bih", [128, 3 * KD])
        bhh = sb(ctx, "bhh", [128, 3 * KD])
        bsum = sb(ctx, "bsum", [128, 3 * KD])
        msg = sb(ctx, "msg", [128, KD, NW_COLS])
        rel = sb(ctx, "rel", [EC, NCH])
        base = sb(ctx, "base", [1, NU], I32)
        idx = sb(ctx, "idx", [EC, 2, UC], I32)
        rows = [sb(ctx, f"rows{j}", [EC, D]) for j in range(ITC)]
        hot = sb(ctx, "hot", [EC, 2, UC, W])
        t1 = sb(ctx, "t1", [128, KD, GC])
        h_rows = sb(ctx, "h_rows", [RT, GT, D])
        r_t = sb(ctx, "r_t", [128, KD, GC])
        t_t = sb(ctx, "t_t", [128, KD, GC])
        n_t = sb(ctx, "n_t", [128, KD, GC])
        z_t = sb(ctx, "z_t", [128, KD, GC])
        d_t = sb(ctx, "d_t", [128, KD, GC])
        p_sum = bank[0:2]
        p_r, p_hn, p_xn, p_z = bank[2:6]
        p_t1 = bank[6:8]
        p_h = (p_r, p_hn, p_xn, p_z)

        def begin(eng, tag):
            rounds = eng.value_load(rounds_t[0:1, 0:1], min_val=1, max_val=MAXROUNDS)
            reg = eng.alloc_register(f"g_its_{tag}")
            eng.reg_mov(reg, 0)
            return rounds, reg

        def count(eng, reg):
            return eng.snap(reg, min_val=0, max_val=STEPS * NIT * MAXROUNDS)

        with nc.Block() as block:
            @block.sync
            def _(sp):
                crowded = sp.value_load(crowded_t[0:1, 0:1], min_val=0, max_val=1)
                with sp.If(crowded > 0):
                    for t, name in ((w1, "w1_0"), (w2, "w2_0"), (wih, "wih_0"), (whh, "whh_0")):
                        sp.dma_start(t[:, :, :], A[name].rearrange("(k p) n -> p k n", p=128)).then_inc(w_in, 16)
                    for t, name in ((b1, "L0_gnn_b1_t"), (bih, "L0_gnn_b_ih_t"), (bhh, "L0_gnn_b_hh_t")):
                        sp.dma_start(t[:, :], A[name]).then_inc(w_in, 16)
                    sp.dma_start(b2_bc[:, :], A["L0_gnn_b2"].rearrange("(o n) -> o n", o=1).broadcast_to((RT, D))).then_inc(w_in, 16)
                    with sp.Fori(0, STEPS) as s:
                        with sp.Fori(0, NG) as g:
                            sp.wait_ge(h_done, START + (s * NG + g) * GT + GT)
                            sp.dma_start(h_dram[bass.ds(g * GC, GC), :].rearrange("(j p) d -> p j d", p=RT),
                                         h_rows[:, :, :]).then_inc(h_stored, 16)
                            wait_alone(sp, h_stored, (s * NG + g) * 16 + 16, passed)

            @block.gpsimd
            def _(pool):
                crowded = pool.value_load(crowded_t[0:1, 0:1], min_val=0, max_val=1)
                with pool.If(crowded > 0):
                    rounds, reg = begin(pool, "pool")
                    with pool.Fori(0, STEPS) as s:
                        wait_alone(pool, z_mm, s * NG * KD, passed)
                        nc.gpsimd.memset(msg[:, :, :], 0.0).then_inc(acc_zero, 1)
                        wait_alone(pool, h_stored, s * NG * 16 + NG * 16, passed)
                        with pool.Fori(0, rounds) as r:
                            with pool.Fori(0, NIT) as i:
                                its = count(pool, reg)
                                for b in range(2):
                                    wait_alone(pool, summed[b], its + i, passed)
                                    nc.gpsimd.tensor_copy(idx[:, b, :], src_t[:, bass.ds(i * ITC + b * UC, UC)])\
                                      .then_inc(idx_ready[b], 1)
                                    wait_alone(pool, idx_ready[b], its + i + 1, passed)
                                    for j in range(UC):
                                        nc.gpsimd.indirect_dma_start(
                                            out=rows[b * UC + j][:, :], out_offset=None, in_=h_dram,
                                            in_offset=bass.IndirectOffsetOnAxis(ap=idx[:, b, j:j + 1], axis=0),
                                        ).then_inc(gathered[b * UC + j], 16)
                            pool.reg_add(reg, reg, NIT)
                            for b in range(2):
                                wait_alone(pool, summed[b], count(pool, reg), passed)
                            nc.gpsimd.inc_swdge_sem(gathered, [NIT * 16] * ITC, mode="sub")
                            pool.sem_inc(reset, 1)

            @block.tensor
            def _(pe):
                crowded = pe.value_load(crowded_t[0:1, 0:1], min_val=0, max_val=1)
                with pe.If(crowded > 0):
                    rounds, reg = begin(pe, "pe")
                    resets = pe.alloc_register("g_resets")
                    pe.reg_mov(resets, 0)
                    pe.wait_ge(w_in, START + 16 * 8)
                    with pe.Fori(0, STEPS) as s:
                        wait_alone(pe, nf_done, s * NG, passed)
                        with pe.Fori(0, NG) as g:
                            q = s * NG + g
                            cols = bass.ds(g * GC, GC)
                            for f in range(KD):
                                pe.wait_ge(t1_done, START + q * KD)
                                for k in range(KD):
                                    ins = nc.tensor.matmul(p_t1[f][:, 0:GC], w1[:, k, f * 128:(f + 1) * 128], nf[:, k, cols],
                                                           start=(k == 0), stop=(k == KD - 1))
                                ins.then_inc(t1_mm, 1)
                            pe.wait_ge(t1_done, START + q * KD + KD)
                            pe.wait_ge(h_done, START + q * GT)
                            for j in range(GT):
                                for k in range(KD):
                                    ins = nc.tensor.matmul(p_h[j][0:RT, 0:D],
                                                           t1[:, k, j * RT:(j + 1) * RT], w2[:, k, :],
                                                           start=(k == 0), stop=(k == KD - 1))
                                ins.then_inc(h_mm, 1)
                        with pe.Fori(0, rounds) as r:
                            wait_alone(pe, reset, pe.snap(resets, min_val=0, max_val=STEPS * MAXROUNDS), passed)
                            with pe.Fori(0, NIT) as i:
                                its = count(pe, reg)
                                for b in range(2):
                                    pe.wait_ge(hot_ready[b], START + its + i + 1)
                                    pe.wait_ge(added, START + (its + i) * 2)
                                    for j in range(UC):
                                        pe.wait_ge(gathered[b * UC + j], i * 16 + 16)
                                        for k in range(KD):
                                            ins = nc.tensor.matmul(p_sum[b][:, k * W:(k + 1) * W],
                                                                   rows[b * UC + j][:, k * 128:(k + 1) * 128],
                                                                   hot[:, b, j, :], start=(j == 0 and k == 0), stop=(j == UC - 1),
                                                                   skip_group_check=True)
                                    ins.then_inc(summed[b], 1)
                            pe.reg_add(reg, reg, NIT)
                            pe.reg_add(resets, resets, 1)
                        wait_alone(pe, added, count(pe, reg) * 2, passed)
                        with pe.Fori(0, NG) as g:
                            cols = bass.ds(g * GC, GC)
                            for f in range(KD):
                                q = (s * NG + g) * KD + f

                                def gate(out_p, n, parts):
                                    ws = [(w, src, k) for w, src in parts for k in range(KD)]
                                    for m, (w, src, k) in enumerate(ws):
                                        ins = nc.tensor.matmul(out_p[:, 0:GC], w[:, k, n * D + f * 128:n * D + (f + 1) * 128],
                                                               src[:, k, cols], start=(m == 0), stop=(m == len(ws) - 1))
                                    return ins
                                pe.wait_ge(r_done, START + q)
                                gate(p_r, 0, ((wih, msg), (whh, nf))).then_inc(r_mm, 1)
                                pe.wait_ge(hn_used, START + q)
                                gate(p_hn, 2, ((whh, nf),)).then_inc(hn_mm, 1)
                                pe.wait_ge(t_done, START + q)
                                gate(p_xn, 2, ((wih, msg),)).then_inc(xn_mm, 1)
                                pe.wait_ge(z_done, START + q)
                                gate(p_z, 1, ((wih, msg), (whh, nf))).then_inc(z_mm, 1)

            @block.vector
            def _(dve):
                crowded = dve.value_load(crowded_t[0:1, 0:1], min_val=0, max_val=1)
                with dve.If(crowded > 0):
                    rounds, reg = begin(dve, "dve")
                    tabs = dve.alloc_register("g_tabs")
                    dve.reg_mov(tabs, 0)
                    dve.wait_ge(w_in, START + 16 * 8)
                    nc.vector.tensor_tensor(bsum[:, :], bih[:, :], bhh[:, :], ALU.add).then_inc(bias_done, 1)
                    with dve.Fori(0, STEPS) as s:
                        nc.vector.tensor_copy(rel[:, :], rel0[:, :]).then_inc(tab, 1)
                        nc.vector.tensor_copy(base[:, :], base_row[:, :]).then_inc(tab, 1)
                        dve.reg_add(tabs, tabs, 2)
                        with dve.Fori(0, NG) as g:
                            q = s * NG + g
                            dve.wait_ge(h_stored, START + q * 16)
                            for j in range(GT):
                                dve.wait_ge(h_mm, START + q * GT + j + 1)
                                nc.vector.tensor_tensor(h_rows[:, j, :], p_h[j][0:RT, 0:D],
                                                        b2_bc[:, :], ALU.add).then_inc(h_done, 1)
                        wait_alone(dve, acc_zero, s + 1, passed)
                        with dve.Fori(0, rounds) as r:
                            wait_alone(dve, tab, dve.snap(tabs, min_val=0, max_val=1 << 20), passed)
                            with dve.Fori(0, NIT) as i:
                                its = count(dve, reg)
                                for b in range(2):
                                    dve.wait_ge(summed[b], START + its + i)
                                    nc.vector.tensor_tensor(
                                        hot[:, b, :, :],
                                        iota_w[:, :].rearrange("p (o w) -> p o w", o=1).broadcast_to((EC, UC, W)),
                                        rel[:, bass.ds(i * ITC + b * UC, UC)].rearrange("p (c o) -> p c o", o=1)
                                        .broadcast_to((EC, UC, W)), ALU.is_equal).then_inc(hot_ready[b], 1)
                                for b in range(2):
                                    at = dve.value_load(base[0:1, bass.ds(i * 2 + b, 1)], min_val=0, max_val=NP)
                                    dve.wait_ge(summed[b], START + its + i + 1)
                                    dve.wait_ge(added, START + (its + i) * 2 + b)
                                    win = msg[:, :, bass.ds(at, W)]
                                    nc.vector.tensor_tensor(win, win, p_sum[b][:, 0:KD * W].rearrange("p (k w) -> p k w", k=KD),
                                                            ALU.add).then_inc(added, 1)
                            dve.reg_add(reg, reg, NIT)
                            nc.vector.tensor_scalar(rel[:, :], rel[:, :], float(W), None, ALU.subtract).then_inc(tab, 1)
                            nc.vector.tensor_scalar(base[:, :], base[:, :], float(W), float(NP), ALU.add, ALU.min)\
                              .then_inc(tab, 1)
                            dve.reg_add(tabs, tabs, 2)
                        with dve.Fori(0, NG) as g:
                            cols = bass.ds(g * GC, GC)
                            for f in range(KD):
                                q = (s * NG + g) * KD + f
                                dve.wait_ge(hn_mm, START + q + 1)
                                dve.wait_ge(r_done, START + q + 1)
                                nc.vector.scalar_tensor_tensor(out=t_t[:, f, :], in0=p_hn[:, 0:GC],
                                                               scalar=bhh[:, 2 * KD + f:2 * KD + f + 1], in1=r_t[:, f, :],
                                                               op0=ALU.add, op1=ALU.mult).then_inc(hn_used, 1)
                                dve.wait_ge(hn_used, START + q + 1)
                                dve.wait_ge(xn_mm, START + q + 1)
                                nc.vector.tensor_tensor(t_t[:, f, :], t_t[:, f, :], p_xn[:, 0:GC], ALU.add).then_inc(t_done, 1)
                            q = s * NG + g
                            dve.wait_ge(n_done, START + q * KD + KD)
                            dve.wait_ge(z_done, START + q * KD + KD)
                            nc.vector.tensor_tensor(d_t[:, :, :], nf[:, :, cols], n_t[:, :, :], ALU.subtract).then_inc(blend, 1)
                            dve.wait_ge(blend, START + q * 2 + 1)
                            nc.vector.tensor_tensor(d_t[:, :, :], d_t[:, :, :], z_t[:, :, :], ALU.mult).then_inc(blend, 1)
                            dve.wait_ge(blend, START + q * 2 + 2)
                            nc.vector.tensor_tensor(nf[:, :, cols], d_t[:, :, :], n_t[:, :, :], ALU.add).then_inc(nf_done, 1)

            @block.scalar
            def _(act):
                crowded = act.value_load(crowded_t[0:1, 0:1], min_val=0, max_val=1)
                with act.If(crowded > 0):
                    act.wait_ge(w_in, START + 16 * 8)
                    act.wait_ge(bias_done, START + 1)
                    with act.Fori(0, STEPS) as s:
                        with act.Fori(0, NG) as g:
                            q = s * NG + g
                            act.wait_ge(h_mm, START + q * GT)
                            for f in range(KD):
                                act.wait_ge(t1_mm, START + q * KD + f + 1)
                                nc.scalar.activation(t1[:, f, :], p_t1[f][:, 0:GC], ACT.Relu, bias=b1[:, f:f + 1], scale=1.0)\
                                  .then_inc(t1_done, 1)
                        with act.Fori(0, NG) as g:
                            for f in range(KD):
                                q = (s * NG + g) * KD + f
                                act.wait_ge(r_mm, START + q + 1)
                                act.wait_ge(hn_used, START + q)
                                nc.scalar.activation(r_t[:, f, :], p_r[:, 0:GC], ACT.Sigmoid, bias=bsum[:, f:f + 1], scale=1.0)\
                                  .then_inc(r_done, 1)
                                act.wait_ge(t_done, START + q + 1)
                                act.wait_ge(nf_done, START + s * NG + g)
                                nc.scalar.activation(n_t[:, f, :], t_t[:, f, :], ACT.Tanh,
                                                     bias=bih[:, 2 * KD + f:2 * KD + f + 1], scale=1.0).then_inc(n_done, 1)
                                act.wait_ge(z_mm, START + q + 1)
                                nc.scalar.activation(z_t[:, f, :], p_z[:, 0:GC], ACT.Sigmoid, bias=bsum[:, KD + f:KD + f + 1],
                                                     scale=1.0).then_inc(z_done, 1)


def add_transposed(nc, tag, sems, bank, sb, ident, x_rows, a_t):
    staged, turned, added = sems(*(f"{tag}_{s}" for s in ("staged", "turned", "added")))
    with ExitStack() as ctx:
        s_t = sb(ctx, "s_t", [128, KD, GC])
        with nc.Block() as block:
            @block.gpsimd
            def _(pool):
                with pool.Fori(0, NG) as g:
                    pool.wait_ge(turned, START + g * GT)
                    nc.gpsimd.tensor_copy(s_t[:, :, :], a_t[:, :, bass.ds(g * GC, GC)]).then_inc(staged, 1)

            @block.tensor
            def _(pe):
                with pe.Fori(0, NG) as g:
                    pe.wait_ge(staged, START + g + 1)
                    pe.wait_ge(added, START + g * GT)
                    for j in range(GT):
                        for k in range(KD):
                            ins = nc.tensor.transpose(bank[j][0:RT, k * 128:(k + 1) * 128], s_t[:, k, j * RT:(j + 1) * RT],
                                                      ident[:, :])
                        ins.then_inc(turned, 1)

            @block.vector
            def _(dve):
                with dve.Fori(0, NG) as g:
                    for j in range(GT):
                        dve.wait_ge(turned, START + g * GT + j + 1)
                        row = x_rows[:, bass.ds(g * GT + j, 1), :].rearrange("p a d -> p (a d)")
                        nc.vector.tensor_tensor(row, row, bank[j][0:RT, 0:D], ALU.add).then_inc(added, 1)


def route(nc, tag, A, sems, sb, bank, xt, hidden, count, w_names, b_names, gates=None, picked=None, wt=None):
    (w_in, hid_mm, hid_done, lg_mm, lg_done, step, ex_done, staged, top_done, gate_done) = sems(*(f"{tag}_{s}" for s in (
        "w_in hid_mm hid lg_mm lg step exp staged top gate").split()))
    nw = len(w_names) + len(b_names)
    with ExitStack() as ctx:
        w1 = sb(ctx, "rw1", [128, KD, 128 if hidden else 8])
        w2 = sb(ctx, "rw2", [128, 8])
        b1 = sb(ctx, "rb1", [128, 1])
        b2 = sb(ctx, "rb2", [RT, 8])
        rh = sb(ctx, "rh", [128, KD, GC])
        lg = sb(ctx, "lg", [RT, NT, 8])
        pr = sb(ctx, "pr", [RT, NT, 8])
        mx = sb(ctx, "mx", [RT, NT])
        best = sb(ctx, "best", [RT, NT, 8])
        at = sb(ctx, "at", [RT, NT, 8], U32)
        at_f = sb(ctx, "at_f", [RT, NT, 8]) if picked is None else picked
        iota_i = sb(ctx, "iota8i", [RT, 8], I32)
        iota_f = sb(ctx, "iota8", [RT, 8])
        wt = sb(ctx, "wt", [RT, NT, 2]) if wt is None else wt
        one = sb(ctx, "one", [RT, NT, 8])
        with nc.Block() as block:
            @block.sync
            def _(sp):
                sp.wait_ge(step, START + 1)
                sp.dma_start(w1[:, :, :], A[w_names[0]].rearrange("(k p) n -> p k n", p=128)).then_inc(w_in, 16)
                if hidden:
                    sp.dma_start(w2[:, :], A[w_names[1]]).then_inc(w_in, 16)
                    sp.dma_start(b1[:, :], A[b_names[0]].rearrange("(p o) -> p o", o=1)).then_inc(w_in, 16)
                    sp.dma_start(b2[:, 0:count], A[b_names[1]].rearrange("(o n) -> o n", o=1).broadcast_to((RT, count)))\
                      .then_inc(w_in, 16)

            @block.gpsimd
            def _(pool):
                nc.gpsimd.iota(iota_i[:, :], pattern=[[1, 8]], base=0, channel_multiplier=0).then_inc(staged, 1)
                if not hidden:
                    with pool.Fori(0, NG) as g:
                        pool.wait_ge(lg_mm, START + g)
                        nc.gpsimd.tensor_copy(rh[:, :, :], xt[:, :, bass.ds(g * GC, GC)]).then_inc(hid_done, 1)

            @block.tensor
            def _(pe):
                pe.wait_ge(w_in, START + 16 * nw)
                with pe.Fori(0, NG) as g:
                    if hidden:
                        pe.wait_ge(hid_done, START + g)
                        for k in range(KD):
                            ins = nc.tensor.matmul(bank[0][:, 0:GC], w1[:, k, :], xt[:, k, bass.ds(g * GC, GC)],
                                                   start=(k == 0), stop=(k == KD - 1))
                        ins.then_inc(hid_mm, 1)
                    pe.wait_ge(hid_done, START + g + 1)
                    pe.wait_ge(lg_done, START + g)
                    for j in range(GT):
                        for k in range(1 if hidden else KD):
                            ins = nc.tensor.matmul(bank[1][0:RT, j * 8:j * 8 + 8], rh[:, k, j * RT:(j + 1) * RT],
                                                   w2[:, :] if hidden else w1[:, k, :],
                                                   start=(k == 0), stop=(hidden or k == KD - 1))
                    ins.then_inc(lg_mm, 1)

            @block.scalar
            def _(act):
                if hidden:
                    act.wait_ge(w_in, START + 16 * nw)
                    with act.Fori(0, NG) as g:
                        act.wait_ge(hid_mm, START + g + 1)
                        act.wait_ge(lg_mm, START + g)
                        nc.scalar.activation(rh[:, 0, :], bank[0][:, 0:GC], ACT.Relu, bias=b1[:, :], scale=1.0)\
                          .then_inc(hid_done, 1)
                act.wait_ge(step, START + 3)
                nc.scalar.activation(pr[:, :, :], lg[:, :, :], ACT.Exp).then_inc(ex_done, 1)
                if hidden:
                    act.wait_ge(step, START + 6)
                    nc.scalar.activation(wt[:, :, 1], mx[:, :], ACT.Exp).then_inc(ex_done, 1)

            @block.vector
            def _(dve):
                n = [0]

                def then(ins):
                    n[0] += 1
                    ins.then_inc(step, 1)
                    dve.wait_ge(step, START + n[0])

                def per_node(a):
                    return a.rearrange("p (t o) -> p t o", o=1).broadcast_to((RT, NT, 8))
                then(nc.vector.memset(b2[:, :], NEG if count < 8 else 0.0))
                if hidden:
                    dve.wait_ge(w_in, START + 16 * nw)
                with dve.Fori(0, NG) as g:
                    dve.wait_ge(lg_mm, START + g + 1)
                    nc.vector.tensor_tensor(lg[:, bass.ds(g * GT, GT), :],
                                            bank[1][0:RT, 0:GT * 8].rearrange("p (j e) -> p j e", j=GT),
                                            b2[:, :].rearrange("p (o e) -> p o e", o=1).broadcast_to((RT, GT, 8)),
                                            ALU.add).then_inc(lg_done, 1)
                dve.wait_ge(lg_done, START + NG)
                then(nc.vector.tensor_reduce(mx[:, :], lg[:, :, :], AX, ALU.max))
                then(nc.vector.tensor_tensor(lg[:, :, :], lg[:, :, :], per_node(mx[:, :]), ALU.subtract))
                dve.wait_ge(ex_done, START + 1)
                then(nc.vector.tensor_reduce(mx[:, :], pr[:, :, :], AX, ALU.add))
                then(nc.vector.reciprocal(mx[:, :], mx[:, :]))
                nc.vector.tensor_tensor(pr[:, :, :], pr[:, :, :], per_node(mx[:, :]), ALU.mult).then_inc(top_done, 1)
                dve.wait_ge(top_done, START + 1)
                for t in range(NT):
                    nc.vector.max(best[:, t, :], pr[:, t, :]).then_inc(top_done, 1)
                dve.wait_ge(top_done, START + NT + 1)
                for t in range(NT):
                    nc.vector.max_index(at[:, t, :], best[:, t, :], pr[:, t, :]).then_inc(top_done, 1)
                if hidden:
                    then(nc.vector.tensor_tensor(mx[:, :], best[:, :, 1], best[:, :, 0], ALU.subtract))
                    dve.wait_ge(ex_done, START + 2)
                    then(nc.vector.tensor_scalar(mx[:, :], wt[:, :, 1], 1.0, None, ALU.add))
                    then(nc.vector.reciprocal(wt[:, :, 0], mx[:, :]))
                    then(nc.vector.tensor_tensor(wt[:, :, 1], wt[:, :, 1], wt[:, :, 0], ALU.mult))
                else:
                    then(nc.vector.tensor_tensor(mx[:, :], best[:, :, 1], best[:, :, 0], ALU.add))
                    then(nc.vector.tensor_scalar(mx[:, :], mx[:, :], 1e-9, None, ALU.add))
                    then(nc.vector.reciprocal(mx[:, :], mx[:, :]))
                    nc.vector.tensor_tensor(wt[:, :, 0], best[:, :, 0], mx[:, :], ALU.mult)
                    then(nc.vector.tensor_tensor(wt[:, :, 1], best[:, :, 1], mx[:, :], ALU.mult))
                dve.wait_ge(top_done, START + 2 * NT + 1)
                dve.wait_ge(staged, START + 1)
                nc.vector.tensor_copy(iota_f[:, :], iota_i[:, :])
                then(nc.vector.tensor_copy(at_f[:, :, :], at[:, :, :]))
                if gates is None:
                    return
                every = iota_f[:, :].rearrange("p (o e) -> p o e", o=1).broadcast_to((RT, NT, 8))
                for c, to in ((0, gates), (1, one)):
                    then(nc.vector.tensor_tensor(to[:, :, :], every, at_f[:, :, c:c + 1].broadcast_to((RT, NT, 8)), ALU.is_equal))
                    then(nc.vector.tensor_tensor(to[:, :, :], to[:, :, :], wt[:, :, c:c + 1].broadcast_to((RT, NT, 8)), ALU.mult))
                nc.vector.tensor_tensor(gates[:, :, :], gates[:, :, :], one[:, :, :], ALU.add)


def expert_mlp(nc, A, sems, sb, bank, xt, x_rows):
    w_in, ones_done, h1_mm, h1_done, h2_mm, h2_done, y_mm, y_done = sems(*("e0_" + s for s in (
        "w_in ones h1_mm h1 h2_mm h2 y_mm y").split()))
    with ExitStack() as ctx:
        gates = sb(ctx, "gates", [RT, NT, 8])
        route(nc, "r0", A, sems, sb, bank, xt, True, E0, ("L0_ffn_router_w1", "rw2_0"),
              ("L0_ffn_router_b1", "L0_ffn_router_b2"), gates)
        w = [sb(ctx, f"ew{i}", [128, E0, KD, D]) for i in range(3)]
        b1 = sb(ctx, "eb1", [128, E0, KD])
        b2 = sb(ctx, "eb2", [128, E0, KD])
        b3 = sb(ctx, "eb3", [1, E0, D])
        ones = sb(ctx, "ones", [1, RT])
        h1 = sb(ctx, "h1", [128, 2, KD, GC])
        h2 = sb(ctx, "h2", [128, 2, KD, GC])
        with nc.Block() as block:
            @block.sync
            def _(sp):
                for t, name in zip(w, ("L0_ffn_expert_w1", "L0_ffn_expert_w2", "L0_ffn_expert_w3")):
                    for e in range(E0):
                        sp.dma_start(t[:, e, :, :], A[name][e].rearrange("(k p) n -> p k n", p=128)).then_inc(w_in, 16)
                for t, name in ((b1, "L0_ffn_expert_b1_t"), (b2, "L0_ffn_expert_b2_t")):
                    sp.dma_start(t[:, :, :], A[name]).then_inc(w_in, 16)
                sp.dma_start(b3[:, :, :], A["L0_ffn_expert_b3"].rearrange("(o e) n -> o e n", o=1)).then_inc(w_in, 16)
            NW = 16 * (3 * E0 + 3)

            @block.tensor
            def _(pe):
                pe.wait_ge(w_in, START + NW)
                pe.wait_ge(ones_done, START + 1)
                with pe.Fori(0, NG) as g:
                    cols = bass.ds(g * GC, GC)

                    def layer1(e):
                        pe.wait_ge(h1_done, START + (g * E0 + e) * KD)
                        for f in range(KD):
                            for k in range(KD):
                                ins = nc.tensor.matmul(bank[f][:, 0:GC], w[0][:, e, k, f * 128:(f + 1) * 128], xt[:, k, cols],
                                                       start=(k == 0), stop=(k == KD - 1))
                            ins.then_inc(h1_mm, 1)

                    def layer2(e):
                        pe.wait_ge(h1_done, START + (g * E0 + e) * KD + KD)
                        pe.wait_ge(h2_done, START + (g * E0 + e) * KD)
                        for f in range(KD):
                            for k in range(KD):
                                ins = nc.tensor.matmul(bank[2 + f][:, 0:GC], w[1][:, e, k, f * 128:(f + 1) * 128],
                                                       h1[:, e % 2, k, :], start=(k == 0), stop=(k == KD - 1))
                            ins.then_inc(h2_mm, 1)

                    def layer3(e):
                        pe.wait_ge(h2_done, START + (g * E0 + e) * KD + KD)
                        pe.wait_ge(y_done, START + (g * E0 + e) * GT)
                        for j in range(GT):
                            o = bank[4 + j][0:RT, 0:D]
                            for k in range(KD):
                                nc.tensor.matmul(o, h2[:, e % 2, k, j * RT:(j + 1) * RT], w[2][:, e, k, :],
                                                 start=(k == 0), stop=False)
                            nc.tensor.matmul(o, ones[:, :], b3[:, e, :], start=False, stop=True).then_inc(y_mm, 1)
                    layer1(0)
                    for e in range(E0):
                        layer2(e)
                        if e + 1 < E0:
                            layer1(e + 1)
                        layer3(e)

            @block.scalar
            def _(act):
                act.wait_ge(w_in, START + NW)
                with act.Fori(0, NG) as g:
                    def relu(e, mm, b, bias, to, done):
                        for f in range(KD):
                            act.wait_ge(mm, START + (g * E0 + e) * KD + f + 1)
                            nc.scalar.activation(to[:, e % 2, f, :], b[f][:, 0:GC], ACT.Relu, bias=bias[:, e, f:f + 1],
                                                 scale=1.0).then_inc(done, 1)
                    relu(0, h1_mm, bank[0:2], b1, h1, h1_done)
                    for e in range(E0):
                        relu(e, h2_mm, bank[2:4], b2, h2, h2_done)
                        if e + 1 < E0:
                            relu(e + 1, h1_mm, bank[0:2], b1, h1, h1_done)

            @block.vector
            def _(dve):
                nc.vector.memset(ones[:, :], 1.0).then_inc(ones_done, 1)
                with dve.Fori(0, NG) as g:
                    for e in range(E0):
                        for j in range(GT):
                            n = (g * E0 + e) * GT + j
                            t = g * GT + j
                            dve.wait_ge(y_mm, START + n + 1)
                            if e:
                                dve.wait_ge(y_done, START + n - GT + 1)
                            row = x_rows[:, bass.ds(t, 1), :].rearrange("p a d -> p (a d)")
                            nc.vector.scalar_tensor_tensor(
                                out=row, in0=bank[4 + j][0:RT, 0:D],
                                scalar=gates[:, bass.ds(t, 1), e:e + 1].rearrange("p a b -> p (a b)"),
                                in1=row, op0=ALU.mult, op1=ALU.add).then_inc(y_done, 1)


def galerkin_and_nodes(nc, A, sems, sb, bank, xt, wcomb, h_dram):
    (w_in, const_done, wc_done, staged, k_mm, v_mm, h_mm, k_done, sq_done, var_done, std_done, r_done, rr_done,
     v_done, h_done, h_stored, d_mm, dots_mm, bd_done, m_mm, m_done, c_mm, c_done) = sems(*("m_" + s for s in (
         "w_in const wc staged k_mm v_mm h_mm k sq var std r rr v h h_stored d_mm dots_mm bd m_mm m c_mm c").split()))
    KI = INNER // 128
    with ExitStack() as ctx:
        wkv = sb(ctx, "wkv1", [128, KD, 2 * INNER])
        mean = sb(ctx, "mean", [128, KD, 2 * HEADS1])
        wq_t = sb(ctx, "wq_t", [128, KI, D])
        wout = sb(ctx, "wout", [128, KI, D])
        wlin = sb(ctx, "wlin", [128, KD, 128])
        z = sb(ctx, "z", [RT, NT])
        z8 = sb(ctx, "z8", [RT, NT])
        zeros = sb(ctx, "zeros", [1, 512])
        stage = sb(ctx, "stage", [128, KD, GC])
        kc = sb(ctx, "kc", [RT, 2, INNER])
        sq = sb(ctx, "sq", [RT, 2, 2 * INNER])
        var = sb(ctx, "var", [RT, 2, 2 * HEADS1])
        rr = sb(ctx, "rr", [RT, 2, HEADS1])
        vs = sb(ctx, "vs", [RT, 2, INNER])
        h_rows = sb(ctx, "h_rows", [RT, GT, D])
        dots = sb(ctx, "dots", [128, KI, 128])
        m_s = sb(ctx, "m_s", [128, KI, D])
        eps_t = sb(ctx, "eps", [RT, 1])
        acc = bank[6]
        NW = 16 * 5

        def last(j, f):
            return f

        with nc.Block() as block:
            @block.sync
            def _(sp):
                sp.dma_start(wkv[:, :, :], A["wkv1"].rearrange("(k p) n -> p k n", p=128)).then_inc(w_in, 16)
                sp.dma_start(wq_t[:, :, :], A["wq1_t"].rearrange("(k p) n -> p k n", p=128)).then_inc(w_in, 16)
                sp.dma_start(wout[:, :, :], A["L1_mix_w_out"].rearrange("(k p) n -> p k n", p=128)).then_inc(w_in, 16)
                sp.dma_start(wlin[:, :, :], A["wlin"].rearrange("(k p) n -> p k n", p=128)).then_inc(w_in, 16)
                sp.dma_start(z[:, :], A["z_rows"]).then_inc(w_in, 16)
                with sp.Fori(0, NG) as g:
                    sp.wait_ge(h_done, START + g * GT + GT)
                    sp.dma_start(h_dram[bass.ds(g * GC, GC), :].rearrange("(j p) d -> p j d", p=RT),
                                 h_rows[:, :, :]).then_inc(h_stored, 16)
                sp.wait_ge(h_stored, START + NG * 16)

            @block.gpsimd
            def _(pool):
                nc.gpsimd.memset(zeros[:, :], 0.0).then_inc(const_done, 1)
                nc.gpsimd.memset(dots[:, :, :], 0.0).then_inc(const_done, 1)
                nc.gpsimd.memset(eps_t[:, :], EPS).then_inc(const_done, 1)
                nc.gpsimd.memset(xt[:, :, N:NP], 0.0).then_inc(const_done, 1)
                pool.wait_ge(const_done, START + 4)
                with pool.Fori(0, NG) as g:
                    pool.wait_ge(h_mm, START + g * GT)
                    nc.gpsimd.tensor_copy(stage[:, :, :], xt[:, :, bass.ds(g * GC, GC)]).then_inc(staged, 1)

            @block.tensor
            def _(pe):
                pe.wait_ge(w_in, START + NW)
                pe.wait_ge(const_done, START + 4)
                pe.wait_ge(wc_done, START + 3)
                nc.tensor.matmul(acc[:, :], zeros[:, 0:128], zeros[:, :], start=True, stop=False, skip_group_check=True)
                with pe.Fori(0, NG) as g:
                    pe.wait_ge(staged, START + g + 1)

                    def maps(j):
                        n = g * GT + j
                        b = 3 * (j % 2)
                        rows = slice(j * RT, (j + 1) * RT)
                        pe.wait_ge(sq_done, START + (n if j > 1 else g * GT))
                        pe.wait_ge(v_done, START + (n - 1 if j > 1 else g * GT))
                        pe.wait_ge(h_done, START + (n - 1 if j > 1 else g * GT))
                        for k in range(KD):
                            ins = nc.tensor.matmul(bank[b][0:RT, :], stage[:, k, rows], wkv[:, k, 0:INNER],
                                                   start=(k == 0), stop=(k == KD - 1))
                        ins.then_inc(k_mm, 1)
                        for k in range(KD):
                            ins = nc.tensor.matmul(bank[b + 1][0:RT, :], stage[:, k, rows], wkv[:, k, INNER:],
                                                   start=(k == 0), stop=(k == KD - 1))
                        ins.then_inc(v_mm, 1)
                        for k in range(KD):
                            ins = nc.tensor.matmul(bank[b + 2][0:RT, k * 128:(k + 1) * 128], stage[:, k, rows], wlin[:, k, :],
                                                   start=True, stop=True)
                        ins.then_inc(h_mm, 1)

                    def sums(j):
                        n = g * GT + j
                        pe.wait_ge(k_done, START + n + 1)
                        pe.wait_ge(v_done, START + n + 1)
                        for f in range(KI):
                            s = slice(f * 128, (f + 1) * 128)
                            ins = nc.tensor.matmul(acc[:, s], vs[:, j % 2, s], kc[:, j % 2, s], start=False, stop=False,
                                                   skip_group_check=True)
                        ins.then_inc(d_mm, 1)
                    maps(0)
                    for j in range(GT):
                        if j + 1 < GT:
                            maps(j + 1)
                        sums(j)
                nc.tensor.matmul(acc[:, :], zeros[:, 0:128], zeros[:, :], start=False, stop=True,
                                 skip_group_check=True).then_inc(dots_mm, 1)
                pe.wait_ge(bd_done, START + 1)
                for f in range(KI):
                    ins = nc.tensor.matmul(bank[f][:, 0:D], dots[:, f, :], wout[:, f, :], start=True, stop=True)
                ins.then_inc(m_mm, 1)
                pe.wait_ge(m_done, START + 1)
                for c in range(KD):
                    for f in range(KI):
                        ins = nc.tensor.matmul(bank[4 + c][:, 0:D], wq_t[:, f, c * 128:(c + 1) * 128], m_s[:, f, :],
                                               start=(f == 0), stop=(f == KI - 1))
                ins.then_inc(c_mm, 1)

            @block.scalar
            def _(act):
                act.wait_ge(w_in, START + NW)
                act.wait_ge(const_done, START + 4)
                nc.scalar.activation(z8[:, :], z[:, :], ACT.Copy, scale=MUL ** -0.5).then_inc(c_done, 1)
                act.wait_ge(c_done, START + 1)
                with act.Fori(0, NG) as g:
                    def squares(j):
                        n = g * GT + j
                        b = 3 * (j % 2)
                        act.wait_ge(k_mm, START + n + 1)
                        act.wait_ge(d_mm, START + (n - 1 if j > 1 else g * GT))
                        act.wait_ge(var_done, START + (n - 1 if j > 1 else g * GT))
                        nc.scalar.activation(kc[:, j % 2, :], bank[b][0:RT, :], ACT.Copy).then_inc(k_done, 1)
                        nc.scalar.activation(sq[:, j % 2, 0:INNER], bank[b][0:RT, :], ACT.Square)
                        act.wait_ge(v_mm, START + n + 1)
                        nc.scalar.activation(sq[:, j % 2, INNER:], bank[b + 1][0:RT, :], ACT.Square).then_inc(sq_done, 1)
                        act.wait_ge(h_mm, START + n + 1)
                        act.wait_ge(h_stored, START + g * 16)
                        nc.scalar.activation(h_rows[:, j, :], bank[b + 2][0:RT, 0:D], ACT.Copy,
                                             scale=z8[:, bass.ds(n, 1)]).then_inc(h_done, 1)

                    def deviation(j):
                        n = g * GT + j
                        act.wait_ge(var_done, START + n + 1)
                        nc.scalar.activation(var[:, j % 2, :], var[:, j % 2, :], ACT.Sqrt, bias=eps_t[:, :], scale=1.0 / DH1)\
                          .then_inc(std_done, 1)
                    squares(0)
                    for j in range(GT):
                        if j + 1 < GT:
                            squares(j + 1)
                        deviation(j)

            @block.vector
            def _(dve):
                dve.wait_ge(w_in, START + NW)
                heads = wkv[:, :, :].rearrange("p k (h d) -> p (k h) d", d=DH1)
                means = mean[:, :, :].rearrange("p k h -> p (k h)")
                nc.vector.tensor_reduce(means, heads, AX, ALU.add).then_inc(wc_done, 1)
                dve.wait_ge(wc_done, START + 1)
                nc.vector.tensor_scalar(means, means, 1.0 / DH1, None, ALU.mult).then_inc(wc_done, 1)
                dve.wait_ge(wc_done, START + 2)
                nc.vector.tensor_tensor(heads, heads, means.rearrange("p (h o) -> p h o", o=1)
                                        .broadcast_to((128, KD * 2 * HEADS1, DH1)), ALU.subtract).then_inc(wc_done, 1)
                with dve.Fori(0, NG) as g:
                    def variance(j):
                        n = g * GT + j
                        dve.wait_ge(sq_done, START + n + 1)
                        dve.wait_ge(rr_done, START + (n - 1 if j > 1 else g * GT))
                        nc.vector.tensor_reduce(var[:, j % 2, :], sq[:, j % 2, :].rearrange("p (h d) -> p h d", d=DH1),
                                                AX, ALU.add).then_inc(var_done, 1)

                    def scaled(j):
                        n = g * GT + j
                        b = 3 * (j % 2)
                        dve.wait_ge(std_done, START + n + 1)
                        nc.vector.reciprocal(var[:, j % 2, :], var[:, j % 2, :]).then_inc(r_done, 1)
                        dve.wait_ge(r_done, START + n + 1)
                        dve.wait_ge(d_mm, START + (n - 1 if j > 1 else g * GT))
                        nc.vector.tensor_tensor(rr[:, j % 2, :], var[:, j % 2, 0:HEADS1], var[:, j % 2, HEADS1:],
                                                ALU.mult).then_inc(rr_done, 1)
                        dve.wait_ge(rr_done, START + n + 1)
                        nc.vector.tensor_tensor(
                            vs[:, j % 2, :].rearrange("p (h d) -> p h d", d=DH1),
                            bank[b + 1][0:RT, :].rearrange("p (h d) -> p h d", d=DH1),
                            rr[:, j % 2, :].rearrange("p (h o) -> p h o", o=1).broadcast_to((RT, HEADS1, DH1)),
                            ALU.mult).then_inc(v_done, 1)
                    variance(0)
                    for j in range(GT):
                        if j + 1 < GT:
                            variance(j + 1)
                        scaled(j)
                dve.wait_ge(dots_mm, START + 1)
                dve.wait_ge(const_done, START + 4)
                for f in range(KI):
                    for h in range(128 // DH1):
                        s = slice(h * DH1, (h + 1) * DH1)
                        ins = nc.vector.tensor_scalar(dots[s, f, s], acc[s, f * 128 + h * DH1:f * 128 + (h + 1) * DH1],
                                                      1.0 / N, None, ALU.mult)
                ins.then_inc(bd_done, 1)
                dve.wait_ge(m_mm, START + 1)
                for f in range(KI):
                    ins = nc.vector.tensor_copy(m_s[:, f, :], bank[f][:, 0:D])
                ins.then_inc(m_done, 1)
                dve.wait_ge(c_mm, START + 1)
                for c in range(KD):
                    nc.vector.tensor_copy(wcomb[:, c, :], bank[4 + c][:, 0:D])


def edge_convolution(nc, A, sems, sb, bank, tables, ident, xt, wcomb, x_rows, h_dram):
    src_t, rel0, base_row, rounds_t, iota_w = tables
    (w_in, scaled, acc_zero, tab, ea_in_a, ea_in_b, hid_mm, hid_done, w_mm, eq_done, hot_done, p_done, sum_mm, sum_copied, turned, added, idx_ready,
     staged, u_mm, mix_mm, t_done, b_done, x_done, passed, *gathered) = sems(*("c_" + s for s in (
         "w_in scaled acc_zero tab ea_in_a ea_in_b hid_mm hid w_mm eq hot prod sum_mm sum_copied turned added idx "
         "staged u_mm mix_mm t b x passed").split()),
                                  *(f"c_gathered{j}" for j in range(ITC)))
    ea_in = (ea_in_a, ea_in_b)
    c_s, c_x = float(np.float32(np.sin(np.pi / 8.0))), float(np.float32(np.cos(np.pi / 8.0)))
    SC = c_s * MUL ** -0.5
    LIN = c_x * 64 ** -0.5 * 16.0 ** -0.5 * (2 * MUL) ** -0.5
    NB = 4
    with ExitStack() as ctx:
        acc = sb(ctx, "acc", [128, NB, NW_COLS])
        rel = sb(ctx, "rel", [EC, NCH])
        base = sb(ctx, "base", [1, NU], I32)
        idx = sb(ctx, "idx", [EC, 2, UC], I32)
        rows = [sb(ctx, f"rows{j}", [EC, D]) for j in range(ITC)]
        ea4 = sb(ctx, "ea4", [EC, NCH, 4])
        ea8 = sb(ctx, "ea8", [8, 2, UE])
        fw0 = sb(ctx, "fw0", [8, 64])
        fw1 = sb(ctx, "fw1", [64, 4 * MUL])
        hid = sb(ctx, "hid", [64, 2, UE])
        eq = sb(ctx, "eq", [EC, 2, UC, W])
        hot = sb(ctx, "hot", [EC, 2, UC, 4, W])
        prod = sb(ctx, "prod", [EC, 2, UC, 8 * MUL])
        sum_rows = sb(ctx, "sum_rows", [W, 2, 8 * MUL])
        wsc = sb(ctx, "wsc", [128, KD, D])
        wl2 = sb(ctx, "wl2", [128, 4, 128])
        z = sb(ctx, "z", [RT, NT])
        bout = sb(ctx, "bout", [RT, D])
        stage = sb(ctx, "stage", [128, NB, GC])
        stage_x = sb(ctx, "stage_x", [128, KD, GC])
        t_rows = sb(ctx, "t_rows", [RT, GT, D])
        p_hid, p_t, p_w, p_sum = bank[0], bank[1], bank[2:6], bank[6:8]
        NW = 16 * 7

        def begin(eng, tag):
            rounds = eng.value_load(rounds_t[0:1, 0:1], min_val=1, max_val=MAXROUNDS)
            reg = eng.alloc_register(f"c_its_{tag}")
            eng.reg_mov(reg, 0)
            return rounds, reg

        def count(eng, reg):
            return eng.snap(reg, min_val=0, max_val=NIT * MAXROUNDS)

        with nc.Block() as block:
            @block.sync
            def _(sp):
                for t, name in ((fw0, "L1_gnn_fc_w0"), (fw1, "fw1"), (ea4, "ea4"), (z, "z_rows")):
                    sp.dma_start(t[:], A[name]).then_inc(w_in, 16)
                sp.dma_start(wsc[:, :, :], A["wsc"].rearrange("(k p) n -> p k n", p=128)).then_inc(w_in, 16)
                sp.dma_start(wl2[:, :, :], A["wl2"].rearrange("(k p) n -> p k n", p=128)).then_inc(w_in, 16)
                sp.dma_start(bout[:, :], A["L1_mix_b_out"].rearrange("(o n) -> o n", o=1).broadcast_to((RT, D))).then_inc(w_in, 16)
                rounds, reg = begin(sp, "sp")
                with sp.Fori(0, rounds) as r:
                    with sp.Fori(0, NIT) as i:
                        its = count(sp, reg)
                        for b in range(2):
                            sp.wait_ge(hid_mm, START + (its + i) * 2 + b - 1)
                            sp.dma_start(ea8[:, b, :], A["ea8"][:, bass.ds((i * 2 + b) * UE, UE)]).then_inc(ea_in[b], 16)
                    sp.reg_add(reg, reg, NIT)

            @block.gpsimd
            def _(pool):
                rounds, reg = begin(pool, "pool")
                nc.gpsimd.memset(acc[:, :, :], 0.0).then_inc(acc_zero, 1)
                with pool.Fori(0, rounds) as r:
                    with pool.Fori(0, NIT) as i:
                        its = count(pool, reg)
                        for b in range(2):
                            wait_alone(pool, p_done, ((its + i) * 2 + b) * UC - UC, passed)
                            nc.gpsimd.tensor_copy(idx[:, b, :], src_t[:, bass.ds(i * ITC + b * UC, UC)])\
                              .then_inc(idx_ready, 1)
                            wait_alone(pool, idx_ready, (its + i) * 2 + b + 1, passed)
                            for j in range(UC):
                                nc.gpsimd.indirect_dma_start(
                                    out=rows[b * UC + j][:, :], out_offset=None, in_=h_dram,
                                    in_offset=bass.IndirectOffsetOnAxis(ap=idx[:, b, j:j + 1], axis=0),
                                ).then_inc(gathered[b * UC + j], 16)
                    pool.reg_add(reg, reg, NIT)
                with pool.Fori(0, NG) as g:
                    cols = bass.ds(g * GC, GC)
                    pool.wait_ge(added, START + count(pool, reg) * 2)
                    pool.wait_ge(mix_mm, START + g * GT)
                    nc.gpsimd.tensor_copy(stage[:, :, :], acc[:, :, cols]).then_inc(staged, 1)
                    nc.gpsimd.tensor_copy(stage_x[:, :, :], xt[:, :, cols]).then_inc(staged, 1)

            @block.tensor
            def _(pe):
                rounds, reg = begin(pe, "pe")
                pe.wait_ge(w_in, START + NW)
                def hidden(q, b):
                    pe.wait_ge(ea_in[b], START + (q - b) * 8 + 16)
                    pe.wait_ge(hid_done, START + q)
                    nc.tensor.matmul(p_hid[0:64, 0:UE], fw0[:, :], ea8[:, b, :], start=True, stop=True)\
                      .then_inc(hid_mm, 1)

                def weights(q, b):
                    pe.wait_ge(hid_done, START + q + 1)
                    for j in range(UC):
                        pe.wait_ge(p_done, START + q * UC + j + 1 - UC)
                        nc.tensor.matmul(p_w[j][0:EC, 0:4 * MUL], hid[:, b, j * EC:(j + 1) * EC], fw1[:, :],
                                         start=True, stop=True).then_inc(w_mm, 1)

                def sums(q, b):
                    pe.wait_ge(sum_copied, START + q - 1)
                    to = p_sum[b][0:W, :].rearrange("p (s u) -> p s u", u=MUL)
                    for j in range(UC):
                        pe.wait_ge(hot_done, START + q * UC + j + 1)
                        pe.wait_ge(p_done, START + q * UC + j + 1)
                        p = prod[:, b, j, :].rearrange("p (s u) -> p s u", u=MUL)
                        nc.tensor.matmul(to[:, 0:4, :], hot[:, b, j, 0, :], p[:, 0:4, :], start=(j == 0), stop=False,
                                         skip_group_check=True)
                        for c in range(3):
                            ins = nc.tensor.matmul(to[:, 4 + c:8:3 - c, :], hot[:, b, j, 1 + c, :], p[:, 4:6 + c:1 + c, :],
                                                   start=False, stop=(j == UC - 1 and c == 2), skip_group_check=True)
                        ins.then_inc(sum_mm, 1)

                def turn(q, b):
                    pe.wait_ge(sum_copied, START + q + 1)
                    pe.wait_ge(added, START + q)
                    for m in range(NB):
                        ins = nc.tensor.transpose(p_t[:, m * W:(m + 1) * W], sum_rows[:, b, m * 128:(m + 1) * 128],
                                                  ident[0:W, 0:W])
                    ins.then_inc(turned, 1)

                def step(q, b, ahead=2, behind=True):
                    if ahead > 0:
                        weights(q + 1, 1 - b)
                    if ahead > 1:
                        hidden(q + 2, b)
                    if behind:
                        turn(q - 1, 1 - b)
                    sums(q, b)
                with pe.Fori(0, rounds) as r:
                    first = count(pe, reg) * 2
                    hidden(first, 0)
                    weights(first, 0)
                    hidden(first + 1, 1)
                    step(first, 0, behind=False)
                    with pe.Fori(0, NIT - 2) as i:
                        for b in range(2):
                            step(first + i * 2 + b + 1, 1 - b)
                    step(first + NU - 3, 1)
                    step(first + NU - 2, 0, ahead=1)
                    step(first + NU - 1, 1, ahead=0)
                    turn(first + NU - 1, 1)
                    pe.reg_add(reg, reg, NIT)
                pe.wait_ge(scaled, START + 3)
                with pe.Fori(0, NG) as g:
                    pe.wait_ge(staged, START + g * 2 + 2)
                    for j in range(GT):
                        n = g * GT + j
                        rows_j = slice(j * RT, (j + 1) * RT)
                        u, m = bank[2 * (j % 2)], bank[2 * (j % 2) + 1]
                        pe.wait_ge(x_done, START + (n - 1 if j > 1 else g * GT))
                        for k in range(KD):
                            nc.tensor.matmul(u[0:RT, 0:D], stage_x[:, k, rows_j], wsc[:, k, :], start=(k == 0), stop=False,
                                             skip_group_check=True)
                        for q in range(NB):
                            at, w = MUL * (0, 2, 1, 0)[q], wl2[:, q, :]
                            to = u[0:RT, at:at + 2 * MUL]
                            if q == NB - 1:
                                to = u[0:RT, :].rearrange("p (s u) -> p s u", u=MUL)[:, 0:4:3, :]
                                w = w.rearrange("p (a b) -> p a b", a=2)
                            ins = nc.tensor.matmul(to, stage[:, q, rows_j], w, start=False, stop=(q == NB - 1),
                                                   skip_group_check=True)
                        ins.then_inc(u_mm, 1)
                        for k in range(KD):
                            ins = nc.tensor.matmul(m[0:RT, 0:D], stage_x[:, k, rows_j], wcomb[:, k, :],
                                                   start=(k == 0), stop=(k == KD - 1))
                        ins.then_inc(mix_mm, 1)

            @block.scalar
            def _(act):
                rounds, reg = begin(act, "act")
                act.wait_ge(w_in, START + NW)
                nc.scalar.activation(wsc[:, :, :], wsc[:, :, :], ACT.Copy, scale=SC).then_inc(scaled, 1)
                nc.scalar.activation(wl2[:, 0:3, :], wl2[:, 0:3, :], ACT.Copy, scale=LIN).then_inc(scaled, 1)
                nc.scalar.activation(wl2[0:MUL, 3, :], wl2[0:MUL, 3, :], ACT.Copy, scale=LIN)
                nc.scalar.activation(wl2[MUL:, 3, :], wl2[MUL:, 3, :], ACT.Copy, scale=LIN * 3.0 ** -0.5).then_inc(scaled, 1)

                def silu(q, b):
                    act.wait_ge(hid_mm, START + q + 1)
                    act.wait_ge(w_mm, START + q * UC - UC)
                    nc.scalar.activation(hid[:, b, :], p_hid[0:64, 0:UE], ACT.Silu, scale=8.0 ** -0.5)\
                      .then_inc(hid_done, 1)

                def weighted_hots(q, b, u):
                    act.wait_ge(eq_done, START + q + 1)
                    for j in range(UC):
                        act.wait_ge(sum_mm, START + q * UC + j + 1 - ITC)
                        for m in range(4):
                            ins = nc.scalar.activation(hot[:, b, j, m, :], eq[:, b, j, :], ACT.Copy,
                                                       scale=ea4[:, bass.ds(u * UC + j, 1), m:m + 1].rearrange("p a b -> p (a b)"))
                        ins.then_inc(hot_done, 1)
                def copy(q, b):
                    act.wait_ge(sum_mm, START + q * UC + UC)
                    act.wait_ge(turned, START + q - 1)
                    nc.scalar.activation(sum_rows[:, b, :], p_sum[b][0:W, :], ACT.Copy).then_inc(sum_copied, 1)

                def step(q, b, u, ahead=2):
                    if ahead > 1:
                        silu(q + 2, b)
                    if ahead > 0:
                        weighted_hots(q + 1, 1 - b, u + 1)
                    copy(q, b)
                with act.Fori(0, rounds) as r:
                    first = count(act, reg) * 2
                    silu(first, 0)
                    weighted_hots(first, 0, 0)
                    silu(first + 1, 1)
                    step(first, 0, 0)
                    with act.Fori(0, NIT - 2) as i:
                        for b in range(2):
                            step(first + i * 2 + b + 1, 1 - b, i * 2 + b + 1)
                    step(first + NU - 3, 1, NU - 3)
                    step(first + NU - 2, 0, NU - 2, ahead=1)
                    step(first + NU - 1, 1, NU - 1, ahead=0)
                    act.reg_add(reg, reg, NIT)

            @block.vector
            def _(dve):
                rounds, reg = begin(dve, "dve")
                tabs = dve.alloc_register("c_tabs")
                dve.reg_mov(tabs, 2)
                dve.wait_ge(w_in, START + NW)
                nc.vector.tensor_copy(rel[:, :], rel0[:, :]).then_inc(tab, 1)
                nc.vector.tensor_copy(base[:, :], base_row[:, :]).then_inc(tab, 1)
                dve.wait_ge(acc_zero, START + 1)

                def one_hots(q, b, u):
                    dve.wait_ge(hot_done, START + q * UC - UC)
                    nc.vector.tensor_tensor(
                        eq[:, b, :, :],
                        iota_w[:, :].rearrange("p (o w) -> p o w", o=1).broadcast_to((EC, UC, W)),
                        rel[:, bass.ds(u * UC, UC)].rearrange("p (c o) -> p c o", o=1).broadcast_to((EC, UC, W)),
                        ALU.is_equal).then_inc(eq_done, 1)

                def products(q, b):
                    dve.wait_ge(sum_mm, START + q * UC - UC)
                    for j in range(UC):
                        dve.wait_ge(gathered[b * UC + j], (q - b) * 8 + 16)
                        dve.wait_ge(w_mm, START + q * UC + j + 1)
                        x, p, w = rows[b * UC + j], prod[:, b, j, :], p_w[j][0:EC, :]
                        two, three = (EC, 2, MUL), (EC, 3, MUL)
                        xs0 = x[:, 0:MUL].rearrange("p (o u) -> p o u", o=1).broadcast_to(two)
                        xs1 = x[:, MUL:D].rearrange("p (c u) -> p c u", c=3)
                        w_c = w[:, 2 * MUL:3 * MUL].rearrange("p (o u) -> p o u", o=1).broadcast_to(three)
                        w_d = w[:, 3 * MUL:4 * MUL].rearrange("p (o u) -> p o u", o=1).broadcast_to(three)
                        slots = p.rearrange("p (s u) -> p s u", u=MUL)
                        nc.vector.tensor_tensor(slots[:, 0:5:4, :], xs0, w[:, 0:2 * MUL].rearrange("p (a u) -> p a u", a=2), ALU.mult)
                        nc.vector.tensor_tensor(slots[:, 1:4, :], xs1, w_c, ALU.mult)
                        nc.vector.tensor_tensor(slots[:, 5:8, :], xs1, w_d, ALU.mult).then_inc(p_done, 1)

                def add(q, u):
                    at = dve.value_load(base[0:1, bass.ds(u, 1)], min_val=0, max_val=NP)
                    dve.wait_ge(turned, START + q + 1)
                    dve.wait_ge(added, START + q)
                    win = acc[:, :, bass.ds(at, W)]
                    nc.vector.tensor_tensor(win, win, p_t[:, 0:NB * W].rearrange("p (k w) -> p k w", k=NB),
                                            ALU.add).then_inc(added, 1)
                with dve.Fori(0, rounds) as r:
                    wait_alone(dve, tab, dve.snap(tabs, min_val=0, max_val=1 << 20), passed)
                    first = count(dve, reg) * 2
                    one_hots(first, 0, 0)
                    products(first, 0)
                    one_hots(first + 1, 1, 1)
                    products(first + 1, 1)
                    with dve.Fori(0, NIT - 1) as i:
                        for b in range(2):
                            q, u = first + i * 2 + b, i * 2 + b
                            one_hots(q + 2, b, u + 2)
                            products(q + 2, b)
                            add(q, u)
                    add(first + NU - 2, NU - 2)
                    add(first + NU - 1, NU - 1)
                    dve.reg_add(reg, reg, NIT)
                    nc.vector.tensor_scalar(rel[:, :], rel[:, :], float(W), None, ALU.subtract).then_inc(tab, 1)
                    nc.vector.tensor_scalar(base[:, :], base[:, :], float(W), float(NP), ALU.add, ALU.min).then_inc(tab, 1)
                    dve.reg_add(tabs, tabs, 2)
                with dve.Fori(0, NG) as g:
                    for j in range(GT):
                        n = g * GT + j
                        u, m = bank[2 * (j % 2)], bank[2 * (j % 2) + 1]
                        row = x_rows[:, bass.ds(n, 1), :].rearrange("p a d -> p (a d)")
                        zt = z[:, bass.ds(n, 1)]
                        dve.wait_ge(mix_mm, START + n + 1)
                        nc.vector.tensor_tensor(t_rows[:, j, :], m[0:RT, 0:D], bout[:, :], ALU.add).then_inc(t_done, 1)
                        dve.wait_ge(t_done, START + n + 1)
                        nc.vector.tensor_tensor(t_rows[:, j, :], t_rows[:, j, :], row, ALU.add).then_inc(b_done, 1)
                        dve.wait_ge(b_done, START + n + 1)
                        dve.wait_ge(u_mm, START + n + 1)
                        nc.vector.scalar_tensor_tensor(out=row[:, 0:MUL], in0=u[0:RT, 0:MUL], scalar=zt, in1=t_rows[:, j, 0:MUL],
                                                       op0=ALU.mult, op1=ALU.add)
                        nc.vector.scalar_tensor_tensor(out=row[:, MUL:D].rearrange("p (u c) -> p u c", c=3),
                                                       in0=u[0:RT, MUL:D].rearrange("p (c u) -> p u c", c=3), scalar=zt,
                                                       in1=t_rows[:, j, MUL:D].rearrange("p (u c) -> p u c", c=3),
                                                       op0=ALU.mult, op1=ALU.add).then_inc(x_done, 1)


def dispatch(nc, A, sems, sb, bank, x_rows, mean_var, rstd, picked, slot_i, expert_i, x_slots, w13, w2, w_names):
    (iota_done, step, mm, staged, idx_done, scattered, w_in, passed) = sems(*("k_" + s for s in (
        "iota step mm staged idx scattered_gathered w_in passed").split()))
    FULL = HID1 // 128
    REST = HID1 - FULL * 128
    with ExitStack() as ctx:
        iota8_i = sb(ctx, "iota8_i", [RT, 8], I32)
        iota8 = sb(ctx, "iota8", [RT, 8])
        block_i = sb(ctx, "block_i", [1, NBLK], I32)
        block_f = sb(ctx, "block_f", [1, NBLK])
        one = [sb(ctx, f"one{c}", [RT, NT, 8]) for c in range(2)]
        both = sb(ctx, "both", [RT, NT, 8])
        sums = [sb(ctx, f"sums{c}", [RT, NT, 8]) for c in range(2)]
        before = sb(ctx, "before", [RT, RT])
        ones = sb(ctx, "ones", [RT, RT])
        count = sb(ctx, "count", [RT, 8])
        count_i = sb(ctx, "count_i", [RT, 8], I32)
        blocks_i = sb(ctx, "blocks_i", [RT, 8], I32)
        blocks = sb(ctx, "blocks", [RT, 8])
        ends = [sb(ctx, f"ends{c}", [RT, 8]) for c in range(2)]
        offset = sb(ctx, "offset", [RT, 8])
        passed_b = sb(ctx, "passed_b", [1, NBLK, 8])
        expert = sb(ctx, "expert", [1, NBLK])
        slot = sb(ctx, "slot", [RT, NT])
        xn = sb(ctx, "xn", [RT, GT, D])
        idx = sb(ctx, "idx", [RT, GT * 2], I32)
        p_before, p_all = bank[0], bank[1]
        with nc.Block() as block:
            @block.sync
            def _(sp):
                for m, name in enumerate(w_names[:2]):
                    for k in range(KD):
                        sp.dma_start(w13[:, :, m, k, :], A[name][:, k * 128:(k + 1) * 128, :].rearrange("e p n -> p e n")).then_inc(w_in, 16)
                for h in range(FULL):
                    sp.dma_start(w2[:, :, h, :], A[w_names[2]][:, h * 128:(h + 1) * 128, :].rearrange("e p n -> p e n")).then_inc(w_in, 16)
                sp.dma_start(w2[0:REST, :, FULL, :], A[w_names[2]][:, FULL * 128:HID1, :].rearrange("e p n -> p e n")).then_inc(w_in, 16)
                sp.wait_ge(w_in, START + (2 * KD + FULL + 1) * 16)

            @block.gpsimd
            def _(pool):
                nc.gpsimd.iota(iota8_i[:, :], pattern=[[1, 8]], base=0, channel_multiplier=0)
                nc.gpsimd.iota(block_i[:, :], pattern=[[1, NBLK]], base=0, channel_multiplier=0)
                nc.gpsimd.memset(ones[:, :], 1.0).then_inc(iota_done, 1)
                pool.wait_ge(iota_done, START + 1)
                nc.gpsimd.affine_select(out=before[:, :], in_=ones[:, :], compare_op=ALU.is_gt, fill=0.0,
                                        base=0, pattern=[[1, RT]], channel_multiplier=-1).then_inc(iota_done, 1)
                with pool.Fori(0, NG) as g:
                    wait_alone(pool, staged, g * GT + GT, passed)
                    nc.gpsimd.tensor_copy(idx[:, :].rearrange("p (t c) -> p t c", c=2), slot_i[:, bass.ds(g * GT, GT), :])\
                      .then_inc(idx_done, 1)
                    wait_alone(pool, idx_done, g + 1, passed)
                    for j in range(GT):
                        for c in range(2):
                            nc.gpsimd.indirect_dma_start(
                                out=x_slots, out_offset=bass.IndirectOffsetOnAxis(ap=idx[:, j * 2 + c:j * 2 + c + 1], axis=0),
                                in_=xn[:, j, :], in_offset=None).then_inc(scattered, 16)
                    pool.wait_ge(scattered, (g + 1) * (GT * 2 * 16))

            @block.tensor
            def _(pe):
                pe.wait_ge(iota_done, START + 2)
                pe.wait_ge(step, START + 9)
                nc.tensor.matmul(p_before[0:RT, 0:8], before[:, :], sums[1][:, NT - 1, :], start=True, stop=True)
                nc.tensor.matmul(p_all[0:RT, 0:8], ones[:, :], sums[1][:, NT - 1, :], start=True, stop=True).then_inc(mm, 1)

            @block.vector
            def _(dve):
                n = [0]

                def then(ins):
                    n[0] += 1
                    ins.then_inc(step, 1)
                    dve.wait_ge(step, START + n[0])
                dve.wait_ge(iota_done, START + 2)
                nc.vector.tensor_copy(block_f[:, :], block_i[:, :])
                then(nc.vector.tensor_copy(iota8[:, :], iota8_i[:, :]))
                every = iota8[:, :].rearrange("p (o e) -> p o e", o=1).broadcast_to((RT, NT, 8))
                nc.vector.tensor_tensor(one[0][:, :, :], every, picked[:, :, 0:1].broadcast_to((RT, NT, 8)), ALU.is_equal)
                then(nc.vector.tensor_tensor(one[1][:, :, :], every, picked[:, :, 1:2].broadcast_to((RT, NT, 8)), ALU.is_equal))
                then(nc.vector.tensor_tensor(both[:, :, :], one[0][:, :, :], one[1][:, :, :], ALU.add))
                then(nc.vector.tensor_copy(sums[0][:, :, :], both[:, :, :]))
                for i in range(5):
                    d, a, b = 1 << i, sums[i % 2], sums[(i + 1) % 2]
                    nc.vector.tensor_copy(b[:, 0:d, :], a[:, 0:d, :])
                    then(nc.vector.tensor_tensor(b[:, d:, :], a[:, d:, :], a[:, 0:NT - d, :], ALU.add))
                dve.wait_ge(mm, START + 1)
                then(nc.vector.tensor_scalar(count[:, :], p_all[0:RT, 0:8], 127.0, None, ALU.add))
                then(nc.vector.tensor_copy(count_i[:, :], count[:, :]))
                then(nc.vector.tensor_scalar(blocks_i[:, :], count_i[:, :], 7, None, ALU.arith_shift_right))
                then(nc.vector.tensor_copy(blocks[:, :], blocks_i[:, :]))
                then(nc.vector.tensor_copy(ends[0][:, :], blocks[:, :]))
                for i in range(3):
                    d, a, b = 1 << i, ends[i % 2], ends[(i + 1) % 2]
                    nc.vector.tensor_copy(b[:, 0:d], a[:, 0:d])
                    then(nc.vector.tensor_tensor(b[:, d:], a[:, d:], a[:, 0:8 - d], ALU.add))
                nc.vector.tensor_tensor(passed_b[:, :, :], block_f[:, :].rearrange("p (b o) -> p b o", o=1).broadcast_to((1, NBLK, 8)),
                                        ends[1][0:1, :].rearrange("p (o e) -> p o e", o=1).broadcast_to((1, NBLK, 8)), ALU.is_ge)
                then(nc.vector.tensor_tensor(offset[:, :], ends[1][:, :], blocks[:, :], ALU.subtract))
                then(nc.vector.tensor_reduce(expert[:, :], passed_b[:, :, :], AX, ALU.add))
                then(nc.vector.tensor_scalar(expert[:, :], expert[:, :], float(E1 - 1), None, ALU.min))
                nc.vector.tensor_copy(expert_i[:, :], expert[:, :])
                then(nc.vector.scalar_tensor_tensor(out=offset[:, :], in0=offset[:, :], scalar=128.0, in1=p_before[0:RT, 0:8],
                                                    op0=ALU.mult, op1=ALU.add))
                then(nc.vector.tensor_tensor(sums[1][:, :, :], sums[1][:, :, :], both[:, :, :], ALU.subtract))
                then(nc.vector.tensor_tensor(sums[1][:, :, :], sums[1][:, :, :],
                                             offset[:, :].rearrange("p (o e) -> p o e", o=1).broadcast_to((RT, NT, 8)), ALU.add))
                for c in range(2):
                    then(nc.vector.tensor_tensor(sums[0][:, :, :], one[c][:, :, :], sums[1][:, :, :], ALU.mult))
                    then(nc.vector.tensor_reduce(slot[:, :], sums[0][:, :, :], AX, ALU.add))
                    then(nc.vector.tensor_copy(slot_i[:, :, c], slot[:, :]))
                with dve.Fori(0, NG) as g:
                    dve.wait_ge(scattered, g * (GT * 2 * 16))
                    for j in range(GT):
                        t = g * GT + j
                        nc.vector.tensor_scalar(xn[:, j, :], x_rows[:, bass.ds(t, 1), :].rearrange("p a d -> p (a d)"),
                                                mean_var[:, bass.ds(t, 1), 0:1].rearrange("p a b -> p (a b)"),
                                                rstd[:, bass.ds(t, 1)], ALU.subtract, ALU.mult).then_inc(staged, 1)


def expert_swiglu(nc, sems, sb, bank, ident, expert_i, x_slots, y_slots, w13, w2):
    (x_in_0, x_in_1, xt_mm, xt_done, h1_mm, h3_mm, s_done, g_done, gt_mm, gt_done, y_mm, y_done, y_out_0, y_out_1, passed) = sems(*(
        "e_" + s for s in "x_in_0 x_in_1 xt_mm xt h1_mm h3_mm s g gt_mm gt y_mm y y_out_0 y_out_1 passed".split()))
    x_in, y_out = (x_in_0, x_in_1), (y_out_0, y_out_1)
    NH = len(HCH)
    HH = HID1 // 2
    IN_0 = 4
    with ExitStack() as ctx:
        x_b = sb(ctx, "x_b", [128, 2, D])
        x_t = sb(ctx, "x_t", [128, 2, KD, 128])
        s_b = sb(ctx, "s_b", [128, 2, HH])
        g_b = sb(ctx, "g_b", [128, HID1])
        g_t = sb(ctx, "g_t", [128, NH, 128])
        y_b = sb(ctx, "y_b", [128, 2, D])
        p_x, p_h1, p_h3, p_g, p_y = bank[0], bank[1:3], bank[3:5], bank[5:7], bank[7]
        with nc.Block() as block:
            @block.sync
            def _(sp):
                def load(n, b):
                    sp.wait_ge(xt_mm, START + n - 1)
                    sp.dma_start(x_b[:, b, :], x_slots[bass.ds(n * 128, 128), :]).then_inc(x_in[b], 16)
                for b in range(2):
                    sp.dma_start(x_b[:, b, :], x_slots[b * 128:(b + 1) * 128, :]).then_inc(x_in[b], 16)

                def store(n, b):
                    sp.wait_ge(y_done, START + n + 1)
                    sp.dma_start(y_slots[bass.ds(n * 128, 128), :], y_b[:, b, :]).then_inc(y_out[b], 16)
                with sp.Fori(0, NBLK // 2 - 1) as i:
                    for b in range(2):
                        load(i * 2 + b + 2, b)
                        store(i * 2 + b, b)
                for b in range(2):
                    sp.wait_ge(y_done, START + NBLK - 1 + b)
                    sp.dma_start(y_slots[(NBLK - 2 + b) * 128:(NBLK - 1 + b) * 128, :], y_b[:, b, :]).then_inc(y_out[b], 16)
                for b in range(2):
                    sp.wait_ge(y_out[b], START + NBLK // 2 * 16)

            @block.tensor
            def _(pe):
                def turn_x(n, b):
                    wait_alone(pe, x_in[b], (n - b) * 8 + 16, passed)
                    pe.wait_ge(xt_done, START + n)
                    for k in range(KD):
                        ins = nc.tensor.transpose(p_x[:, k * 128:(k + 1) * 128], x_b[:, b, k * 128:(k + 1) * 128], ident[:, :])
                    ins.then_inc(xt_mm, 1)

                def up(n, b):
                    e = pe.value_load(expert_i[0:1, bass.ds(n, 1)], min_val=0, max_val=E1 - 1)
                    wait_alone(pe, xt_done, n + 1, passed)
                    wait_alone(pe, g_done, n * 2, passed)
                    for half in range(2):
                        for m, (p, done) in enumerate(((p_h1, h1_mm), (p_h3, h3_mm))):
                            for k in range(KD):
                                ins = nc.tensor.matmul(p[half][:, 0:HH], x_t[:, b, k, :],
                                                       w13[:, bass.ds(e, 1), m, k, half * HH:(half + 1) * HH]
                                                       .rearrange("p o n -> p (o n)"), start=(k == 0), stop=(k == KD - 1))
                            ins.then_inc(done, 1)

                def turn_g(n):
                    pe.wait_ge(g_done, START + n * 2 + 2)
                    pe.wait_ge(gt_done, START + n * 2)
                    for h, (o, sz) in enumerate(HCH):
                        at = h % IN_0 * 128
                        ins = nc.tensor.transpose(p_g[h // IN_0][0:sz, at:at + 128], g_b[:, o:o + sz], ident[:, :])
                        if h in (IN_0 - 1, NH - 1):
                            ins.then_inc(gt_mm, 1)

                def down(n):
                    e = pe.value_load(expert_i[0:1, bass.ds(n, 1)], min_val=0, max_val=E1 - 1)
                    wait_alone(pe, gt_done, n * 2 + 2, passed)
                    wait_alone(pe, y_done, n, passed)
                    for h, (o, sz) in enumerate(HCH):
                        ins = nc.tensor.matmul(p_y[:, 0:D], g_t[0:sz, h, :], w2[0:sz, bass.ds(e, 1), h, :].rearrange("p o n -> p (o n)"),
                                               start=(h == 0), stop=(h == NH - 1))
                    ins.then_inc(y_mm, 1)
                turn_x(0, 0)
                turn_x(1, 1)
                up(0, 0)
                turn_g(0)
                with pe.Fori(0, NBLK // 2 - 1) as i:
                    for b in range(2):
                        n = i * 2 + b + 1
                        up(n, 1 - b)
                        down(n - 1)
                        turn_x(n + 1, b)
                        turn_g(n)
                up(NBLK - 1, 1)
                down(NBLK - 2)
                turn_g(NBLK - 1)
                down(NBLK - 1)

            @block.scalar
            def _(act):
                def gate(n):
                    for half in range(2):
                        act.wait_ge(h1_mm, START + n * 2 + half + 1)
                        act.wait_ge(g_done, START + n * 2 + half - 1)
                        nc.scalar.activation(s_b[:, half, :], p_h1[half][:, 0:HH], ACT.Silu).then_inc(s_done, 1)

                def turned(n):
                    act.wait_ge(gt_mm, START + n * 2 + 1)
                    act.wait_ge(y_mm, START + n)
                    nc.scalar.activation(g_t[:, 0:IN_0, :], p_g[0][:, 0:IN_0 * 128].rearrange("p (h c) -> p h c", c=128), ACT.Copy)\
                      .then_inc(gt_done, 1)
                with act.Fori(0, NBLK) as n:
                    gate(n)
                    turned(n)

            @block.vector
            def _(dve):
                def copy_x(n, b):
                    dve.wait_ge(xt_mm, START + n + 1)
                    dve.wait_ge(h3_mm, START + n * 2 - 2)
                    nc.vector.tensor_copy(x_t[:, b, :, :], p_x[:, 0:D].rearrange("p (k c) -> p k c", k=KD)).then_inc(xt_done, 1)

                def product(n):
                    dve.wait_ge(gt_mm, START + n * 2)
                    for half in range(2):
                        dve.wait_ge(s_done, START + n * 2 + half + 1)
                        dve.wait_ge(h3_mm, START + n * 2 + half + 1)
                        nc.vector.tensor_tensor(g_b[:, half * HH:(half + 1) * HH], s_b[:, half, :], p_h3[half][:, 0:HH], ALU.mult)\
                          .then_inc(g_done, 1)

                def turned(n):
                    dve.wait_ge(gt_mm, START + n * 2 + 2)
                    dve.wait_ge(y_mm, START + n)
                    o, sz = HCH[-1]
                    nc.vector.tensor_copy(g_t[:, IN_0:NH - 1, :], p_g[1][:, 0:(NH - 1 - IN_0) * 128].rearrange("p (h c) -> p h c", c=128))
                    at = (NH - 1 - IN_0) * 128
                    nc.vector.tensor_copy(g_t[0:sz, NH - 1, :], p_g[1][0:sz, at:at + 128]).then_inc(gt_done, 1)

                def output(n, b):
                    dve.wait_ge(y_mm, START + n + 1)
                    dve.wait_ge(y_out[b], START + (n - b) * 8)
                    nc.vector.tensor_copy(y_b[:, b, :], p_y[:, 0:D]).then_inc(y_done, 1)
                copy_x(0, 0)
                copy_x(1, 1)
                product(0)
                turned(0)
                with dve.Fori(0, NBLK // 2 - 1) as i:
                    for b in range(2):
                        n = i * 2 + b + 1
                        product(n)
                        output(n - 1, b)
                        copy_x(n + 1, b)
                        turned(n)
                product(NBLK - 1)
                output(NBLK - 2, 0)
                turned(NBLK - 1)
                output(NBLK - 1, 1)


def combine(nc, sems, sb, x_rows, slot_i, weight, y_slots):
    idx_done, added, passed, *gathered = sems("m_idx", "m_added", "m_passed", *(f"m_gathered{j}" for j in range(GT * 2)))
    with ExitStack() as ctx:
        idx = sb(ctx, "idx", [RT, 2, 2, GT // 2 * 2], I32)
        rows = [sb(ctx, f"rows{j}", [RT, D]) for j in range(GT * 2)]
        with nc.Block() as block:
            @block.gpsimd
            def _(pool):
                with pool.Fori(0, NG) as g:
                    for b in range(2):
                        n = g * 2 + b
                        wait_alone(pool, added, n * GT - GT, passed)
                        nc.gpsimd.tensor_copy(idx[:, b, 0, :].rearrange("p (t c) -> p t c", c=2), slot_i[:, bass.ds(n * 2, 2), :])\
                          .then_inc(idx_done, 1)
                        wait_alone(pool, idx_done, n + 1, passed)
                        for j in range(GT):
                            nc.gpsimd.indirect_dma_start(
                                out=rows[b * GT + j][:, :], out_offset=None, in_=y_slots,
                                in_offset=bass.IndirectOffsetOnAxis(ap=idx[:, b, 0, j:j + 1], axis=0),
                            ).then_inc(gathered[b * GT + j], 16)

            @block.vector
            def _(dve):
                with dve.Fori(0, NG) as g:
                    for b in range(2):
                        for j in range(GT):
                            n = (g * 2 + b) * GT + j
                            t = g * GT + b * 2 + j // 2
                            row = x_rows[:, bass.ds(t, 1), :].rearrange("p a d -> p (a d)")
                            dve.wait_ge(gathered[b * GT + j], g * 16 + 16)
                            dve.wait_ge(added, START + n)
                            nc.vector.scalar_tensor_tensor(
                                out=row, in0=rows[b * GT + j][:, :],
                                scalar=weight[:, bass.ds(t, 1), j % 2:j % 2 + 1].rearrange("p a b -> p (a b)"),
                                in1=row, op0=ALU.mult, op1=ALU.add).then_inc(added, 1)


def layouts(i):
    c = np.ascontiguousarray
    src, dst = np.asarray(i["src"]), np.asarray(i["dst"])
    x = np.zeros((NP, D), np.float32)
    x[:N] = i["x"]
    z = np.zeros((NP,), np.float32)
    z[:N] = np.asarray(i["node_vec1"])[:, 0]
    pad8 = np.zeros((128, 8), np.float32)
    pad8[:, :E0] = i["L0_ffn_router_w2"]
    vec = np.concatenate([np.arange(MUL)] + [MUL + 3 * np.arange(MUL) + k for k in range(3)])
    qkv = np.asarray(i["L1_mix_w_qkv"])[vec]
    none = np.zeros((128, 128), np.float32)
    swap = np.r_[MUL:2 * MUL, 0:MUL]
    l0, l1 = np.asarray(i["L1_gnn_W_lin2_0"]), np.asarray(i["L1_gnn_W_lin2_1"])

    def diag(p, q):
        m = np.zeros((2 * MUL, 2 * MUL), np.float32)
        m[:MUL, :MUL], m[MUL:, MUL:] = p, q
        return m

    a = {
        "x_rows": c(x.reshape(NT, RT, D).transpose(1, 0, 2)),
        "src_t": c(src.reshape(NCH, EC).T),
        "dst_t": c(dst.reshape(NCH, EC).T),
        "dst_c": c(dst.reshape(NU, UE)),
        "wkv0": c(np.concatenate([i["L0_mix_wk"], i["L0_mix_wv"]], axis=1)),
        "wq0": i["L0_mix_wq"], "wo0": i["L0_mix_wo"],
        "w1_0": c(np.asarray(i["L0_gnn_W1"]).T), "w2_0": c(np.asarray(i["L0_gnn_W2"]).T),
        "wih_0": c(np.asarray(i["L0_gnn_W_ih"]).T), "whh_0": c(np.asarray(i["L0_gnn_W_hh"]).T),
        "rw2_0": pad8,
        "z_rows": c(z.reshape(NT, RT).T),
        "ea4": c(np.asarray(i["edge_attr_4"]).reshape(NCH, EC, 4).transpose(1, 0, 2)),
        "ea8": c(np.asarray(i["edge_attr_8"]).T),
        "wlin": np.concatenate([diag(i["L1_gnn_W_lin1_0"], i["L1_gnn_W_lin1_1"]),
                                diag(i["L1_gnn_W_lin1_1"], i["L1_gnn_W_lin1_1"])]),
        "wsc": np.concatenate([np.concatenate([diag(i["L1_gnn_W_sc0"], i["L1_gnn_W_sc1"]), none], axis=1),
                               np.concatenate([none, diag(i["L1_gnn_W_sc1"], i["L1_gnn_W_sc1"])], axis=1)]),
        "wl2": np.concatenate([diag(l0[:MUL], l1[MUL:]), diag(l1[MUL:], l1[MUL:]),
                               diag(l1[:MUL], l1[:MUL]), diag(l1[:MUL], l0[MUL:])[:, swap]]),
        "fw1": np.asarray(i["L1_gnn_fc_w1"]),
        "wkv1": c(qkv[:, INNER:]), "wq1_t": c(qkv[:, :INNER].T),
        "rw1": c(np.asarray(i["L1_ffn_router_w"]).T),
        "w1_1": c(np.asarray(i["L1_ffn_w1"]).transpose(0, 2, 1)),
        "w3_1": c(np.asarray(i["L1_ffn_w3"]).transpose(0, 2, 1)),
        "w2_1": c(np.asarray(i["L1_ffn_w2"]).transpose(0, 2, 1)),
    }
    for name in ("L0_mix_bq", "L0_mix_bo", "L0_gnn_b1", "L0_gnn_b_ih", "L0_gnn_b_hh"):
        a[name + "_t"] = np.asarray(i[name]).reshape(-1, 128).T
    for name in ("L0_ffn_expert_b1", "L0_ffn_expert_b2"):
        a[name + "_t"] = np.asarray(i[name]).reshape(E0, KD, 128).transpose(2, 0, 1)
    for name in ("L0_mix_bk", "L0_mix_bv", "L0_gnn_b2",
                 "L0_ffn_router_w1", "L0_ffn_router_b1", "L0_ffn_router_b2", "L0_ffn_expert_w1", "L0_ffn_expert_w2",
                 "L0_ffn_expert_w3", "L0_ffn_expert_b3",
                 "L1_gnn_fc_w0", "L1_mix_w_out", "L1_mix_b_out"):
        a[name] = i[name]
    return {k: np.ascontiguousarray(v) for k, v in a.items()}


def kernel(**inputs):
    import concourse.bacc as _bacc
    from concourse.bass_utils import run_bass_kernel_spmd as _run

    nc = _bacc.Bacc("TRN2", target_bir_lowering=False, num_devices=1)
    arrays = {f"in_{k}": v for k, v in layouts(inputs).items()}
    args = {k[3:]: nc.dram_tensor(k, v.shape, mybir.dt.from_np(v.dtype), kind="ExternalInput").ap()
            for k, v in arrays.items()}
    out = nc.dram_tensor("out_0", (N, D), F32, kind="ExternalOutput").ap()
    build(nc, args, out)
    r = _run(nc, [arrays], core_ids=[0])
    return r.results[0]["out_0"]
```
